# Optimizing a Trainium2 kernel written in Bass

```python
import numpy as np
import jax
import jax.numpy as jnp

def _softmax(x, axis=-1):
    return jax.nn.softmax(x, axis=axis)

def _gelu(x):
    return jax.nn.gelu(x, approximate=True)

def _silu(x):
    return jax.nn.silu(x)

def _sigmoid(x):
    return jax.nn.sigmoid(x)

def _layernorm(x, axis=-1, eps=1e-05):
    m = jnp.mean(x, axis=axis, keepdims=True)
    v = jnp.var(x, axis=axis, keepdims=True)
    return (x - m) / jnp.sqrt(v + eps)

def _scatter_add(tgt, idx, src, axis=0):
    return tgt.at[idx].add(src)

def _segment_sum(src, seg, n):
    return jax.ops.segment_sum(src, seg, n)
kernel_name = 'mk_flamingo_gated_d2_seqx_r4_3ed9f8'

def setup_inputs(seed: int=0):
    np.random.seed(seed)
    _w = jnp.asarray

    def _rec_inputs():
        import jax
        import jax.numpy as jnp
        _rk = jax.random.key(seed)
        x = -0.0002928 + 1 * jax.random.normal(jax.random.fold_in(_rk, 1), (4, 512, 256), jnp.float32)
        _lenS = 512 - jax.random.randint(jax.random.fold_in(_rk, 7), (4,), 0, max(1, 512 // 4) + 1, jnp.int32)
        _lenS2 = 1601 - jax.random.randint(jax.random.fold_in(_rk, 8), (4,), 0, max(1, 1601 // 4) + 1, jnp.int32)
        _ctx_1024P = jax.random.normal(jax.random.fold_in(_rk, 11), (4, 16, 256), jnp.float32)
        _ctx_1024c = jax.random.dirichlet(jax.random.fold_in(_rk, 511), 0.3 * jnp.ones((16,), jnp.float32), (4, 1601))
        _ctx_1024t = jnp.einsum('bsk,bkd->bsd', _ctx_1024c, _ctx_1024P)
        _ctx_1024t = _ctx_1024t * jax.lax.rsqrt(jnp.mean(jnp.square(_ctx_1024t)) + 1e-12) * 0.953939
        ctx_1024 = -1.39393e-06 + 0.999914 * (_ctx_1024t + 0.3 * jax.random.normal(jax.random.fold_in(_rk, 611), (4, 1601, 256), jnp.float32))
        _validS = jnp.arange(512)[None, :] < _lenS[:, None]
        _validS2 = jnp.arange(1601)[None, :] < _lenS2[:, None]
        _causal = jnp.tril(jnp.ones((512, 512), dtype=bool))
        mask_1x1xSxS2_ik0 = jnp.where(jnp.broadcast_to(_validS2[0:1, None, None, :], (1, 1, 512, 1601)), 0, 1).astype(jnp.int32)
        _g = jax.random.normal(jax.random.fold_in(_rk, 9001), (2, 2), jnp.float32)
        _g = jnp.sign(_g) * jnp.maximum(jnp.abs(_g), 1.0) + (_g == 0) * 1.0
        g_xattn = _g[0]
        g_ffn = _g[1]
        return (x, ctx_1024, mask_1x1xSxS2_ik0, g_xattn, g_ffn)
    x, ctx_1024, mask_1x1xSxS2_ik0, g_xattn, g_ffn = _rec_inputs()

    def _L0_xattn_setup():
        import jax, jax.numpy as jnp
        import numpy as np
        HEADS = 16
        DIM_HEAD = 64
        QUERY_DIM = 256
        INNER = HEADS * DIM_HEAD
        SCALE = DIM_HEAD ** (-0.5)
        key = jax.random.key(seed)
        ks = jax.random.split(key, 6)
        B, N, M = (2, 512, 512)
        x = jax.random.normal(ks[0], (B, N, QUERY_DIM), dtype=jnp.float32)
        context = jax.random.normal(ks[1], (B, M, QUERY_DIM), dtype=jnp.float32)
        s = QUERY_DIM ** (-0.5)
        Wq = jax.random.normal(ks[2], (QUERY_DIM, INNER), dtype=jnp.float32) * s
        Wk = jax.random.normal(ks[3], (QUERY_DIM, INNER), dtype=jnp.float32) * s
        Wv = jax.random.normal(ks[4], (QUERY_DIM, INNER), dtype=jnp.float32) * s
        Wo = jax.random.normal(ks[5], (INNER, QUERY_DIM), dtype=jnp.float32) * INNER ** (-0.5)
        return {'x': x, 'context': context, 'Wq': Wq, 'Wk': Wk, 'Wv': Wv, 'Wo': Wo}
    _L0_xattn_all = _L0_xattn_setup()
    _L0_xattn_in = {k: v for k, v in _L0_xattn_all.items() if k in ('Wq', 'Wk', 'Wv', 'Wo')}
    del _L0_xattn_all

    def _L0_ffn_setup():
        import jax, jax.numpy as jnp
        import numpy as np
        D_MODEL = 256
        N_HEADS = 16
        N_KV = 4
        NUM_REP = N_HEADS // N_KV
        HEAD_DIM = D_MODEL // N_HEADS
        N_EXPERTS = 8
        TOP_K = 2
        CAP_FACTOR = 1.25
        EPS_NORM = 1e-06

        def _rmsnorm(x, w):
            var = jnp.mean(x * x, axis=-1, keepdims=True)
            return w * (x * jax.lax.rsqrt(var + EPS_NORM))

        def _gqa(x, qw, qb, kw, kb, vw, vb, ow, ob):
            B, S, D = x.shape
            q = (x @ qw + qb).reshape(B, S, N_HEADS, HEAD_DIM).transpose(0, 2, 1, 3)
            k = (x @ kw + kb).reshape(B, S, N_KV, HEAD_DIM).transpose(0, 2, 1, 3)
            v = (x @ vw + vb).reshape(B, S, N_KV, HEAD_DIM).transpose(0, 2, 1, 3)
            k = jnp.repeat(k, NUM_REP, axis=1)
            v = jnp.repeat(v, NUM_REP, axis=1)
            scores = jnp.einsum('bhqd,bhkd->bhqk', q, k) / np.sqrt(HEAD_DIM).astype(np.float32)
            attn = jax.nn.softmax(scores, axis=-1)
            out = jnp.einsum('bhqk,bhkd->bhqd', attn, v)
            out = out.transpose(0, 2, 1, 3).reshape(B, S, D)
            return out @ ow + ob

        def _moe(x, gate_w, w1, w2):
            B, S, D = x.shape
            T = B * S
            x_flat = x.reshape(T, D)
            capacity = int(CAP_FACTOR * T * TOP_K / N_EXPERTS)
            logits = x_flat @ gate_w
            probs = jax.nn.sigmoid(logits)
            _, sel = jax.lax.top_k(probs, TOP_K)
            w_topk = jnp.take_along_axis(probs, sel, axis=1)
            w_topk = w_topk / (jnp.sum(w_topk, axis=-1, keepdims=True) + 1e-06)
            flat_sel = sel.reshape(-1)
            em = jax.nn.one_hot(flat_sel, N_EXPERTS, dtype=jnp.int32)
            ranks = jnp.take_along_axis(jnp.cumsum(em, axis=0), flat_sel[:, None], axis=1)[:, 0] - 1
            valid = ranks < capacity
            slot = flat_sel * capacity + ranks
            scatter_idx = jnp.where(valid, slot, N_EXPERTS * capacity)
            x_rep = jnp.repeat(x_flat, TOP_K, axis=0)
            padded = jnp.zeros((N_EXPERTS * capacity + 1, D), x.dtype).at[scatter_idx].set(x_rep)
            padded_x = padded[:N_EXPERTS * capacity].reshape(N_EXPERTS, capacity, D)
            h = jax.nn.gelu(jnp.einsum('ecd,edf->ecf', padded_x, w1), approximate=False)
            out_padded = jnp.einsum('ecf,efd->ecd', h, w2).reshape(N_EXPERTS * capacity, D)
            gather_idx = jnp.where(valid, slot, 0)
            out_rep = jnp.where(valid[:, None], out_padded[gather_idx], 0.0)
            out_w = out_rep * w_topk.reshape(-1)[:, None]
            return out_w.reshape(T, TOP_K, D).sum(axis=1).reshape(B, S, D)
        key = jax.random.key(seed)
        ks = jax.random.split(key, 12)
        s = 0.02
        return {'x': jax.random.normal(ks[0], (4, 256, D_MODEL), jnp.float32), 'qw': jax.random.normal(ks[1], (D_MODEL, D_MODEL), jnp.float32) * s, 'qb': jnp.zeros((D_MODEL,), jnp.float32), 'kw': jax.random.normal(ks[2], (D_MODEL, N_KV * HEAD_DIM), jnp.float32) * s, 'kb': jnp.zeros((N_KV * HEAD_DIM,), jnp.float32), 'vw': jax.random.normal(ks[3], (D_MODEL, N_KV * HEAD_DIM), jnp.float32) * s, 'vb': jnp.zeros((N_KV * HEAD_DIM,), jnp.float32), 'ow': jax.random.normal(ks[4], (D_MODEL, D_MODEL), jnp.float32) * s, 'ob': jnp.zeros((D_MODEL,), jnp.float32), 'gate_w': jax.random.normal(ks[5], (D_MODEL, N_EXPERTS), jnp.float32) * s, 'w1': jax.random.normal(ks[6], (N_EXPERTS, D_MODEL, 512), jnp.float32) * s, 'w2': jax.random.normal(ks[7], (N_EXPERTS, 512, D_MODEL), jnp.float32) * s, 'norm1_w': jnp.ones((D_MODEL,), jnp.float32), 'norm2_w': jnp.ones((D_MODEL,), jnp.float32)}
    _L0_ffn_all = _L0_ffn_setup()
    _L0_ffn_in = {k: v for k, v in _L0_ffn_all.items() if k in ('qw', 'qb', 'kw', 'kb', 'vw', 'vb', 'ow', 'ob', 'gate_w', 'w1', 'w2', 'norm1_w', 'norm2_w')}
    del _L0_ffn_all

    def _L1_xattn_setup():
        import jax, jax.numpy as jnp
        import numpy as np
        import math
        EMBED = 256
        HEADS = 16
        HEAD_DIM = EMBED // HEADS
        WINDOW = 128
        B, S = (2, 512)
        key = jax.random.key(seed)
        k1, k2, k3, k4 = jax.random.split(key, 4)
        values = jax.random.normal(k1, (B, S, EMBED), dtype=jnp.float32)
        keys = jax.random.normal(k2, (B, S, EMBED), dtype=jnp.float32)
        queries = jax.random.normal(k3, (B, S, EMBED), dtype=jnp.float32)
        idx = jnp.arange(S)
        band = (jnp.abs(idx[:, None] - idx[None, :]) <= WINDOW // 2).astype(jnp.int32)
        mask = band[None, None, :, :]
        w_out = jax.random.normal(k4, (EMBED, EMBED), dtype=jnp.float32) * (1.0 / math.sqrt(EMBED))
        b_out = jnp.zeros((EMBED,), dtype=jnp.float32)
        return {'values': values, 'keys': keys, 'queries': queries, 'mask': mask, 'w_out': w_out, 'b_out': b_out}
    _L1_xattn_all = _L1_xattn_setup()
    _L1_xattn_in = {k: v for k, v in _L1_xattn_all.items() if k in ('w_out', 'b_out')}
    del _L1_xattn_all

    def _L1_ffn_setup():
        import jax, jax.numpy as jnp
        import numpy as np
        NUM_HEADS = 16
        TOP_K = 2
        key = jax.random.key(seed)
        ks = jax.random.split(key, 5)
        B, S, D, E = (4, 512, 256, 8)
        scale = 0.02
        return {'x': jax.random.normal(ks[0], (B, S, D), dtype=jnp.float32), 'W_qkv': jax.random.normal(ks[1], (D, 3 * D), dtype=jnp.float32) * scale, 'b_qkv': jnp.zeros((3 * D,), dtype=jnp.float32), 'W_gate': jax.random.normal(ks[2], (D, E), dtype=jnp.float32) * scale, 'b_gate': jnp.zeros((E,), dtype=jnp.float32), 'W_experts': jax.random.normal(ks[3], (E, D, D), dtype=jnp.float32) * scale, 'b_experts': jnp.zeros((E, D), dtype=jnp.float32)}
    _L1_ffn_all = _L1_ffn_setup()
    _L1_ffn_in = {k: v for k, v in _L1_ffn_all.items() if k in ('W_qkv', 'b_qkv', 'W_gate', 'b_gate', 'W_experts', 'b_experts')}
    del _L1_ffn_all
    return {'x': x, 'ctx_1024': ctx_1024, 'mask_1x1xSxS2_ik0': mask_1x1xSxS2_ik0, 'g_xattn': g_xattn, 'g_ffn': g_ffn, 'L0_xattn_Wq': _L0_xattn_in['Wq'], 'L0_xattn_Wk': _L0_xattn_in['Wk'], 'L0_xattn_Wv': _L0_xattn_in['Wv'], 'L0_xattn_Wo': _L0_xattn_in['Wo'], 'L0_ffn_qw': _L0_ffn_in['qw'], 'L0_ffn_qb': _L0_ffn_in['qb'], 'L0_ffn_kw': _L0_ffn_in['kw'], 'L0_ffn_kb': _L0_ffn_in['kb'], 'L0_ffn_vw': _L0_ffn_in['vw'], 'L0_ffn_vb': _L0_ffn_in['vb'], 'L0_ffn_ow': _L0_ffn_in['ow'], 'L0_ffn_ob': _L0_ffn_in['ob'], 'L0_ffn_gate_w': _L0_ffn_in['gate_w'], 'L0_ffn_w1': _L0_ffn_in['w1'], 'L0_ffn_w2': _L0_ffn_in['w2'], 'L0_ffn_norm1_w': _L0_ffn_in['norm1_w'], 'L0_ffn_norm2_w': _L0_ffn_in['norm2_w'], 'L1_xattn_w_out': _L1_xattn_in['w_out'], 'L1_xattn_b_out': _L1_xattn_in['b_out'], 'L1_ffn_W_qkv': _L1_ffn_in['W_qkv'], 'L1_ffn_b_qkv': _L1_ffn_in['b_qkv'], 'L1_ffn_W_gate': _L1_ffn_in['W_gate'], 'L1_ffn_b_gate': _L1_ffn_in['b_gate'], 'L1_ffn_W_experts': _L1_ffn_in['W_experts'], 'L1_ffn_b_experts': _L1_ffn_in['b_experts']}

def reference(x, ctx_1024, mask_1x1xSxS2_ik0, g_xattn, g_ffn, L0_xattn_Wq, L0_xattn_Wk, L0_xattn_Wv, L0_xattn_Wo, L0_ffn_qw, L0_ffn_qb, L0_ffn_kw, L0_ffn_kb, L0_ffn_vw, L0_ffn_vb, L0_ffn_ow, L0_ffn_ob, L0_ffn_gate_w, L0_ffn_w1, L0_ffn_w2, L0_ffn_norm1_w, L0_ffn_norm2_w, L1_xattn_w_out, L1_xattn_b_out, L1_ffn_W_qkv, L1_ffn_b_qkv, L1_ffn_W_gate, L1_ffn_b_gate, L1_ffn_W_experts, L1_ffn_b_experts):
    import jax
    import jax.numpy as jnp

    def _L0_xattn_ref(x, context, Wq, Wk, Wv, Wo):
        import jax, jax.numpy as jnp
        import numpy as np
        HEADS = 16
        DIM_HEAD = 64
        QUERY_DIM = 256
        INNER = HEADS * DIM_HEAD
        SCALE = DIM_HEAD ** (-0.5)
        B, N, _ = x.shape
        M = context.shape[1]
        q = (x @ Wq).reshape(B, N, HEADS, DIM_HEAD)
        k = (context @ Wk).reshape(B, M, HEADS, DIM_HEAD)
        v = (context @ Wv).reshape(B, M, HEADS, DIM_HEAD)
        sim = jnp.einsum('bihd,bjhd->bhij', q, k) * SCALE
        attn = jax.nn.softmax(sim, axis=-1)
        out = jnp.einsum('bhij,bjhd->bihd', attn, v)
        out = out.reshape(B, N, INNER)
        return out @ Wo

    def _L0_ffn_ref(x, qw, qb, kw, kb, vw, vb, ow, ob, gate_w, w1, w2, norm1_w, norm2_w):
        import jax, jax.numpy as jnp
        import numpy as np
        D_MODEL = 256
        N_HEADS = 16
        N_KV = 4
        NUM_REP = N_HEADS // N_KV
        HEAD_DIM = D_MODEL // N_HEADS
        N_EXPERTS = 8
        TOP_K = 2
        CAP_FACTOR = 1.25
        EPS_NORM = 1e-06

        def _rmsnorm(x, w):
            var = jnp.mean(x * x, axis=-1, keepdims=True)
            return w * (x * jax.lax.rsqrt(var + EPS_NORM))

        def _gqa(x, qw, qb, kw, kb, vw, vb, ow, ob):
            B, S, D = x.shape
            q = (x @ qw + qb).reshape(B, S, N_HEADS, HEAD_DIM).transpose(0, 2, 1, 3)
            k = (x @ kw + kb).reshape(B, S, N_KV, HEAD_DIM).transpose(0, 2, 1, 3)
            v = (x @ vw + vb).reshape(B, S, N_KV, HEAD_DIM).transpose(0, 2, 1, 3)
            k = jnp.repeat(k, NUM_REP, axis=1)
            v = jnp.repeat(v, NUM_REP, axis=1)
            scores = jnp.einsum('bhqd,bhkd->bhqk', q, k) / np.sqrt(HEAD_DIM).astype(np.float32)
            attn = jax.nn.softmax(scores, axis=-1)
            out = jnp.einsum('bhqk,bhkd->bhqd', attn, v)
            out = out.transpose(0, 2, 1, 3).reshape(B, S, D)
            return out @ ow + ob

        def _moe(x, gate_w, w1, w2):
            B, S, D = x.shape
            T = B * S
            x_flat = x.reshape(T, D)
            capacity = int(CAP_FACTOR * T * TOP_K / N_EXPERTS)
            logits = x_flat @ gate_w
            probs = jax.nn.sigmoid(logits)
            _, sel = jax.lax.top_k(probs, TOP_K)
            w_topk = jnp.take_along_axis(probs, sel, axis=1)
            w_topk = w_topk / (jnp.sum(w_topk, axis=-1, keepdims=True) + 1e-06)
            flat_sel = sel.reshape(-1)
            em = jax.nn.one_hot(flat_sel, N_EXPERTS, dtype=jnp.int32)
            ranks = jnp.take_along_axis(jnp.cumsum(em, axis=0), flat_sel[:, None], axis=1)[:, 0] - 1
            valid = ranks < capacity
            slot = flat_sel * capacity + ranks
            scatter_idx = jnp.where(valid, slot, N_EXPERTS * capacity)
            x_rep = jnp.repeat(x_flat, TOP_K, axis=0)
            padded = jnp.zeros((N_EXPERTS * capacity + 1, D), x.dtype).at[scatter_idx].set(x_rep)
            padded_x = padded[:N_EXPERTS * capacity].reshape(N_EXPERTS, capacity, D)
            h = jax.nn.gelu(jnp.einsum('ecd,edf->ecf', padded_x, w1), approximate=False)
            out_padded = jnp.einsum('ecf,efd->ecd', h, w2).reshape(N_EXPERTS * capacity, D)
            gather_idx = jnp.where(valid, slot, 0)
            out_rep = jnp.where(valid[:, None], out_padded[gather_idx], 0.0)
            out_w = out_rep * w_topk.reshape(-1)[:, None]
            return out_w.reshape(T, TOP_K, D).sum(axis=1).reshape(B, S, D)
        src = x + _gqa(x, qw, qb, kw, kb, vw, vb, ow, ob)
        src = _rmsnorm(src, norm1_w)
        src = src + _moe(src, gate_w, w1, w2)
        return _rmsnorm(src, norm2_w)

    def _L1_xattn_ref(values, keys, queries, mask, w_out, b_out):
        import jax, jax.numpy as jnp
        import numpy as np
        import math
        EMBED = 256
        HEADS = 16
        HEAD_DIM = EMBED // HEADS
        WINDOW = 128
        B, S = (2, 512)
        N, q_len = (queries.shape[0], queries.shape[1])
        v = values.reshape(N, -1, HEADS, HEAD_DIM)
        k = keys.reshape(N, -1, HEADS, HEAD_DIM)
        q = queries.reshape(N, -1, HEADS, HEAD_DIM)
        energy = jnp.einsum('nqhd,nkhd->nhqk', q, k)
        energy = jnp.where(mask == 0, jnp.float32(-1e+20), energy)
        attn = jax.nn.softmax(energy / math.sqrt(EMBED), axis=3)
        out = jnp.einsum('nhql,nlhd->nqhd', attn, v).reshape(N, q_len, HEADS * HEAD_DIM)
        return out @ w_out.T + b_out

    def _L1_ffn_ref(x, W_qkv, b_qkv, W_gate, b_gate, W_experts, b_experts):
        import jax, jax.numpy as jnp
        import numpy as np
        NUM_HEADS = 16
        TOP_K = 2
        B, S, D = x.shape
        H = NUM_HEADS
        hd = D // H
        E = W_gate.shape[-1]
        qkv = (x @ W_qkv + b_qkv).reshape(B, S, 3, H, hd)
        q, k, v = (qkv[:, :, 0], qkv[:, :, 1], qkv[:, :, 2])
        attn = jnp.einsum('bqhd,bkhd->bhqk', q, k) / jnp.sqrt(jnp.asarray(hd, x.dtype))
        attn = jax.nn.softmax(attn, axis=-1)
        attn_out = jnp.einsum('bhqk,bkhd->bqhd', attn, v).reshape(B, S, D)
        gate = jax.nn.softmax(x @ W_gate + b_gate, axis=-1)
        top_g, top_i = jax.lax.top_k(gate, TOP_K)
        combine = jnp.sum(jax.nn.one_hot(top_i, E, dtype=x.dtype) * top_g[..., None], axis=2)
        expert_out = jnp.einsum('bsd,edf->bsef', x, W_experts) + b_experts
        moe_out = jnp.einsum('bsef,bse->bsf', expert_out, combine)
        return attn_out + moe_out
    x = x + jnp.tanh(g_xattn[0]) * _L0_xattn_ref(_layernorm(x, axis=-1), ctx_1024, L0_xattn_Wq, L0_xattn_Wk, L0_xattn_Wv, L0_xattn_Wo)
    x = x + jnp.tanh(g_ffn[0]) * _L0_ffn_ref(_layernorm(x, axis=-1), L0_ffn_qw, L0_ffn_qb, L0_ffn_kw, L0_ffn_kb, L0_ffn_vw, L0_ffn_vb, L0_ffn_ow, L0_ffn_ob, L0_ffn_gate_w, L0_ffn_w1, L0_ffn_w2, L0_ffn_norm1_w, L0_ffn_norm2_w)
    x = x + jnp.tanh(g_xattn[1]) * _L1_xattn_ref(ctx_1024, ctx_1024, _layernorm(x, axis=-1), mask_1x1xSxS2_ik0, L1_xattn_w_out, L1_xattn_b_out)
    x = x + jnp.tanh(g_ffn[1]) * _L1_ffn_ref(_layernorm(x, axis=-1), L1_ffn_W_qkv, L1_ffn_b_qkv, L1_ffn_W_gate, L1_ffn_b_gate, L1_ffn_W_experts, L1_ffn_b_experts)
    return x

_drawn_inputs = setup_inputs


def setup_inputs(seed=0):
    import zlib

    import numpy as np

    out = dict(_drawn_inputs(seed))
    spreads = {'g_ffn': (-1.0, 0.548),
     'L0_ffn_qb': (0.0, 0.8),
     'L0_ffn_kb': (0.0, 0.8),
     'L0_ffn_vb': (0.0, 0.1),
     'L0_ffn_ob': (0.0, 0.1),
     'L0_ffn_norm1_w': (1.0, 0.2),
     'L0_ffn_norm2_w': (1.0, 0.2),
     'L1_xattn_b_out': (0.0, 0.1),
     'L1_ffn_b_qkv': (0.0, 0.1),
     'L1_ffn_b_gate': (0.0, 0.1),
     'L1_ffn_b_experts': (0.0, 0.267)}
    factors = {'L0_ffn_qw': 8.0, 'L0_ffn_kw': 8.0}
    for name, (base, spread) in spreads.items():
        noise = np.random.default_rng([zlib.crc32(name.encode()), seed]).standard_normal(out[name].shape)
        drawn = base * np.exp(spread * noise) if base else spread * noise
        out[name] = jnp.asarray(drawn.astype(out[name].dtype))
    for name, factor in factors.items():
        out[name] = (out[name] * factor).astype(out[name].dtype)
    return out
```

```python
import numpy as np
import concourse.bass as bass
from concourse import mybir
from contextlib import ExitStack

B, S, D = 4, 512, 256
CTX = 1601
HEADS = 16
WIDE = 64
SLIM = 16
KV_HEADS = 4
EXPERTS, FFN = 8, 512
CAPACITY = int(1.25 * B * S * 2 / EXPERTS)
P = 128
BANK = 512
QT = S // P
FT = D // P
LN_EPS, RMS_EPS = 1e-5, 1e-6
MASKED = -1e20
GROUP = 4
PAD = P // GROUP
PAIRS = HEADS // 2
SLOTS = 8

CTX_TILE = 124
CTX_TILES = [(k, min(CTX_TILE, CTX - k)) for k in range(0, CTX, CTX_TILE)]
CTX_CHUNKS = [(0, 401), (401, 400), (801, 400), (1201, 400)]
SELF_TILES = [(k, P) for k in range(0, S, P)]
NKT = len(CTX_TILES)

TERMS = [(0, 0), (0, 1), (0, 2), (1, 0), (1, 1), (2, 0)]
STACK = len(TERMS) * SLIM

F32, BF16, I32 = mybir.dt.float32, mybir.dt.bfloat16, mybir.dt.int32
ALU, ACT, AX = mybir.AluOpType, mybir.ActivationFunctionType, mybir.AxisListType

C_IDENT, C_SELECT, C_TIE, C_EARLIER = 0, P, 3 * P, 3 * P + EXPERTS
C_ALL = 4 * P + EXPERTS


class Lane:

    def __init__(self, sem):
        self.sem, self.queue, self.marks, self.seen = sem, [], 0, {}

    def do(self, emit):
        self.queue.append(emit)

    def mark(self, emit):
        self.marks += 1
        self.queue.append(lambda e: emit(e).then_inc(self.sem, 1))
        return (self.sem, self.marks)

    def wait(self, *marks):
        for sem, value in marks:
            if self.seen.get(sem.name, 0) < value:
                self.seen[sem.name] = value
                self.queue.append(lambda e, s=sem, v=value: e.wait_ge(s, v))

    def step(self, emit, *marks):
        if self.marks:
            self.wait((self.sem, self.marks))
        self.wait(*marks)
        return self.mark(emit)

    def run(self, engine):
        for emit in self.queue:
            emit(engine)


class Landing:

    def __init__(self, lane, sem):
        self.lane, self.sem, self.count = lane, sem, 0

    def dma(self, out, in_):
        self.count += 16
        self.lane.do(lambda e: e.dma_start(out, in_).then_inc(self.sem, 16))
        return (self.sem, self.count)

    def all(self):
        return (self.sem, self.count)


class Ring:

    def __init__(self, views):
        self.views, self.freed, self.turn = views, [()] * len(views), 0

    def next(self):
        i = self.turn % len(self.views)
        self.turn += 1
        return i, self.views[i]


def mm(out, lhsT, rhs, start=True, stop=True):
    return lambda e: e.matmul(out, lhsT, rhs, start=start, stop=stop)


def transpose(out, in_, ident):
    return lambda e: e.transpose(out, in_, ident)


def copy(out, in_):
    return lambda e: e.tensor_copy(out, in_)


def acopy(out, in_):
    return lambda e: e.activation(out, in_, ACT.Copy)


def act(out, in_, func, scale=1.0):
    return lambda e: e.activation(out, in_, func, scale=scale)


def tt(out, a, b, op):
    return lambda e: e.tensor_tensor(out, a, b, op)


def ts(out, a, s1, op0, s2=None, op1=None):
    if op1 is None:
        return lambda e: e.tensor_scalar(out, a, s1, None, op0)
    return lambda e: e.tensor_scalar(out, a, s1, s2, op0, op1)


def stt(out, a, s, b, op0, op1):
    return lambda e: e.scalar_tensor_tensor(out=out, in0=a, scalar=s, in1=b, op0=op0, op1=op1)


def rmax(out, in_):
    return lambda e: e.reduce_max(out, in_, AX.X)


def turn(out, in_):
    return lambda e: e.transpose(out, in_)


def blocks(tile):
    return tile[:, :].rearrange("p (b r) -> p b r", r=32)


def memset(ap, value):
    return lambda e: e.memset(ap, value)


def together(main, prep, ratio):
    debt = 0.0
    for _ in main:
        debt += ratio
        while debt >= 1:
            debt -= 1
            next(prep, None)
    for _ in prep:
        pass


def flamingo(nc, t, out):
    ctx = ExitStack()
    with ctx:
        def sb(name, shape, dt=F32):
            return ctx.enter_context(nc.sbuf_tensor(name, shape, dt))

        def sem(name):
            return ctx.enter_context(nc.semaphore(name))

        x_sb = sb("x_sb", [P, QT, D])
        xn = sb("xn", [P, QT, D])
        xnT = sb("xnT", [P, FT, S])
        ctxT = sb("ctxT", [P, FT, CTX])
        values = sb("values", [P, NKT * 512])
        kbuf = sb("kbuf", [P, 2, GROUP, CTX], BF16)
        qbuf = sb("qbuf", [P, 2, 6, S], BF16)
        exps = sb("exps", [P, SLOTS, 2, S])
        stage_ws = sb("stage_ws", [P, NKT * 512])
        outT = sb("outT", [P, PAIRS, S])
        kparts = sb("kparts", [P, 3, CTX], BF16)
        qparts = sb("qparts", [P, 3, S], BF16)
        rest = sb("rest", [P, S])
        raw = sb("raw", [P, S])
        inverse = sb("inverse", [P, S // 32])
        w_pair = sb("w_pair", [P, 2, 2, FT, P])
        ident_f = sb("ident_f", [P, C_ALL])
        ident_b = sb("ident_b", [P, P], BF16)
        select_b = sb("select_b", [P, 2, P], BF16)
        earlier_b = sb("earlier_b", [P, P], BF16)
        ones_b = sb("ones_b", [P, P], BF16)
        ones_f = sb("ones_f", [P, WIDE])
        max_chunks = sb("max_chunks", [P, GROUP, QT, 4])
        neg_max = sb("neg_max", [P, GROUP, QT])
        neg_rest = sb("neg_rest", [P, GROUP, QT])
        max_junk = sb("max_junk", [P, 401], BF16)
        neg_cols = sb("neg_cols", [P, QT, P], BF16)
        neg_rows = sb("neg_rows", [P, 2, S], BF16)
        stats = sb("stats", [P, QT, 6])
        moments = sb("moments", [P, QT, 2])
        rstd = sb("rstd", [P, QT])
        gates = sb("gates", [P, 4])
        prob = sb("prob", [P, QT, EXPERTS])
        prob2 = sb("prob2", [P, QT, EXPERTS])
        hit = sb("hit", [P, QT, EXPERTS])
        pick1 = sb("pick1", [P, QT, EXPERTS])
        pick2 = sb("pick2", [P, QT, EXPERTS])
        best1 = sb("best1", [P, QT])
        best2 = sb("best2", [P, QT])
        combine = sb("combine", [P, QT, EXPERTS])
        chosen_b = sb("chosen_b", [P, QT, EXPERTS], BF16)
        before_b = sb("before_b", [P, EXPERTS], BF16)
        before_f = sb("before_f", [P, EXPERTS])
        combT = sb("combT", [EXPERTS, S])
        gqa_w = sb("gqa_w", [P, FT, D + 2 * KV_HEADS * SLIM])
        out_w = sb("out_w", [P, GROUP, D])
        gate_w0 = sb("gate_w0", [P, FT, EXPERTS])
        gate_w1 = sb("gate_w1", [P, FT, EXPERTS])
        qk_bias = sb("qk_bias", [P, 7])
        rows = sb("rows", [P, 4 * D + KV_HEADS * SLIM + D + EXPERTS])
        b_exp = sb("b_exp", [EXPERTS, D])

        row_ob, row_n1, row_n2, row_bo = (rows[:, i * D:(i + 1) * D] for i in range(4))
        row_vb = rows[:, 4 * D:4 * D + KV_HEADS * SLIM]
        row_v1 = rows[:, 4 * D + KV_HEADS * SLIM:5 * D + KV_HEADS * SLIM]
        row_bg = rows[:, 5 * D + KV_HEADS * SLIM:]

        ident = ident_f[:, C_IDENT:C_IDENT + P]
        tie = ident_f[:, C_TIE:C_TIE + EXPERTS]

        work_t = ctx.enter_context(nc.psum_tensor("work", [P, 2, BANK], F32))
        score_t = ctx.enter_context(nc.psum_tensor("score", [P, 2, 2, BANK], F32))
        pv_t = ctx.enter_context(nc.psum_tensor("pv", [P, 2, BANK], F32))
        work = Ring([work_t[:, i, :] for i in range(2)])
        score = Ring([score_t[:, i, :, :] for i in range(2)])
        pv = Ring([pv_t[:, i, :] for i in range(2)])
        expo = Ring([exps[:, i, :, :] for i in range(SLOTS)])

        pool_sum = stage_ws[:, 0:2048].rearrange("p (h j n) -> p h j n", h=2, j=2)
        wv_sb = stage_ws[:, 2048:4096].rearrange("p (f n) -> p f n", f=FT)
        wo_sb = stage_ws[:, 4096:6144].rearrange("p (g n) -> p g n", g=PAIRS)
        w1_sb = stage_ws[:, 0:2048].rearrange("p (s f n) -> p s f n", s=2, f=FT)
        w2_sb = stage_ws[:, 2048:4096].rearrange("p (s f n) -> p s f n", s=2, f=FFN // P)
        hidden = outT[:, :, :].rearrange("p (s f) n -> p s f n", s=2)
        masks = stage_ws[:, :].bitcast(BF16)
        maskT_sb = masks[:, 0:NKT * S].rearrange("p (k n) -> p k n", k=NKT)
        maskQ_sb = masks[:, NKT * S:NKT * S + QT * CTX].rearrange("p (q n) -> p q n", q=QT)
        we_sb = stage_ws[:, 0:4096].rearrange("p (e f n) -> p e f n", e=EXPERTS, f=FT)
        wqkv_sb = stage_ws[:, 4096:4096 + FT * 3 * D].rearrange("p (f n) -> p f n", f=FT)
        v_wide = values[:, :].rearrange("p (s k n) -> p s k n", s=2, k=NKT)
        v_slim = values[:, :].rearrange("p (k h c) -> p k h c", k=NKT, h=HEADS)
        ctx_rows = exps[:, 0:4, :, :].rearrange("p a b n -> p (a b n)")[:, 0:NKT * D]
        mask_ints = exps[:, :, :, :].rearrange("p a b n -> p (a b n)").bitcast(I32)

        pe, sc, ve, po, sp = (Lane(sem("s_" + n)) for n in ("pe", "sc", "ve", "po", "sp"))

        def landing(name):
            return Landing(sp, sem("d_" + name))

        l_const, l_x, l_ctxT, l_ws, l_wp = (landing(n) for n in ("const", "x", "ctxT", "ws", "wp"))
        l_pair = [landing(f"pair{i}") for i in range(2)]
        l_kst = [landing(f"kst{i}") for i in range(2)]
        l_qst = [landing(f"qst{i}") for i in range(2)]
        l_neg = [landing(f"neg{i}") for i in range(2)]
        l_exp = [landing(f"expert{i}") for i in range(2)]
        l_scratch, l_kctx, l_mask, l_ctxr = (landing(n) for n in ("scratch", "kctx", "mask", "ctxr"))
        l_out = landing("out")

        free = {n: [] for n in ("ws", "values", "outT", "kparts", "qparts", "out_w", "ctxT", "x")}
        kfree, qfree, pairfree, vfree = [(), ()], [(), ()], [(), ()], [(), ()]
        negfree = [(), ()]

        l_const.dma(ident_f[:, :], t["consts"])
        l_const.dma(gqa_w[:, :, :], t["gqa_w"])
        l_const.dma(gate_w0[:, :, :], t["gate0"])
        l_const.dma(gate_w1[:, :, :], t["gate1"])
        l_const.dma(qk_bias[:, :], t["qk_bias"])
        for row, src in ((row_ob, t["L0_ffn_ob"]), (row_n1, t["L0_ffn_norm1_w"]),
                         (row_n2, t["L0_ffn_norm2_w"]), (row_bo, t["L1_xattn_b_out"]),
                         (row_vb, t["L0_ffn_vb"]), (row_v1, t["L1_ffn_b_qkv"][2 * D:3 * D]),
                         (row_bg, t["L1_ffn_b_gate"])):
            l_const.dma(row, src.partition_broadcast(P))
        l_const.dma(gates[:, 0:2], t["g_xattn"].partition_broadcast(P))
        l_const.dma(gates[:, 2:4], t["g_ffn"].partition_broadcast(P))
        l_const.dma(b_exp[:, :], t["L1_ffn_b_experts"])

        def load_x(b):
            sp.wait(*free["x"])
            return l_x.dma(x_sb[:, :, :], t["x"][b].rearrange("(q p) n -> p q n", p=P))

        def load_ctxT(b):
            sp.wait(*free["ctxT"])
            return l_ctxT.dma(ctxT[:, :, :], t["ctxT"][b].rearrange("(f p) n -> p f n", p=P))

        x_in, ctxT_in = load_x(0), load_ctxT(0)

        po.mark(memset(ones_f[:, :], 1.0))
        po.mark(memset(ones_b[:, :], 1.0))
        po.mark(memset(before_f[:, :], 0.0))
        pool_ready = po.mark(memset(neg_cols[:, :, :], 0.0))
        sc.wait(l_const.all())
        gates_ready = sc.step(act(gates[:, :], gates[:, :], ACT.Tanh))
        ve.wait(l_const.all(), pool_ready, gates_ready)
        ve.step(copy(ident_b[:, :], ident))
        ve.step(copy(select_b[:, :, :], ident_f[:, C_SELECT:C_TIE].rearrange("p (h n) -> p h n", h=2)))
        consts_ready = ve.step(copy(earlier_b[:, :], ident_f[:, C_EARLIER:C_ALL]))
        pe.wait(consts_ready, l_const.all())
        po.wait(consts_ready)

        maskT_dram = nc.dram_tensor("maskT_add", [NKT * CTX_TILE, S], BF16, kind="Internal").ap()
        maskQ_dram = nc.dram_tensor("maskQ_add", [S, CTX], BF16, kind="Internal").ap()
        full = NKT - 1
        tail = CTX_TILES[-1][1]

        def key_rows(ap):
            return (ap[0:full * CTX_TILE].rearrange("(k p) n -> p k n", p=CTX_TILE),
                    ap[full * CTX_TILE:CTX])

        mt = mask_ints[:, 0:NKT * S].rearrange("p (k n) -> p k n", k=NKT)
        a, z = key_rows(t["maskT"])
        l_mask.dma(mt[0:CTX_TILE, 0:full, :], a)
        l_mask.dma(mt[0:tail, full, :], z)
        ve.step(ts(maskT_sb[0:CTX_TILE, 0:full, :], mt[0:CTX_TILE, 0:full, :], 0.0, ALU.is_equal,
                   MASKED, ALU.mult), l_mask.all())
        done = ve.step(ts(maskT_sb[0:tail, full, :], mt[0:tail, full, :], 0.0, ALU.is_equal,
                          MASKED, ALU.mult))
        sp.wait(done)
        a, z = key_rows(maskT_dram)
        l_scratch.dma(a, maskT_sb[0:CTX_TILE, 0:full, :])
        l_scratch.dma(z, maskT_sb[0:tail, full, :])
        mq = mask_ints[:, 0:QT * CTX].rearrange("p (q n) -> p q n", q=QT)
        l_mask.dma(mq, t["maskQ"].rearrange("(q p) n -> p q n", p=P))
        done = ve.step(ts(maskQ_sb[:, :, :], mq, 0.0, ALU.is_equal, MASKED, ALU.mult), l_mask.all())
        sp.wait(done)
        masks_stored = l_scratch.dma(maskQ_dram.rearrange("(q p) n -> p q n", p=P), maskQ_sb)
        free["ws"] = [masks_stored]
        for i in range(SLOTS):
            expo.freed[i] = (done,)

        def inverse_root(eps):
            ve.step(ts(rstd[:, :], rstd[:, :], eps, ALU.add))
            last = ve.step(lambda e: e.reciprocal(rstd[:, :], rstd[:, :]))
            root = sc.step(act(rstd[:, :], rstd[:, :], ACT.Sqrt), last)
            ve.wait(root)
            return root

        def rms(src, eps, after=()):
            for q in range(QT):
                ve.step(lambda e, q=q: e.tensor_tensor_reduce(
                    out=rest[:, 0:D], in0=src[:, q, :], in1=src[:, q, :], scale=1.0, scalar=0.0,
                    op0=ALU.mult, op1=ALU.add, accum_out=rstd[:, q:q + 1]), *after)
            ve.step(ts(rstd[:, :], rstd[:, :], 1.0 / D, ALU.mult))
            return inverse_root(eps)

        def layer_norm(*after):
            for q in range(QT):
                ve.step(lambda e, q=q: e.bn_stats(stats[:, q, :], x_sb[:, q, :]), *after)
                ve.step(lambda e, q=q: e.bn_aggr(moments[:, q, :], stats[:, q, :]))
            ve.step(copy(rstd[:, :], moments[:, :, 1]))
            inverse_root(LN_EPS)
            for q in range(QT):
                last = ve.step(ts(xn[:, q, :], x_sb[:, q, :], moments[:, q, 0:1], ALU.subtract,
                                  rstd[:, q:q + 1], ALU.mult))
            return last

        def transpose_xn(ready, *readers):
            for f in range(FT):
                i, bank = work.next()
                pe.wait(ready, *work.freed[i])
                for q in range(QT):
                    done = pe.mark(transpose(bank[:, q * P:(q + 1) * P],
                                             xn[:, q, f * P:(f + 1) * P], ident))
                last = sc.step(acopy(xnT[:, f, :], bank), done, *readers)
                work.freed[i] = (last,)
            return last

        def split(src, parts, n, *after):
            high = sc.step(acopy(parts[0], src), *after)
            read = ve.step(tt(rest[0:n[0], 0:n[1]], src, parts[0], ALU.subtract), high, *after)
            ve.step(copy(parts[1], rest[0:n[0], 0:n[1]]))
            last = ve.step(tt(parts[2], rest[0:n[0], 0:n[1]], parts[1], ALU.subtract))
            return read, last

        def negate_maximum(heads, chunks, column, *after):
            if chunks > 1:
                ve.step(rmax(neg_max[:, 0:heads, :], max_chunks[:, 0:heads, :, 0:chunks]), *after)
                src = neg_max[:, 0:heads, :]
            else:
                src = max_chunks[:, 0:heads, :, 0]
                ve.wait(*after)
            ve.step(ts(neg_max[:, 0:heads, :], src, -1.0, ALU.mult))
            src = neg_max[:, 0:heads, :]
            for i in range(3):
                c = column(i)
                part = neg_cols[:, :, c:c + heads].rearrange("p q h -> p h q")
                last = ve.step(copy(part, src))
                if i < 2:
                    ve.step(tt(neg_rest[:, 0:heads, :], src, part, ALU.subtract))
                    src = neg_rest[:, 0:heads, :]
            return last

        def rows_of_maximum(slot, ready):
            i, bank = work.next()
            pe.wait(ready, *work.freed[i])
            for q in range(QT):
                done = pe.mark(mm(bank[:, q * P:(q + 1) * P], neg_cols[:, q, :], ident_b[:, :]))
            last = sc.step(acopy(neg_rows[:, slot, :], bank), done, *negfree[slot])
            work.freed[i] = (last,)
            return done, last

        def project_out(weights, tiles, ready):
            for q in range(0, QT, 2):
                i, bank = work.next()
                pe.wait(*ready, *work.freed[i])
                for j in range(2):
                    for g in range(tiles):
                        last = mm(bank[:, j * D:(j + 1) * D],
                                  outT[:, g, (q + j) * P:(q + j + 1) * P], weights[:, g, :],
                                  start=g == 0, stop=g == tiles - 1)
                        done = pe.mark(last) if g == tiles - 1 else pe.do(last)
                for j in range(2):
                    yield i, q + j, bank[:, j * D:(j + 1) * D], done

        def load_pair(p):
            sp.wait(*pairfree[p % 2])
            return l_pair[p % 2].dma(w_pair[:, p % 2, :, :, :], t["w_pair"][p])

        def wide_prep(p, pair_in, xnT_ready, ws_ready, state):
            s = p % 2
            if p % 2 == 0:
                v_slot = (p // 2) % 2
                for k in range(0, NKT, 2):
                    i, bank = work.next()
                    pe.wait(ctxT_in_now[0], ws_ready, *work.freed[i])
                    for j, (k0, kn) in enumerate(CTX_TILES[k:k + 2]):
                        for f in range(FT):
                            op = mm(bank[0:kn, j * D:(j + 1) * D], ctxT[:, f, k0:k0 + kn],
                                    wv_sb[:, f, (p // 2) * D:(p // 2 + 1) * D], start=f == 0, stop=f == FT - 1)
                            done = pe.mark(op) if f == FT - 1 else pe.do(op)
                    both = len(CTX_TILES[k:k + 2])
                    kn = CTX_TILES[k][1]
                    last = sc.step(acopy(v_wide[0:kn, v_slot, k:k + both, :],
                                         bank[0:kn, 0:both * D].rearrange("p (j n) -> p j n", j=both)),
                                   done, *vfree[v_slot])
                    work.freed[i] = (last,)
                    yield
                state["v"][v_slot] = last
            for c0, cn in CTX_CHUNKS:
                i, bank = work.next()
                pe.wait(pair_in, ctxT_in_now[0], *work.freed[i])
                for f in range(FT):
                    done = pe.mark(mm(bank[:, 0:cn], w_pair[:, s, 1, f, :], ctxT[:, f, c0:c0 + cn],
                                      start=f == 0, stop=f == FT - 1))
                read, last = split(bank[:, 0:cn], [kparts[:, n, c0:c0 + cn] for n in range(3)],
                                   (P, cn), done, *free["kparts"])
                work.freed[i] = (read,)
                yield
            sp.wait(last, *kfree[s])
            for h in range(2):
                own, other = slice(64 * h, 64 * h + 64), slice(64 - 64 * h, 128 - 64 * h)
                for kind in range(2):
                    l_kst[s].dma(kbuf[own, s, 2 * h + kind, :], kparts[own, 0, :])
                l_kst[s].dma(kbuf[other, s, 2 * h:2 * h + 2, :], kparts[own, 1:3, :])
            free["kparts"] = [l_kst[s].all()]
            i, bank = work.next()
            pe.wait(pair_in, xnT_ready, *work.freed[i])
            for f in range(FT):
                done = pe.mark(mm(bank, w_pair[:, s, 0, f, :], xnT[:, f, :], start=f == 0, stop=f == FT - 1))
            pairfree[s] = (done,)
            state["proj"] = done
            read, last = split(bank, [qparts[:, n, :] for n in range(3)], (P, S), done, *free["qparts"])
            work.freed[i] = (read,)
            sp.wait(last, *qfree[s])
            for h in range(2):
                own, other = slice(64 * h, 64 * h + 64), slice(64 - 64 * h, 128 - 64 * h)
                l_qst[s].dma(qbuf[own, s, 3 * h:3 * h + 3, :], qparts[own, :, :])
                l_qst[s].dma(qbuf[other, s, 3 * h:3 * h + 2, :], qparts[own, 0:2, :])
                l_qst[s].dma(qbuf[other, s, 3 * h + 2, :], qparts[own, 0, :])
            free["qparts"] = [l_qst[s].all()]
            yield
            pe.wait(l_kst[s].all(), l_qst[s].all())
            for h in range(2):
                for q in range(QT):
                    for c, (c0, cn) in enumerate(CTX_CHUNKS):
                        i, bank = work.next()
                        pe.wait(*work.freed[i])
                        for kind in range(2):
                            op = mm(bank[:, 0:cn], qbuf[:, s, 3 * h + kind, q * P:(q + 1) * P],
                                    kbuf[:, s, 2 * h, c0:c0 + cn], start=kind == 0, stop=kind == 1)
                            done = pe.mark(op) if kind else pe.do(op)
                        ve.wait(done, *state["neg_read"])
                        last = ve.mark(rmax(max_chunks[:, h, q, c:c + 1], bank[:, 0:cn]))
                        work.freed[i] = (last,)
                        yield
            ready = negate_maximum(2, len(CTX_CHUNKS), lambda i: 2 * i, *state["neg_read"])
            read, last = rows_of_maximum(s, ready)
            state["neg_read"] = (read,)
            state["neg"][s] = last
            yield

        def wide_main(p, state):
            s = p % 2
            v_slot = (p // 2) % 2
            pe.wait(state["neg"][s], state["v"][v_slot], l_kst[s].all(), l_qst[s].all())
            o, pv_bank = pv.next()
            pending = []
            last_add = [None, None]

            def values_of(step):
                k, tiles, made = step
                for j, (k0, kn) in enumerate(tiles):
                    for h in range(2):
                        i, view, ready = made[h]
                        pe.wait(ready, *pv.freed[o])
                        op = mm(pv_bank[64 * h:64 * h + 64, :],
                                v_wide[0:kn, v_slot, k + j, 128 * (p % 2) + 64 * h:128 * (p % 2) + 64 * h + 64],
                                view[0:kn, j, :], start=k + j == 0, stop=k + j == NKT - 1)
                        last = pe.mark(op)
                for h in range(2):
                    i = made[h][0]
                    expo.freed[i] = expo.freed[i] + (last,)
                return last

            for k in range(0, NKT, 2):
                tiles = CTX_TILES[k:k + 2]
                made = []
                for h in range(2):
                    i, banks = score.next()
                    pe.wait(*score.freed[i])
                    for j, (k0, kn) in enumerate(tiles):
                        out_ = banks[0:kn, j, :]
                        for kind in range(3):
                            pe.do(mm(out_, kbuf[:, s, 2 * h + kind // 2, k0:k0 + kn],
                                     qbuf[:, s, 3 * h + kind, :], start=kind == 0, stop=False))
                        done = pe.mark(mm(out_, select_b[:, h, 0:kn], neg_rows[:, s, :], start=False))
                    kn = tiles[0][1]
                    n = len(tiles)
                    e, view = expo.next()
                    sc.wait(done, *expo.freed[e])
                    ready = sc.mark(act(view[0:kn, 0:n, :], banks[0:kn, 0:n, :], ACT.Exp, WIDE ** -0.5))
                    score.freed[i] = (ready,)
                    made.append((e, view, ready))
                    po.wait(ready)
                    total = pool_sum[0:kn, h, 0:n, :]
                    if k == 0:
                        add = po.step(memset(pool_sum[:, h, :, :], 0.0), *state["sum_read"][h])
                    add = po.step(tt(total, total, view[0:kn, 0:n, :], ALU.add))
                    last_add[h] = add
                    expo.freed[e] = (add,)
                    yield
                pending.append((k, tiles, made))
                if len(pending) > 1:
                    values_of(pending.pop(0))
                    yield
            kfree[s] = qfree[s] = negfree[s] = (done,)
            last = values_of(pending.pop(0))
            if p % 2:
                vfree[v_slot] = (last,)
            taken = sc.step(acopy(raw[:, :], pv_bank), last, *state["raw_read"])
            pv.freed[o] = (taken,)
            yield
            i, bank = work.next()
            pe.wait(*work.freed[i])
            for h in range(2):
                pe.wait(last_add[h])
                for j in range(2):
                    done = pe.mark(mm(bank[64 * h:64 * h + 64, :], ones_f[:, :], pool_sum[:, h, j, :],
                                      start=j == 0, stop=j == 1))
                state["sum_read"][h] = (done,)
            ve.step(turn(rest[:, :], raw[:, :]), taken)
            read = ve.step(turn(raw[:, :], bank), done)
            work.freed[i] = (read,)
            ve.step(lambda e: e.reciprocal(inverse[:, :], blocks(raw)[:, :, 0]))
            ve.step(tt(blocks(rest), blocks(rest),
                       inverse[:, :].unsqueeze(2).to_broadcast([P, S // 32, 32]), ALU.mult))
            last = ve.step(turn(outT[:, p, :], rest[:, :]), *free["outT"])
            state["raw_read"] = (last,)
            state["out"] = last
            yield

        def context_parts(b, k_dram):
            for f in range(FT):
                for c0, cn in CTX_CHUNKS:
                    _, last = split(ctxT[:, f, c0:c0 + cn], [kparts[:, n, c0:c0 + cn] for n in range(3)],
                                    (P, cn), *free["kparts"])
                    yield
                sp.wait(last)
                for n in range(3):
                    l_kctx.dma(k_dram[n, f * P:(f + 1) * P, :], kparts[:, n, :])
                free["kparts"] = [l_kctx.all()]
            free["ctxT"] = [last, context_matmuls[0]]
            yield

        def slim_load(g, k_dram, k_in, kv_of, keys, q_dram, q_in):
            s = g % 2
            sp.wait(k_in, q_in, *kfree[s])
            for n, (qp, kp) in enumerate(TERMS):
                r = slice(n * SLIM, (n + 1) * SLIM)
                if kv_of:
                    l_kst[s].dma(kbuf[r, s, 0, 0:keys], k_dram[kp, g * SLIM:(g + 1) * SLIM, :])
                else:
                    l_kst[s].dma(kbuf[r, s, :, 0:keys],
                                 k_dram[kp, g * 64:(g + 1) * 64, :].rearrange("(h d) n -> d h n", d=SLIM))
            sp.wait(*qfree[s])
            for n, (qp, kp) in enumerate(TERMS):
                r = slice(n * SLIM, (n + 1) * SLIM)
                l_qst[s].dma(qbuf[r, s, 0:GROUP, :],
                             q_dram[qp, g * 64:(g + 1) * 64, :].rearrange("(h d) n -> d h n", d=SLIM))

        def slim_prep(g, grouped, keys, masked, state):
            s = g % 2
            chunks = CTX_CHUNKS if keys == CTX else [(0, keys)]
            pe.wait(l_kst[s].all(), l_qst[s].all())
            for h in range(GROUP):
                for q in range(QT):
                    for c, (c0, cn) in enumerate(chunks):
                        i, bank = work.next()
                        pe.wait(*work.freed[i])
                        done = pe.mark(mm(bank[:, 0:cn], qbuf[0:STACK, s, h, q * P:(q + 1) * P],
                                          kbuf[0:STACK, s, 0 if grouped else h, c0:c0 + cn]))
                        ve.wait(done, *state["neg_read"])
                        if masked:
                            last = ve.mark(lambda e, h=h, q=q, c=c, c0=c0, cn=cn, bank=bank: e.tensor_tensor_reduce(
                                out=max_junk[:, 0:cn], in0=bank[:, 0:cn], in1=maskQ_sb[:, q, c0:c0 + cn],
                                scale=1.0, scalar=-3e38, op0=ALU.add, op1=ALU.max,
                                accum_out=max_chunks[:, h, q, c:c + 1]))
                            ve.wait(last)
                        else:
                            last = ve.mark(rmax(max_chunks[:, h, q, c:c + 1], bank[:, 0:cn]))
                        work.freed[i] = (last,)
                        yield
            ready = negate_maximum(GROUP, len(chunks), lambda i: GROUP * i, *state["neg_read"])
            read, last = rows_of_maximum(s, ready)
            state["neg_read"] = (read,)
            sp.wait(last)
            for n in range(3):
                l_neg[s].dma(qbuf[STACK + n:STACK + n + 1, s, 0:GROUP, :],
                             neg_rows[GROUP * n:GROUP * n + GROUP, s, :])
            negfree[s] = (l_neg[s].all(),)
            yield

        def slim_main(g, grouped, tiles, scale, masked, values_ready, state):
            s = g % 2
            pe.wait(l_neg[s].all(), l_kst[s].all(), l_qst[s].all(), *values_ready)
            o, pv_bank = pv.next()
            pending = []

            def values_of(step):
                k, some, made = step
                for j, (k0, kn) in enumerate(some):
                    for h in range(GROUP):
                        i, view, ready = made[h]
                        pe.wait(ready, *pv.freed[o])
                        last = pe.mark(mm(pv_bank[PAD * h:PAD * h + PAD, :],
                                          v_slim[0:kn, k + j, g if grouped else GROUP * g + h, :],
                                          view[0:kn, j, :], start=k + j == 0, stop=k + j == len(tiles) - 1))
                for h in range(GROUP):
                    expo.freed[made[h][0]] = (last,)
                return last

            for k in range(0, len(tiles), 2):
                some = tiles[k:k + 2]
                made = []
                for h in range(GROUP):
                    i, banks = score.next()
                    pe.wait(*score.freed[i])
                    for j, (k0, kn) in enumerate(some):
                        op = mm(banks[0:kn, j, :], kbuf[0:STACK + 3, s, 0 if grouped else h, k0:k0 + kn],
                                qbuf[0:STACK + 3, s, h, :], stop=not masked)
                        if masked:
                            pe.do(op)
                            op = mm(banks[0:kn, j, :], ident_b[0:kn, 0:kn], maskT_sb[0:kn, k + j, :], start=False)
                        done = pe.mark(op)
                    kn, n = some[0][1], len(some)
                    e, view = expo.next()
                    sc.wait(done, *expo.freed[e])
                    ready = sc.mark(act(view[0:kn, 0:n, :], banks[0:kn, 0:n, :], ACT.Exp, scale))
                    score.freed[i] = (ready,)
                    made.append((e, view, ready))
                    yield
                pending.append((k, some, made))
                if len(pending) > 1:
                    values_of(pending.pop(0))
                    yield
            kfree[s] = qfree[s] = (done,)
            last = values_of(pending.pop(0))
            state["pv_last"] = last
            taken = sc.step(acopy(raw[:, :], pv_bank), last, *state["raw_read"])
            pv.freed[o] = (taken,)
            ve.step(turn(rest[:, :], raw[:, :]), taken)
            ve.step(lambda e: e.reciprocal(inverse[:, :], blocks(rest)[:, :, SLIM]))
            ve.step(tt(blocks(rest)[:, :, 0:SLIM], blocks(rest)[:, :, 0:SLIM],
                       inverse[:, :].unsqueeze(2).to_broadcast([P, S // 32, SLIM]), ALU.mult))
            last = ve.step(turn(outT[:, g, :], rest[:, :]), *free["outT"])
            state["raw_read"] = (last,)
            state["out"] = last
            yield

        def slim_attention(grouped, keys, scale, masked, k_dram, k_in, q_dram, q_in, values_ready,
                           masks_ready=()):
            tiles = CTX_TILES if keys == CTX else SELF_TILES
            state = {"neg_read": (), "raw_read": (), "out": None}
            args = (k_dram, k_in, grouped, keys, q_dram, q_in)
            slim_load(0, *args)
            slim_load(1, *args)
            ve.wait(*masks_ready)
            pe.wait(*masks_ready)
            for _ in slim_prep(0, grouped, keys, masked, state):
                pass
            ratio = len(CTX_CHUNKS) * 16 / 35 if keys == CTX else 16 / 11
            for g in range(HEADS // GROUP):
                if g + 1 < HEADS // GROUP:
                    nxt = slim_prep(g + 1, grouped, keys, masked, state)
                else:
                    nxt = iter(())
                together(slim_main(g, grouped, tiles, scale, masked, values_ready, state), nxt, ratio)
                if g + 2 < HEADS // GROUP:
                    slim_load(g + 2, *args)
            free["values"] = [state["pv_last"]]
            return state["out"]

        def ones_in_values(tiles, heads):
            return po.step(memset(v_slim[:, 0:tiles, 0:heads, SLIM:PAD], 1.0), *free["values"])

        def scratch(name, rows_, n):
            return nc.dram_tensor(name, [3, rows_, n], BF16, kind="Internal").ap()

        def part_slots():
            return ([[kparts[:, n, c * S:(c + 1) * S] for n in range(3)] for c in range(3)]
                    + [[qparts[:, n, :] for n in range(3)]])

        def top_two(src_ready):
            def wide(ap):
                return ap.unsqueeze(2).to_broadcast([P, QT, EXPERTS])

            tie_b = tie.unsqueeze(1).to_broadcast([P, QT, EXPERTS])
            src = prob
            ve.wait(src_ready)
            for pick, best in ((pick1, best1), (pick2, best2)):
                ve.step(rmax(best[:, :], src[:, :, :]))
                ve.step(tt(hit[:, :, :], src[:, :, :], wide(best[:, :]), ALU.is_equal))
                ve.step(tt(hit[:, :, :], hit[:, :, :], tie_b, ALU.mult))
                ve.step(rmax(rstd[:, :], hit[:, :, :]))
                last = ve.step(tt(pick[:, :, :], hit[:, :, :], wide(rstd[:, :]), ALU.is_equal))
                if pick is pick1:
                    ve.step(stt(prob2[:, :, :], pick1[:, :, :], -4.0, prob[:, :, :], ALU.mult, ALU.add))
                    src = prob2
            return last

        def gate_logits(weights, ready):
            i, bank = work.next()
            pe.wait(ready, *work.freed[i])
            for q in range(QT):
                for f in range(FT):
                    done = pe.mark(mm(bank[:, q * EXPERTS:(q + 1) * EXPERTS], xnT[:, f, q * P:(q + 1) * P],
                                      weights[:, f, :], start=f == 0, stop=f == FT - 1))
            return i, bank[:, 0:QT * EXPERTS].rearrange("p (q e) -> p q e", q=QT), done

        context_matmuls = [None]
        for b in range(B):
            if b >= BATCHES:
                break
            ctxT_in_now = [ctxT_in]
            sp.wait(*free["ws"])
            l_ws.dma(wv_sb, t["wv"])
            ws_in = l_ws.dma(wo_sb, t["wo"])
            pair_in = load_pair(0)
            ready = layer_norm(x_in)
            xnT_ready = transpose_xn(ready)
            state = {"v": [None, None], "neg": [None, None], "neg_read": (), "sum_read": [free["ws"], free["ws"]],
                     "raw_read": (), "out": None, "proj": None}
            for v in range(2):
                vfree[v] = tuple(free["values"])
            for _ in wide_prep(0, pair_in, xnT_ready, ws_in, state):
                pass
            k_ctx = scratch(f"ctx_parts{b}", D, CTX)
            for p in range(PAIRS):
                if p + 1 < PAIRS:
                    pair_in = load_pair(p + 1)
                    nxt = wide_prep(p + 1, pair_in, xnT_ready, ws_in, state)
                else:
                    context_matmuls[0] = state["proj"]
                    nxt = context_parts(b, k_ctx)
                together(wide_main(p, state), nxt, 2.3)
            last_values = vfree[1]
            for i, q, psum, done in project_out(wo_sb, PAIRS, (state["out"],)):
                last = ve.step(stt(x_sb[:, q, :], psum, gates[:, 0:1], x_sb[:, q, :], ALU.mult, ALU.add), done)
                work.freed[i] = (last,)
            free["ws"], free["outT"] = [done], [done]
            free["values"] = list(last_values)
            if b + 1 < BATCHES:
                ctxT_in = load_ctxT(b + 1)

            sp.wait(*free["out_w"])
            out_w_in = l_wp.dma(out_w[:, :, :], t["ow"])
            po.wait(*kfree[0], *kfree[1])
            key_ones = po.step(memset(kbuf[STACK:STACK + 3, :, :, :], 1.0))
            v_ones = ones_in_values(QT, KV_HEADS)
            ready = layer_norm(last)
            xnT_ready = transpose_xn(ready, state["proj"])
            q_dram, k_dram = scratch(f"q2_{b}", D, S), scratch(f"k2_{b}", KV_HEADS * SLIM, S)
            slots = part_slots()
            for m in range(3):
                n = P if m < 2 else 64
                i, bank = work.next()
                pe.wait(xnT_ready, *work.freed[i])
                for f in range(FT):
                    done = pe.mark(mm(bank[0:n, :], gqa_w[:, f, m * P:m * P + n], xnT[:, f, :],
                                      start=f == 0, stop=f == FT - 1))
                biased = ve.step(ts(raw[0:n, :], bank[0:n, :], qk_bias[0:n, m:m + 1], ALU.add), done, *state["raw_read"])
                work.freed[i] = (biased,)
                _, last = split(raw[0:n, :], [s_[0:n, :] for s_ in slots[m]], (n, S), biased, *free["kparts"])
                state["raw_read"] = (last,)
                sp.wait(last)
                for part in range(3):
                    dst = q_dram[part, m * P:m * P + n, :] if m < 2 else k_dram[part, :, :]
                    l_scratch.dma(dst, slots[m][part][0:n, :])
            qk_in = l_scratch.all()
            free["kparts"] = [qk_in]
            i, bank = work.next()
            pe.wait(xnT_ready, *work.freed[i])
            kv = KV_HEADS * SLIM
            for k in range(QT):
                for f in range(FT):
                    done = pe.mark(mm(bank[:, k * kv:(k + 1) * kv], xnT[:, f, k * P:(k + 1) * P],
                                      gqa_w[:, f, D + kv:D + 2 * kv], start=f == 0, stop=f == FT - 1))
            last = ve.step(tt(v_slim[:, 0:QT, 0:KV_HEADS, 0:SLIM],
                              bank[:, 0:QT * kv].rearrange("p (k h d) -> p k h d", k=QT, h=KV_HEADS),
                              row_vb.rearrange("p (h d) -> p h d", h=KV_HEADS).unsqueeze(1)
                              .to_broadcast([P, QT, KV_HEADS, SLIM]), ALU.add), done, *free["values"])
            work.freed[i] = (last,)
            pe.wait(key_ones)
            att = slim_attention(True, S, SLIM ** -0.5, False, k_dram, qk_in, q_dram, qk_in, (last, v_ones))
            expert_free = [tuple(free["ws"]), tuple(free["ws"])]

            def load_expert(e):
                s = e % 2
                sp.wait(*expert_free[s])
                l_exp[s].dma(w1_sb[:, s, :, :], t["w1"][e])
                return l_exp[s].dma(w2_sb[:, s, :, :], t["w2"][e])

            expert_in = [load_expert(0), load_expert(1)]
            for i, q, psum, done in project_out(out_w, GROUP, (att, out_w_in)):
                ve.step(tt(xn[:, q, :], xn[:, q, :], row_ob, ALU.add), xnT_ready)
                last = ve.step(tt(xn[:, q, :], psum, xn[:, q, :], ALU.add), done)
                work.freed[i] = (last,)
            free["outT"], free["out_w"] = [done], [done]
            rms(xn, RMS_EPS)
            for q in range(QT):
                last = ve.step(stt(xn[:, q, :], xn[:, q, :], rstd[:, q:q + 1], row_n1, ALU.mult, ALU.mult))
            xnT_ready = transpose_xn(last, done)
            i, logits, done = gate_logits(gate_w0, xnT_ready)
            sig = sc.step(act(prob[:, :, :], logits, ACT.Exp, -1.0), done)
            work.freed[i] = (sig,)
            ve.step(ts(prob[:, :, :], prob[:, :, :], 1.0, ALU.add), sig)
            last = ve.step(lambda e: e.reciprocal(prob[:, :, :], prob[:, :, :]))
            top_two(last)
            picked = pick2
            ve.step(tt(best1[:, :], best1[:, :], best2[:, :], ALU.add))
            ve.step(ts(best1[:, :], best1[:, :], 1e-6, ALU.add))
            ve.step(lambda e: e.reciprocal(best1[:, :], best1[:, :]))
            ve.step(tt(picked[:, :, :], pick1[:, :, :], pick2[:, :, :], ALU.add))
            ve.step(copy(chosen_b[:, :, :], picked[:, :, :]))
            ve.step(tt(combine[:, :, :], prob[:, :, :], picked[:, :, :], ALU.mult))
            ve.step(tt(combine[:, :, :], combine[:, :, :],
                       best1[:, :].unsqueeze(2).to_broadcast([P, QT, EXPERTS]), ALU.mult))
            i, bank = work.next()
            pe.wait(*work.freed[i])
            before_read = done
            for q in range(QT):
                last = ve.step(copy(before_b[:, :], before_f[:, :]), before_read)
                out_ = bank[:, q * EXPERTS:(q + 1) * EXPERTS]
                pe.wait(last)
                pe.do(mm(out_, earlier_b[:, :], chosen_b[:, q, :], stop=False))
                before_read = done = pe.mark(mm(out_, ones_b[:, :], before_b[:, :], start=False))
                ve.step(tt(before_f[:, :], before_f[:, :], picked[:, q, :], ALU.add))
            ranks = bank[:, 0:QT * EXPERTS].rearrange("p (q e) -> p q e", q=QT)
            last = ve.step(stt(combine[:, :, :], ranks, float(CAPACITY), combine[:, :, :], ALU.is_lt, ALU.mult), done)
            work.freed[i] = (last,)
            h_free = [tuple(free["outT"]), tuple(free["outT"])]

            def expert_up(e):
                s = e % 2
                for m in range(FFN // P):
                    i, bank = work.next()
                    pe.wait(expert_in[s], xnT_ready, *work.freed[i])
                    for f in range(FT):
                        done = pe.mark(mm(bank, w1_sb[:, s, f, m * P:(m + 1) * P], xnT[:, f, :],
                                          start=f == 0, stop=f == FT - 1))
                    last = sc.step(act(hidden[:, s, m, :], bank, ACT.Gelu), done, *h_free[s])
                    work.freed[i] = (last,)
                return last

            def expert_down(e, h_ready):
                s = e % 2
                for q in range(0, QT, 2):
                    i, bank = work.next()
                    pe.wait(h_ready, *work.freed[i])
                    for j in range(2):
                        for m in range(FFN // P):
                            op = mm(bank[:, j * D:(j + 1) * D], hidden[:, s, m, (q + j) * P:(q + j + 1) * P],
                                    w2_sb[:, s, m, :], start=m == 0, stop=m == FFN // P - 1)
                            done = pe.mark(op) if m == FFN // P - 1 else pe.do(op)
                    for j in range(2):
                        last = ve.step(stt(xn[:, q + j, :], bank[:, j * D:(j + 1) * D],
                                           combine[:, q + j, e:e + 1], xn[:, q + j, :], ALU.mult, ALU.add), done)
                    work.freed[i] = (last,)
                h_free[s] = expert_free[s] = (done,)
                return done, last

            h_ready = expert_up(0)
            for e in range(EXPERTS):
                nxt = expert_up(e + 1) if e + 1 < EXPERTS else None
                done, last = expert_down(e, h_ready)
                h_ready = nxt
                if e + 2 < EXPERTS:
                    expert_in[e % 2] = load_expert(e + 2)
            free["outT"], free["ws"] = [done], [done]
            rms(xn, RMS_EPS)
            for q in range(QT):
                ve.step(stt(xn[:, q, :], xn[:, q, :], rstd[:, q:q + 1], row_n2, ALU.mult, ALU.mult))
                last = ve.step(stt(x_sb[:, q, :], xn[:, q, :], gates[:, 2:3], x_sb[:, q, :], ALU.mult, ALU.add))

            if BLOCKS >= 3:
                sp.wait(masks_stored, *free["ws"])
                a, z = key_rows(maskT_dram)
                l_ws.dma(maskT_sb[0:CTX_TILE, 0:full, :], a)
                l_ws.dma(maskT_sb[0:tail, full, :], z)
                masks_in = l_ws.dma(maskQ_sb, maskQ_dram.rearrange("(q p) n -> p q n", p=P))
                sp.wait(*free["out_w"])
                out_w_in = l_wp.dma(out_w[:, :, :], t["w_out"])
                cr = ctx_rows.rearrange("p (k n) -> p k n", k=NKT)
                for i in range(4):
                    sp.wait(*expo.freed[i])
                a, z = key_rows(t["ctx"][b])
                l_ctxr.dma(cr[0:CTX_TILE, 0:full, :], a)
                rows_in = l_ctxr.dma(cr[0:tail, full, :], z)
                v_ones = ones_in_values(NKT, HEADS)
                ready = layer_norm(last)
                xnT_ready = transpose_xn(ready, done)
                for kn, ks in ((CTX_TILE, slice(0, full)), (tail, slice(full, NKT))):
                    last = ve.step(copy(v_slim[0:kn, ks, :, 0:SLIM],
                                        cr[0:kn, ks, :].rearrange("p k (h d) -> p k h d", h=HEADS)),
                                   rows_in, *free["values"])
                for i in range(4):
                    expo.freed[i] = (last,)
                values_ready = (last, v_ones)
                q_dram = scratch(f"q3_{b}", D, S)
                slots = part_slots()
                for m in range(FT):
                    _, last = split(xnT[:, m, :], slots[m], (P, S), xnT_ready, *free["kparts"])
                    sp.wait(last)
                    for part in range(3):
                        l_scratch.dma(q_dram[part, m * P:(m + 1) * P, :], slots[m][part])
                free["kparts"] = [l_scratch.all()]
                att = slim_attention(False, CTX, D ** -0.5, True, k_ctx, l_kctx.all(), q_dram, l_scratch.all(),
                                     values_ready, (masks_in,))
                free["ws"] = [free["values"][0], (ve.sem, ve.marks)]
                ws_free = free["ws"]
                for i, q, psum, done in project_out(out_w, GROUP, (att, out_w_in)):
                    ve.step(tt(xn[:, q, :], psum, row_bo, ALU.add), done)
                    last = ve.step(stt(x_sb[:, q, :], xn[:, q, :], gates[:, 1:2], x_sb[:, q, :], ALU.mult, ALU.add))
                    work.freed[i] = (last,)
                free["outT"], free["out_w"] = [done], [done]

            if BLOCKS >= 4:
                sp.wait(*free["ws"])
                l_ws.dma(wqkv_sb, t["wqkv"])
                ws_in = l_ws.dma(we_sb, t["we"])
                sp.wait(*free["out_w"])
                out_w_in = l_wp.dma(out_w[:, :, :], t["scatter"])
                v_ones = ones_in_values(QT, HEADS)
                ready = layer_norm(last)
                xnT_ready = transpose_xn(ready, (sc.sem, sc.marks), (ve.sem, ve.marks))
                q_dram, k_dram = scratch(f"q4_{b}", D, S), scratch(f"k4_{b}", D, S)
                slots = part_slots()
                for m in range(4):
                    i, bank = work.next()
                    pe.wait(xnT_ready, ws_in, *work.freed[i])
                    for f in range(FT):
                        done = pe.mark(mm(bank, wqkv_sb[:, f, m * P:(m + 1) * P], xnT[:, f, :],
                                          start=f == 0, stop=f == FT - 1))
                    biased = ve.step(ts(raw[:, :], bank, qk_bias[:, 3 + m:4 + m], ALU.add), done)
                    work.freed[i] = (biased,)
                    _, last = split(raw[:, :], slots[m], (P, S), biased, *free["kparts"], *free["qparts"])
                    sp.wait(last)
                    for part in range(3):
                        dst = q_dram if m < 2 else k_dram
                        l_scratch.dma(dst[part, (m % 2) * P:(m % 2 + 1) * P, :], slots[m][part])
                qk_in = l_scratch.all()
                free["kparts"] = free["qparts"] = [qk_in]
                for k in range(0, QT, 2):
                    i, bank = work.next()
                    pe.wait(*work.freed[i])
                    for j in range(2):
                        for f in range(FT):
                            done = pe.mark(mm(bank[:, j * D:(j + 1) * D], xnT[:, f, (k + j) * P:(k + j + 1) * P],
                                              wqkv_sb[:, f, 2 * D:3 * D], start=f == 0, stop=f == FT - 1))
                    last = ve.step(tt(v_slim[:, k:k + 2, :, 0:SLIM],
                                      bank.rearrange("p (k h d) -> p k h d", k=2, h=HEADS),
                                      row_v1.rearrange("p (h d) -> p h d", h=HEADS).unsqueeze(1)
                                      .to_broadcast([P, 2, HEADS, SLIM]), ALU.add), done, *free["values"])
                    work.freed[i] = (last,)
                values_ready = (last, v_ones)
                i, logits, done = gate_logits(gate_w1, xnT_ready)
                ve.step(tt(prob[:, :, :], logits, row_bg.unsqueeze(1).to_broadcast([P, QT, EXPERTS]), ALU.add), done)
                work.freed[i] = ((ve.sem, ve.marks),)
                ve.step(rmax(best1[:, :], prob[:, :, :]))
                last = ve.step(tt(prob[:, :, :], prob[:, :, :],
                                  best1[:, :].unsqueeze(2).to_broadcast([P, QT, EXPERTS]), ALU.subtract))
                last = sc.step(act(prob[:, :, :], prob[:, :, :], ACT.Exp), last)
                ve.step(lambda e: e.reduce_sum(best1[:, :], prob[:, :, :], AX.X), last)
                ve.step(lambda e: e.reciprocal(best1[:, :], best1[:, :]))
                last = ve.step(tt(prob[:, :, :], prob[:, :, :],
                                  best1[:, :].unsqueeze(2).to_broadcast([P, QT, EXPERTS]), ALU.mult))
                top_two(last)
                ve.step(tt(combine[:, :, :], pick1[:, :, :], pick2[:, :, :], ALU.add))
                comb = ve.step(tt(combine[:, :, :], combine[:, :, :], prob[:, :, :], ALU.mult))
                i, bank = work.next()
                pe.wait(comb, *work.freed[i])
                for q in range(QT):
                    done = pe.mark(transpose(bank[0:EXPERTS, q * P:(q + 1) * P], combine[:, q, :], ident))
                combT_ready = sc.step(acopy(combT[:, :], bank[0:EXPERTS, :]), done)
                work.freed[i] = (combT_ready,)
                for q in range(0, QT, 2):
                    i, bank = work.next()
                    pe.wait(combT_ready, *work.freed[i])
                    for j in range(2):
                        done = pe.mark(mm(bank[:, j * D:(j + 1) * D], combT[:, (q + j) * P:(q + j + 1) * P], b_exp[:, :]))
                    last = ve.step(copy(xn[:, q:q + 2, :], bank.rearrange("p (q n) -> p q n", q=2)), done, xnT_ready)
                    work.freed[i] = (last,)
                for e in range(EXPERTS):
                    for q in range(0, QT, 2):
                        i, bank = work.next()
                        pe.wait(*work.freed[i])
                        for j in range(2):
                            for f in range(FT):
                                done = pe.mark(mm(bank[:, j * D:(j + 1) * D], xnT[:, f, (q + j) * P:(q + j + 1) * P],
                                                  we_sb[:, e, f, :], start=f == 0, stop=f == FT - 1))
                        for j in range(2):
                            last = ve.step(stt(xn[:, q + j, :], bank[:, j * D:(j + 1) * D],
                                               combine[:, q + j, e:e + 1], xn[:, q + j, :], ALU.mult, ALU.add), done)
                        work.freed[i] = (last,)
                free["ws"] = [done]
                att = slim_attention(False, S, SLIM ** -0.5, False, k_dram, qk_in, q_dram, qk_in, values_ready)
                for i, q, psum, done in project_out(out_w, GROUP, (att, out_w_in)):
                    ve.step(tt(xn[:, q, :], psum, xn[:, q, :], ALU.add), done)
                    last = ve.step(stt(x_sb[:, q, :], xn[:, q, :], gates[:, 3:4], x_sb[:, q, :], ALU.mult, ALU.add))
                    work.freed[i] = (last,)
                free["outT"], free["out_w"] = [done], [done]

            sp.wait(last)
            stored = l_out.dma(out[b].rearrange("(q p) n -> p q n", p=P), x_sb[:, :, :])
            free["x"] = [stored]
            if b + 1 < BATCHES:
                x_in = load_x(b + 1)

        sp.wait(l_out.all(), l_scratch.all(), l_kctx.all())

        block = ctx.enter_context(nc.Block())

        @block.sync
        def _(eng):
            sp.run(eng)

        @block.tensor
        def _(eng):
            pe.run(eng)

        @block.scalar
        def _(eng):
            sc.run(eng)

        @block.vector
        def _(eng):
            ve.run(eng)

        @block.gpsimd
        def _(eng):
            po.run(eng)


BATCHES, BLOCKS = B, 4


def lay_out(inputs):
    def a(name):
        return np.asarray(inputs[name])

    def tiles(w):
        return np.ascontiguousarray(w.reshape(-1, P, w.shape[-1]).transpose(1, 0, 2))

    def padded(w):
        out = np.zeros((HEADS, PAD, w.shape[-1]), w.dtype)
        out[:, :SLIM] = w.reshape(HEADS, SLIM, -1)
        return tiles(out.reshape(HEADS * PAD, -1))

    consts = np.zeros((P, C_ALL), np.float32)
    consts[:, C_IDENT:C_IDENT + P] = np.eye(P)
    for h in range(2):
        consts[h:6:2, C_SELECT + h * P:C_SELECT + (h + 1) * P] = 1
    consts[:, C_TIE:C_EARLIER] = EXPERTS - np.arange(EXPERTS)
    consts[:, C_EARLIER:] = np.triu(np.ones((P, P)), 1)
    mask = a("mask_1x1xSxS2_ik0")[0, 0]
    pair = np.stack([a(n).reshape(FT, P, PAIRS, P) for n in ("L0_xattn_Wq", "L0_xattn_Wk")])
    arrays = {
        "x": a("x"), "ctx": a("ctx_1024"),
        "ctxT": np.ascontiguousarray(a("ctx_1024").transpose(0, 2, 1)),
        "maskQ": np.ascontiguousarray(mask), "maskT": np.ascontiguousarray(mask.T),
        "consts": consts,
        "w_pair": np.ascontiguousarray(pair.transpose(3, 2, 0, 1, 4)),
        "wv": tiles(a("L0_xattn_Wv")), "wo": tiles(a("L0_xattn_Wo")),
        "gqa_w": tiles(np.concatenate([a("L0_ffn_qw"), a("L0_ffn_kw"), a("L0_ffn_vw")], 1)),
        "ow": padded(a("L0_ffn_ow")), "w_out": padded(a("L1_xattn_w_out").T),
        "scatter": padded(np.eye(D, dtype=np.float32)),
        "gate0": tiles(a("L0_ffn_gate_w")), "gate1": tiles(a("L1_ffn_W_gate")),
        "w1": np.stack([tiles(w) for w in a("L0_ffn_w1")]),
        "w2": np.stack([tiles(w) for w in a("L0_ffn_w2")]),
        "wqkv": tiles(a("L1_ffn_W_qkv")),
        "we": np.ascontiguousarray(a("L1_ffn_W_experts").reshape(EXPERTS, FT, P, D).transpose(2, 0, 1, 3)),
    }
    qk = np.zeros((7, P), np.float32)
    qk[0:2], qk[2, 0:64] = a("L0_ffn_qb").reshape(2, P), a("L0_ffn_kb")
    qk[3:7] = a("L1_ffn_b_qkv")[0:2 * D].reshape(4, P)
    arrays["qk_bias"] = np.ascontiguousarray(qk.T)
    for n in ("g_xattn", "g_ffn", "L0_ffn_vb", "L0_ffn_ob", "L0_ffn_norm1_w",
              "L0_ffn_norm2_w", "L1_xattn_b_out", "L1_ffn_b_qkv", "L1_ffn_b_gate", "L1_ffn_b_experts"):
        arrays[n] = a(n)
    return arrays


def kernel(**inputs):
    import concourse.bacc as bacc
    from concourse.bass_utils import run_bass_kernel_spmd

    nc = bacc.Bacc("TRN2", target_bir_lowering=False, num_devices=1)
    arrays = {"in_" + n: v for n, v in lay_out(inputs).items()}
    t = {n[3:]: nc.dram_tensor(n, v.shape, mybir.dt.from_np(v.dtype), kind="ExternalInput").ap()
         for n, v in arrays.items()}
    out = nc.dram_tensor("out_x", (B, S, D), F32, kind="ExternalOutput").ap()
    flamingo(nc, t, out)
    r = run_bass_kernel_spmd(nc, [arrays], core_ids=[0])
    return r.results[0]["out_x"]
```

```python
import numpy as np
import concourse.bass as bass
from concourse import mybir
from contextlib import ExitStack
from itertools import chain

B, S, D = 4, 512, 256
CTX = 1601
HEADS = 16
WIDE = 64
SLIM = 16
KV_HEADS = 4
EXPERTS, FFN = 8, 512
CAPACITY = int(1.25 * B * S * 2 / EXPERTS)
P = 128
BANK = 512
QT = S // P
FT = D // P
LN_EPS, RMS_EPS = 1e-5, 1e-6
MASKED = -1e20
GROUP = 4
PAD = P // GROUP
PAIRS = HEADS // 2

CTX_TILE = 124
CTX_TILES = [(k, min(CTX_TILE, CTX - k)) for k in range(0, CTX, CTX_TILE)]
CTX_CHUNKS = [(0, 401), (401, 400), (801, 400), (1201, 400)]
SELF_TILES = [(k, P) for k in range(0, S, P)]
NKT = len(CTX_TILES)

TERMS = [(0, 0), (0, 1), (0, 2), (1, 0), (1, 1), (2, 0)]
STACK = len(TERMS) * SLIM

F32, BF16, I32 = mybir.dt.float32, mybir.dt.bfloat16, mybir.dt.int32
ALU, ACT, AX = mybir.AluOpType, mybir.ActivationFunctionType, mybir.AxisListType

C_IDENT, C_SELECT, C_TIE, C_EARLIER = 0, P, 3 * P, 3 * P + EXPERTS
C_ALL = 4 * P + EXPERTS


class Lane:

    def __init__(self, sem):
        self.sem, self.queue, self.marks, self.seen = sem, [], 0, {}

    def do(self, emit):
        self.queue.append(emit)

    def mark(self, emit):
        self.marks += 1
        self.queue.append(lambda e: emit(e).then_inc(self.sem, 1))
        return (self.sem, self.marks)

    def wait(self, *marks):
        for sem, value in marks:
            if self.seen.get(sem.name, 0) < value:
                self.seen[sem.name] = value
                self.queue.append(lambda e, s=sem, v=value: e.wait_ge(s, v))

    def step(self, emit, *marks):
        if self.marks:
            self.wait((self.sem, self.marks))
        self.wait(*marks)
        return self.mark(emit)

    def run(self, engine):
        for emit in self.queue:
            emit(engine)


class Landing:

    def __init__(self, lane, sem):
        self.lane, self.sem, self.count = lane, sem, 0

    def dma(self, out, in_):
        self.count += 16
        self.lane.do(lambda e: e.dma_start(out, in_).then_inc(self.sem, 16))
        return (self.sem, self.count)

    def all(self):
        return (self.sem, self.count)


class Ring:

    def __init__(self, views):
        self.views, self.freed, self.turn = views, [()] * len(views), 0

    def next(self):
        i = self.turn % len(self.views)
        self.turn += 1
        return i, self.views[i]


def mm(out, lhsT, rhs, start=True, stop=True):
    return lambda e: e.matmul(out, lhsT, rhs, start=start, stop=stop)


def transpose(out, in_, ident):
    return lambda e: e.transpose(out, in_, ident)


def copy(out, in_):
    return lambda e: e.tensor_copy(out, in_)


def acopy(out, in_):
    return lambda e: e.activation(out, in_, ACT.Copy)


def act(out, in_, func, scale=1.0):
    return lambda e: e.activation(out, in_, func, scale=scale)


def tt(out, a, b, op):
    return lambda e: e.tensor_tensor(out, a, b, op)


def ts(out, a, s1, op0, s2=None, op1=None):
    if op1 is None:
        return lambda e: e.tensor_scalar(out, a, s1, None, op0)
    return lambda e: e.tensor_scalar(out, a, s1, s2, op0, op1)


def stt(out, a, s, b, op0, op1):
    return lambda e: e.scalar_tensor_tensor(out=out, in0=a, scalar=s, in1=b, op0=op0, op1=op1)


def rmax(out, in_):
    return lambda e: e.reduce_max(out, in_, AX.X)


def turn(out, in_):
    return lambda e: e.transpose(out, in_)


def blocks(tile):
    return tile[:, :].rearrange("p (b r) -> p b r", r=32)


def memset(ap, value):
    return lambda e: e.memset(ap, value)


def beside(main, prep, ratio):
    debt = 0.0
    for step in main:
        yield step
        debt += ratio
        while debt >= 1:
            debt -= 1
            more = next(prep, None)
            if more is not None:
                yield more
    yield from prep


class Step:

    def __init__(self, pe=0.0, ve=0.0, sc=0.0, ring=None, late=None):
        self.pe, self.ve, self.sc, self.ring, self.late = pe, ve, sc, ring, late


class Pace:

    def __init__(self):
        self.pe = self.ve = self.sc = 0.0
        self.rings = {}

    def start(self, step, ready):
        at = max(self.pe, ready)
        if step.ring:
            held = self.rings.setdefault(id(step.ring), [0.0] * len(step.ring.views))
            at = max(at, held[0])
        return at

    def add(self, step, ready):
        at = self.start(step, ready)
        end = at + step.pe
        if step.pe:
            self.pe = end
        if step.sc:
            self.sc = max(self.sc, end + HOP) + step.sc
        if step.ve:
            self.ve = max(self.ve, end + HOP, self.sc + HOP if step.sc else 0) + step.ve
        last = max(end, self.ve if step.ve else 0, self.sc if step.sc else 0)
        if step.ring:
            held = self.rings[id(step.ring)]
            held.pop(0)
            held.append(last + HOP)
        return end if step.late is None else last + step.late


HOP = 0.2


def merge(chains, totals, pace):
    last, ready, done = {}, {}, {}
    for n in range(len(chains)):
        last[n], ready[n], done[n] = Step(), pace.pe, 0.0
    alive = list(range(len(chains)))
    while alive:
        at = {n: pace.start(last[n], ready[n]) for n in alive}
        first = min(at.values())
        n = min((n for n in alive if at[n] <= first + SLACK), key=lambda n: done[n] / totals[n])
        step = next(chains[n], None)
        if step is None:
            alive.remove(n)
            continue
        ready[n] = pace.add(step, ready[n])
        done[n] += max(step.pe, 0.1)
        last[n] = step
    return done


def flamingo(nc, t, out):
    ctx = ExitStack()
    with ctx:
        def sb(name, shape, dt=F32):
            return ctx.enter_context(nc.sbuf_tensor(name, shape, dt))

        def sem(name):
            return ctx.enter_context(nc.semaphore(name))

        x_bufs = [sb(f"x{i}", [P, QT, D]) for i in range(2)]
        xnT_a = sb("xnT_a", [P, FT, S])
        xn_b = sb("xn_b", [P, QT, D])
        xnT_b = sb("xnT_b", [P, FT, S])
        ctxT = sb("ctxT", [P, FT, CTX])
        vbuf = sb("vbuf", [P, 2, QT * HEADS * PAD])
        kbuf = sb("kbuf", [P, 2, GROUP, CTX], BF16)
        qbuf = sb("qbuf", [P, 2, 6, S], BF16)
        exps_a = sb("exps_a", [P, 6, S])
        exps_b = sb("exps_b", [P, 8, S])
        sums = sb("sums", [P, 2, S])
        ws = sb("ws", [P, NKT * 512])
        outT_a = sb("outT_a", [P, S])
        outT_b = sb("outT_b", [P, GROUP, S])
        kparts_t = sb("kparts", [P, 3 * CTX + 1], BF16)
        kparts = kparts_t[:, 0:3 * CTX].rearrange("p (a n) -> p a n", a=3)
        qparts = sb("qparts", [P, 3, S], BF16)
        rest = sb("rest", [P, S])
        raw_a = sb("raw_a", [P, S])
        raw_b = sb("raw_b", [P, S])
        inverse = sb("inverse", [P, S // 32])
        w_pair = sb("w_pair", [P, 2, 4, D])
        ident_f = sb("ident_f", [P, C_ALL])
        ident_b = sb("ident_b", [P, P], BF16)
        select_b = sb("select_b", [P, 2, P], BF16)
        earlier_b = sb("earlier_b", [P, P], BF16)
        ones_b = sb("ones_b", [P, P], BF16)
        ones_f = sb("ones_f", [P, WIDE])
        max_a = sb("max_a", [P, 2, QT, 4])
        max_b = sb("max_b", [P, GROUP, QT, 4])
        neg_max = sb("neg_max", [P, GROUP, QT])
        neg_rest = sb("neg_rest", [P, GROUP, QT])
        max_junk = sb("max_junk", [P, 401], BF16)
        neg_cols = sb("neg_cols", [P, 2, QT, P], BF16)
        neg_rows = sb("neg_rows", [P, 2, S], BF16)
        stats = sb("stats", [P, QT, 6])
        moments = sb("moments", [P, QT, 2])
        rstd = sb("rstd", [P, QT])
        gates = sb("gates", [P, 4])
        prob = sb("prob", [P, QT, EXPERTS])
        prob2 = sb("prob2", [P, QT, EXPERTS])
        hit = sb("hit", [P, QT, EXPERTS])
        pick1 = sb("pick1", [P, QT, EXPERTS])
        pick2 = sb("pick2", [P, QT, EXPERTS])
        best1 = sb("best1", [P, QT])
        best2 = sb("best2", [P, QT])
        combine = sb("combine", [P, QT, EXPERTS])
        chosen_b = sb("chosen_b", [P, QT, EXPERTS], BF16)
        before_b = sb("before_b", [P, EXPERTS], BF16)
        before_f = sb("before_f", [P, EXPERTS])
        combT = raw_b[0:EXPERTS, :]
        gqa_w = sb("gqa_w", [P, FT, D + 2 * KV_HEADS * SLIM])
        out_w = sb("out_w", [P, GROUP, D])
        gate_w0 = sb("gate_w0", [P, FT, EXPERTS])
        gate_w1 = sb("gate_w1", [P, FT, EXPERTS])
        qk_bias = sb("qk_bias", [P, 7])
        rows = sb("rows", [P, 4 * D + KV_HEADS * SLIM + D + EXPERTS])
        b_exp = sb("b_exp", [EXPERTS, D])

        row_ob, row_n1, row_n2, row_bo = (rows[:, i * D:(i + 1) * D] for i in range(4))
        row_vb = rows[:, 4 * D:4 * D + KV_HEADS * SLIM]
        row_v1 = rows[:, 4 * D + KV_HEADS * SLIM:5 * D + KV_HEADS * SLIM]
        row_bg = rows[:, 5 * D + KV_HEADS * SLIM:]

        ident = ident_f[:, C_IDENT:C_IDENT + P]
        tie = ident_f[:, C_TIE:C_TIE + EXPERTS]

        work_t = ctx.enter_context(nc.psum_tensor("work", [P, WORK, BANK], F32))
        score_t = ctx.enter_context(nc.psum_tensor("score", [P, SCORE, BANK], F32))
        pv_t = ctx.enter_context(nc.psum_tensor("pv", [P, 2, BANK], F32))
        work = Ring([work_t[:, i, :] for i in range(WORK)])
        score = Ring([score_t[:, i, :] for i in range(SCORE)])
        pv_a, pv_b = pv_t[:, 0, :], pv_t[:, 1, :]
        expo_a = Ring([exps_a[:, i, :] for i in range(6)])
        expo_b = Ring([exps_b[:, i, :] for i in range(8)])

        xn_a = kparts_t[:, :].bitcast(F32)[:, 0:QT * D].rearrange("p (q n) -> p q n", q=QT)
        w1_sb = ws[:, 0:2048].rearrange("p (s f n) -> p s f n", s=2, f=FT)
        w2_sb = ws[:, 2048:4096].rearrange("p (s f n) -> p s f n", s=2, f=FFN // P)
        hidden = exps_b[:, :, :].rearrange("p (s f) n -> p s f n", s=2)
        masks = ws[:, :].bitcast(BF16)
        maskT_sb = masks[:, 0:NKT * S].rearrange("p (k n) -> p k n", k=NKT)
        maskQ_sb = masks[:, NKT * S:NKT * S + QT * CTX].rearrange("p (q n) -> p q n", q=QT)
        we_sb = ws[:, 0:4096].rearrange("p (e f n) -> p e f n", e=EXPERTS, f=FT)
        wqkv_sb = ws[:, 4096:4096 + FT * 3 * D].rearrange("p (f n) -> p f n", f=FT)
        v_wide = [vbuf[:, s, 0:NKT * P].rearrange("p (k n) -> p k n", k=NKT) for s in range(2)]
        v_group = [vbuf[:, s, 0:NKT * P].rearrange("p (k h c) -> p k h c", k=NKT, h=GROUP) for s in range(2)]
        v_self = vbuf[:, 1, :].rearrange("p (k h c) -> p k h c", k=QT, h=HEADS)

        pe, sc, ve, po, sp = (Lane(sem("s_" + n)) for n in ("pe", "sc", "ve", "po", "sp"))

        def landing(name):
            return Landing(sp, sem("d_" + name))

        l_const, l_ctxT, l_ws, l_wp = (landing(n) for n in ("const", "ctxT", "ws", "wp"))
        l_x = [landing(f"x{i}") for i in range(2)]
        l_pair = [landing(f"pair{i}") for i in range(2)]
        l_kst = [landing(f"kst{i}") for i in range(2)]
        l_qst = [landing(f"qst{i}") for i in range(2)]
        l_neg = [landing(f"neg{i}") for i in range(2)]
        l_v = [landing(f"v{i}") for i in range(2)]
        l_up = [landing(f"up{i}") for i in range(2)]
        l_down = [landing(f"down{i}") for i in range(2)]
        l_scratch, l_kctx, l_mask, l_stored = (landing(n) for n in ("scratch", "kctx", "mask", "stored"))
        l_out = [landing(f"out{i}") for i in range(2)]

        free = {n: [] for n in ("ws", "outT_a", "outT_b", "kparts", "qparts", "out_w", "ctxT",
                                "raw_a", "raw_b", "pv_a", "pv_b", "sum0", "sum1",
                                "xnT_a", "xnT_b", "x0", "x1", "chosen")}
        kfree, qfree, vfree, negfree, colfree, pairfree = ([(), ()] for _ in range(6))

        def newest(lane):
            return (lane.sem, lane.marks)

        def load_x(b):
            sp.wait(*free[f"x{b % 2}"])
            return l_x[b % 2].dma(x_bufs[b % 2][:, :, :], t["x"][b].rearrange("(q p) n -> p q n", p=P))

        def load_ctxT(b):
            sp.wait(*free["ctxT"])
            return l_ctxT.dma(ctxT[:, :, :], t["ctxT"][b].rearrange("(f p) n -> p f n", p=P))

        def load_pair(p):
            sp.wait(*pairfree[p % 2])
            return l_pair[p % 2].dma(w_pair[:, p % 2, :, :], t["w_pair"][p])

        l_const.dma(ident_f[:, :], t["consts"])
        l_const.dma(gates[:, 0:2], t["g_xattn"].partition_broadcast(P))
        l_const.dma(gates[:, 2:4], t["g_ffn"].partition_broadcast(P))
        consts_in = l_const.all()
        x_in, ctxT_in, first_pair_in = load_x(0), load_ctxT(0), load_pair(0)

        po.mark(memset(ones_f[:, :], 1.0))
        po.mark(memset(ones_b[:, :], 1.0))
        po.mark(memset(before_f[:, :], 0.0))
        pool_ready = po.mark(memset(neg_cols[:, :, :, :], 0.0))
        gates_ready = sc.step(act(gates[:, :], gates[:, :], ACT.Tanh), consts_in)
        ve.wait(consts_in, pool_ready, gates_ready)
        ve.step(copy(ident_b[:, :], ident))
        ve.step(copy(select_b[:, :, :], ident_f[:, C_SELECT:C_TIE].rearrange("p (h n) -> p h n", h=2)))
        consts_ready = ve.step(copy(earlier_b[:, :], ident_f[:, C_EARLIER:C_ALL]))
        pe.wait(consts_ready)
        po.wait(consts_ready)

        l_small = landing("small")
        l_small.dma(gqa_w[:, :, :], t["gqa_w"])
        l_small.dma(gate_w0[:, :, :], t["gate0"])
        l_small.dma(gate_w1[:, :, :], t["gate1"])
        l_small.dma(qk_bias[:, :], t["qk_bias"])
        for row, src in ((row_ob, t["L0_ffn_ob"]), (row_n1, t["L0_ffn_norm1_w"]),
                         (row_n2, t["L0_ffn_norm2_w"]), (row_bo, t["L1_xattn_b_out"]),
                         (row_vb, t["L0_ffn_vb"]), (row_v1, t["L1_ffn_b_qkv"][2 * D:3 * D]),
                         (row_bg, t["L1_ffn_b_gate"])):
            l_small.dma(row, src.partition_broadcast(P))
        small_in = l_small.dma(b_exp[:, :], t["L1_ffn_b_experts"])

        maskT_dram = nc.dram_tensor("maskT_add", [NKT * CTX_TILE, S], BF16, kind="Internal").ap()
        maskQ_dram = nc.dram_tensor("maskQ_add", [S, CTX], BF16, kind="Internal").ap()
        full = NKT - 1
        tail = CTX_TILES[-1][1]

        def key_rows(ap):
            return (ap[0:full * CTX_TILE].rearrange("(k p) n -> p k n", p=CTX_TILE),
                    ap[full * CTX_TILE:CTX])

        def make_masks():
            ints = exps_b[:, :, :].bitcast(I32)
            landed = ()
            for k in range(0, full, 6):
                sp.wait(*landed)
                a, _ = key_rows(t["maskT"])
                here = l_mask.dma(ints[0:CTX_TILE, 0:6, :], a[:, k:k + 6, :])
                landed = (ve.step(ts(maskT_sb[0:CTX_TILE, k:k + 6, :], ints[0:CTX_TILE, 0:6, :], 0.0,
                                     ALU.is_equal, MASKED, ALU.mult), here),)
                yield Step(ve=4, late=4)
            sp.wait(*landed)
            here = l_mask.dma(ints[0:tail, 0, :], key_rows(t["maskT"])[1])
            landed = (ve.step(ts(maskT_sb[0:tail, full, :], ints[0:tail, 0, :], 0.0, ALU.is_equal,
                                 MASKED, ALU.mult), here),)
            sp.wait(*landed)
            a, z = key_rows(maskT_dram)
            l_stored.dma(a, maskT_sb[0:CTX_TILE, 0:full, :])
            l_stored.dma(z, maskT_sb[0:tail, full, :])
            yield Step()
            flat = ints.rearrange("p a n -> p (a n)")
            for q in range(0, QT, 2):
                sp.wait(*landed)
                view = flat[:, 0:2 * CTX].rearrange("p (q n) -> p q n", q=2)
                here = l_mask.dma(view, t["maskQ"][q * P:(q + 2) * P].rearrange("(q p) n -> p q n", p=P))
                landed = (ve.step(ts(maskQ_sb[:, q:q + 2, :], view, 0.0, ALU.is_equal, MASKED, ALU.mult), here),)
                yield Step(ve=4, late=4)
            sp.wait(*landed)
            masks_stored[0] = l_stored.dma(maskQ_dram.rearrange("(q p) n -> p q n", p=P), maskQ_sb)
            free["ws"] = [masks_stored[0]]
            for i in range(8):
                expo_b.freed[i] = landed

        masks_stored = [None]

        def inverse_root(eps):
            ve.step(ts(rstd[:, :], rstd[:, :], eps, ALU.add))
            last = ve.step(lambda e: e.reciprocal(rstd[:, :], rstd[:, :]))
            root = sc.step(act(rstd[:, :], rstd[:, :], ACT.Sqrt), last)
            ve.wait(root)
            return root

        def rms(src, eps):
            for q in range(QT):
                ve.step(lambda e, q=q: e.tensor_tensor_reduce(
                    out=rest[:, 0:D], in0=src[:, q, :], in1=src[:, q, :], scale=1.0, scalar=0.0,
                    op0=ALU.mult, op1=ALU.add, accum_out=rstd[:, q:q + 1]))
            ve.step(ts(rstd[:, :], rstd[:, :], 1.0 / D, ALU.mult))
            return inverse_root(eps)

        def layer_norm(x_sb, xn, *after):
            for q in range(QT):
                ve.step(lambda e, q=q: e.bn_stats(stats[:, q, :], x_sb[:, q, :]), *after)
                ve.step(lambda e, q=q: e.bn_aggr(moments[:, q, :], stats[:, q, :]))
            ve.step(copy(rstd[:, :], moments[:, :, 1]))
            inverse_root(LN_EPS)
            for q in range(QT):
                last = ve.step(ts(xn[:, q, :], x_sb[:, q, :], moments[:, q, 0:1], ALU.subtract,
                                  rstd[:, q:q + 1], ALU.mult))
            return last

        def transpose_xn(xn, xnT, ready, *readers):
            for f in range(FT):
                i, bank = work.next()
                pe.wait(ready, *work.freed[i])
                for q in range(QT):
                    done = pe.mark(transpose(bank[:, q * P:(q + 1) * P],
                                             xn[:, q, f * P:(f + 1) * P], ident))
                last = sc.step(acopy(xnT[:, f, :], bank), done, *readers)
                work.freed[i] = (last,)
            return done, last

        def split(src, parts, n, *after):
            high = sc.step(acopy(parts[0], src), *after)
            read = ve.step(tt(rest[0:n[0], 0:n[1]], src, parts[0], ALU.subtract), high, *after)
            ve.step(copy(parts[1], rest[0:n[0], 0:n[1]]))
            last = ve.step(tt(parts[2], rest[0:n[0], 0:n[1]], parts[1], ALU.subtract))
            return read, last

        def negate_maximum(s, chunked, heads, chunks):
            if chunks > 1:
                ve.step(rmax(neg_max[:, 0:heads, :], chunked[:, 0:heads, :, 0:chunks]), *colfree[s])
                src = neg_max[:, 0:heads, :]
            else:
                src = chunked[:, 0:heads, :, 0]
                ve.wait(*colfree[s])
            ve.step(ts(neg_max[:, 0:heads, :], src, -1.0, ALU.mult))
            src = neg_max[:, 0:heads, :]
            for i in range(3):
                part = neg_cols[:, s, :, i * heads:i * heads + heads].rearrange("p q h -> p h q")
                last = ve.step(copy(part, src))
                if i < 2:
                    ve.step(tt(neg_rest[:, 0:heads, :], src, part, ALU.subtract))
                    src = neg_rest[:, 0:heads, :]
            return last

        def rows_of_maximum(s, ready):
            i, bank = work.next()
            pe.wait(ready, *work.freed[i])
            for q in range(QT):
                done = pe.mark(mm(bank[:, q * P:(q + 1) * P], neg_cols[:, s, q, :], ident_b[:, :]))
            last = sc.step(acopy(neg_rows[:, s, :], bank), done, *negfree[s])
            work.freed[i] = (last,)
            colfree[s] = (done,)
            return last

        def project_out(lhs, weights, tiles, ready):
            for q in range(0, QT, 2):
                i, bank = work.next()
                pe.wait(*ready, *work.freed[i])
                for j in range(2):
                    for g in range(tiles):
                        op = mm(bank[:, j * D:(j + 1) * D],
                                lhs(g)[:, (q + j) * P:(q + j + 1) * P], weights(g),
                                start=g == 0, stop=g == tiles - 1)
                        done = pe.mark(op) if g == tiles - 1 else pe.do(op)
                for j in range(2):
                    yield i, q + j, bank[:, j * D:(j + 1) * D], done

        def wide_project(p, pair_in, now):
            w = w_pair[:, p % 2, :, :].rearrange("p a (f n) -> p a f n", f=FT)
            for c0, cn in CTX_CHUNKS:
                i, bank = work.next()
                pe.wait(pair_in, now["ctxT"], *work.freed[i])
                for f in range(FT):
                    done = pe.mark(mm(bank[:, 0:cn], w[:, 1, f, :], ctxT[:, f, c0:c0 + cn],
                                      start=f == 0, stop=f == FT - 1))
                read, last = split(bank[:, 0:cn], [kparts[:, n, c0:c0 + cn] for n in range(3)],
                                   (P, cn), done, *free["kparts"])
                work.freed[i] = (read,)
                yield Step(pe=1.34, ve=1.7, sc=0.45, ring=work)
            now["k"] = last
            i, bank = work.next()
            pe.wait(now["xnT"], *work.freed[i])
            for f in range(FT):
                done = pe.mark(mm(bank, w[:, 0, f, :], xnT_a[:, f, :], start=f == 0, stop=f == FT - 1))
            read, last = split(bank, [qparts[:, n, :] for n in range(3)], (P, S), done, *free["qparts"])
            work.freed[i] = (read,)
            now["q"] = last
            free["xnT_a"] = [done]
            yield Step(pe=1.72, ve=1.9, sc=0.5, ring=work)

        def wide_stack(p, s, now):
            sp.wait(now["k"], *kfree[s])
            for h in range(2):
                own, other = slice(64 * h, 64 * h + 64), slice(64 - 64 * h, 128 - 64 * h)
                for kind in range(2):
                    l_kst[s].dma(kbuf[own, s, 2 * h + kind, :], kparts[own, 0, :])
                l_kst[s].dma(kbuf[other, s, 2 * h:2 * h + 2, :], kparts[own, 1:3, :])
            k_in = l_kst[s].all()
            free["kparts"] = [k_in]
            sp.wait(now["q"], *qfree[s])
            for h in range(2):
                own, other = slice(64 * h, 64 * h + 64), slice(64 - 64 * h, 128 - 64 * h)
                l_qst[s].dma(qbuf[own, s, 3 * h:3 * h + 3, :], qparts[own, :, :])
                l_qst[s].dma(qbuf[other, s, 3 * h:3 * h + 2, :], qparts[own, 0:2, :])
                l_qst[s].dma(qbuf[other, s, 3 * h + 2, :], qparts[own, 0, :])
            q_in = l_qst[s].all()
            free["qparts"] = [q_in]
            w = w_pair[:, p % 2, :, :].rearrange("p a (f n) -> p a f n", f=FT)
            for k in range(0, NKT, 4):
                some = CTX_TILES[k:k + 4]
                i, bank = work.next()
                pe.wait(*work.freed[i])
                for j, (k0, kn) in enumerate(some):
                    for f in range(FT):
                        op = mm(bank[0:kn, j * P:(j + 1) * P], ctxT[:, f, k0:k0 + kn], w[:, 2, f, :],
                                start=f == 0, stop=f == FT - 1)
                        done = pe.mark(op) if f == FT - 1 else pe.do(op)
                kn, n = some[0][1], len(some)
                last = sc.step(acopy(v_wide[s][0:kn, k:k + n, :],
                                     bank[0:kn, 0:n * P].rearrange("p (j n) -> p j n", j=n)), done, *vfree[s])
                work.freed[i] = (last,)
                yield Step(pe=1.72, sc=0.5, ring=work)
            now["v", s] = last
            free["ctxT"] = [done]
            pe.wait(k_in, q_in)
            for h in range(2):
                for q in range(QT):
                    for c, (c0, cn) in enumerate(CTX_CHUNKS):
                        i, bank = work.next()
                        pe.wait(*work.freed[i])
                        for kind in range(2):
                            op = mm(bank[:, 0:cn], qbuf[:, s, 3 * h + kind, q * P:(q + 1) * P],
                                    kbuf[:, s, 2 * h, c0:c0 + cn], start=kind == 0, stop=kind == 1)
                            done = pe.mark(op) if kind else pe.do(op)
                        ve.wait(done)
                        work.freed[i] = (ve.mark(rmax(max_a[:, h, q, c:c + 1], bank[:, 0:cn])),)
                        yield Step(pe=0.36, ve=0.5, ring=work)
            ready = negate_maximum(s, max_a, 2, len(CTX_CHUNKS))
            yield Step(ve=1.3, late=0.3)
            now["neg", s] = rows_of_maximum(s, ready)
            yield Step(pe=0.25, sc=0.5, ring=work, late=0.3)

        def wide_main(p, s, x_sb, now):
            pe.wait(now["neg", s], now["v", s])
            pending = []
            head_slot = [None, None]

            def values_of(step):
                k, kn, made = step
                for h in range(2):
                    i, view, ready = made[h]
                    pe.wait(ready, *free["pv_a"])
                    last = pe.mark(mm(pv_a[64 * h:64 * h + 64, :], v_wide[s][0:kn, k, 64 * h:64 * h + 64],
                                      view[0:kn, :], start=k == 0, stop=k == NKT - 1))
                for h in range(2):
                    i = made[h][0]
                    expo_a.freed[i] = expo_a.freed[i] + (last,)
                return last

            added = [None, None]
            for k, (k0, kn) in enumerate(CTX_TILES):
                made = []
                for h in range(2):
                    i, bank = score.next()
                    pe.wait(*score.freed[i])
                    for kind in range(3):
                        pe.do(mm(bank[0:kn, :], kbuf[:, s, 2 * h + kind // 2, k0:k0 + kn],
                                 qbuf[:, s, 3 * h + kind, :], start=kind == 0, stop=False))
                    done = pe.mark(mm(bank[0:kn, :], select_b[:, h, 0:kn], neg_rows[:, s, :], start=False))
                    e, view = expo_a.next()
                    sc.wait(done, *expo_a.freed[e])
                    ready = sc.mark(act(view[0:kn, :], bank[0:kn, :], ACT.Exp, WIDE ** -0.5))
                    score.freed[i] = (ready,)
                    made.append((e, view, ready))
                    expo_a.freed[e] = ()
                    if k == 0:
                        head_slot[h] = (e, view)
                    elif k == 1:
                        first, first_view = head_slot[h]
                        added[h] = po.step(tt(sums[0:kn, h, :], first_view[0:kn, :], view[0:kn, :], ALU.add),
                                           ready, *free[f"sum{h}"])
                        expo_a.freed[first] = expo_a.freed[first] + (added[h],)
                        expo_a.freed[e] = (added[h],)
                    else:
                        added[h] = po.step(tt(sums[0:kn, h, :], sums[0:kn, h, :], view[0:kn, :], ALU.add), ready)
                        expo_a.freed[e] = (added[h],)
                    yield Step(pe=0.87, sc=0.48, ring=score)
                pending.append((k, kn, made))
                if len(pending) > 1:
                    values_of(pending.pop(0))
                    yield Step(pe=0.91)
            kfree[s] = qfree[s] = negfree[s] = (done,)
            last = values_of(pending.pop(0))
            vfree[s] = (last,)
            taken = sc.step(acopy(raw_a[:, :], pv_a), last, *free["raw_a"])
            free["pv_a"] = [taken]
            yield Step(pe=0.91, sc=0.5, late=0.5)
            i, bank = work.next()
            pe.wait(*work.freed[i])
            for h in range(2):
                pe.wait(added[h])
                done = pe.mark(mm(bank[64 * h:64 * h + 64, :], ones_f[0:CTX_TILE, :], sums[0:CTX_TILE, h, :]))
                free[f"sum{h}"] = [done]
            ve.step(turn(rest[:, :], raw_a[:, :]), taken)
            work.freed[i] = (ve.step(turn(raw_a[:, :], bank), done),)
            ve.step(lambda e: e.reciprocal(inverse[:, :], blocks(raw_a)[:, :, 0]))
            ve.step(tt(blocks(rest), blocks(rest),
                       inverse[:, :].unsqueeze(2).to_broadcast([P, S // 32, 32]), ALU.mult))
            last = ve.step(turn(outT_a[:, :], rest[:, :]), *free["outT_a"])
            free["raw_a"] = [last]
            now["out"] = last
            yield Step(pe=0.9, ve=2.9, ring=work, late=0.3)

        def wide_output(p, x_sb, now):
            for i, q, psum, done in project_out(lambda g: outT_a, lambda g: w_pair[:, p % 2, 3, :], 1,
                                                (now["out"],)):
                now["x"] = ve.step(stt(x_sb[:, q, :], psum, gates[:, 0:1], x_sb[:, q, :], ALU.mult, ALU.add), done)
                work.freed[i] = (now["x"],)
                if q % 2:
                    yield Step(pe=0.86, ve=0.9, ring=work)
            free["outT_a"] = [done]
            pairfree[p % 2] = (done,)

        def context_parts(k_dram):
            readers = list(free["ctxT"])
            for f in range(FT):
                for c0, cn in CTX_CHUNKS:
                    _, last = split(ctxT[:, f, c0:c0 + cn], [kparts[:, n, c0:c0 + cn] for n in range(3)],
                                    (P, cn), *free["kparts"])
                    yield Step(ve=1.7, sc=0.45)
                sp.wait(last)
                for n in range(3):
                    l_kctx.dma(k_dram[n, f * P:(f + 1) * P, :], kparts[:, n, :])
                free["kparts"] = [l_kctx.all()]
            free["ctxT"] = readers + [last]
            yield Step()

        def block_1(b, sets, x_in, pair_in, handed):
            x_sb = x_bufs[b % 2]
            now = {"ctxT": handed["ctxT_in"]}
            ve.wait(*free["kparts"])
            ready = layer_norm(x_sb, xn_a, x_in)
            yield Step(ve=5, sc=1.0, late=2)
            xn_read, now["xnT"] = transpose_xn(xn_a, xnT_a, ready, *free["xnT_a"])
            free["kparts"] = [xn_read]
            yield Step(pe=1.0, sc=1.0, ring=work, late=0.2)
            yield from wide_project(0, pair_in, now)
            yield from wide_stack(0, sets[0], now)
            k_ctx = scratch(f"ctx_parts{b}", D, CTX)
            for p in range(PAIRS):
                s = sets[p % len(sets)]
                if p + 1 < PAIRS:
                    pair_in = load_pair(p + 1)
                    nxt = wide_project(p + 1, pair_in, now)
                    if len(sets) == 2:
                        nxt = chain(nxt, wide_stack(p + 1, sets[(p + 1) % 2], now))
                        yield from beside(wide_main(p, s, x_sb, now), nxt, 1.2)
                        yield from wide_output(p, x_sb, now)
                    else:
                        yield from beside(wide_main(p, s, x_sb, now), nxt, 0.12)
                        yield from beside(wide_stack(p + 1, s, now), wide_output(p, x_sb, now), 0.2)
                else:
                    yield from beside(wide_main(p, s, x_sb, now), context_parts(k_ctx), 0.25)
                    yield from wide_output(p, x_sb, now)
            if b + 1 < BATCHES:
                handed["ctxT_in"] = load_ctxT(b + 1)
            handed["k_ctx"], handed["k_ctx_in"], handed["x"] = k_ctx, l_kctx.all(), now["x"]

        def slim_load(g, s, spec):
            keys = spec["keys"]
            sp.wait(spec["k_in"], spec["q_in"], *kfree[s])
            for n, (qp, kp) in enumerate(TERMS):
                r = slice(n * SLIM, (n + 1) * SLIM)
                if spec["grouped"]:
                    l_kst[s].dma(kbuf[r, s, 0, 0:keys], spec["k_dram"][kp, g * SLIM:(g + 1) * SLIM, :])
                else:
                    l_kst[s].dma(kbuf[r, s, :, 0:keys],
                                 spec["k_dram"][kp, g * 64:(g + 1) * 64, :].rearrange("(h d) n -> d h n", d=SLIM))
            sp.wait(*qfree[s])
            for n, (qp, kp) in enumerate(TERMS):
                r = slice(n * SLIM, (n + 1) * SLIM)
                l_qst[s].dma(qbuf[r, s, 0:GROUP, :],
                             spec["q_dram"][qp, g * 64:(g + 1) * 64, :].rearrange("(h d) n -> d h n", d=SLIM))
            if "v_dram" in spec:
                sp.wait(*vfree[s])
                a, z = key_rows(spec["v_dram"][g])
                l_v[s].dma(v_group[s][0:CTX_TILE, 0:full, :, :].rearrange("p k h c -> p k (h c)"), a)
                l_v[s].dma(v_group[s][0:tail, full, :, :].rearrange("p h c -> p (h c)"), z)
            if spec["stale_ones"][s]:
                spec["stale_ones"][s] = False
                spec["ones_in", s] = po.step(memset(kbuf[STACK:STACK + 3, s, :, :], 1.0), *kfree[s])

        def slim_prep(g, s, spec):
            grouped, masked, keys = spec["grouped"], spec["masked"], spec["keys"]
            chunks = CTX_CHUNKS if keys == CTX else [(0, keys)]
            pe.wait(l_kst[s].all(), l_qst[s].all())
            for h in range(GROUP):
                for q in range(QT):
                    for c, (c0, cn) in enumerate(chunks):
                        i, bank = work.next()
                        pe.wait(*work.freed[i])
                        done = pe.mark(mm(bank[:, 0:cn], qbuf[0:STACK, s, h, q * P:(q + 1) * P],
                                          kbuf[0:STACK, s, 0 if grouped else h, c0:c0 + cn]))
                        ve.wait(done)
                        if masked:
                            ve.wait(newest(ve))
                            last = ve.mark(lambda e, h=h, q=q, c=c, c0=c0, cn=cn, bank=bank: e.tensor_tensor_reduce(
                                out=max_junk[:, 0:cn], in0=bank[:, 0:cn], in1=maskQ_sb[:, q, c0:c0 + cn],
                                scale=1.0, scalar=-3e38, op0=ALU.add, op1=ALU.max,
                                accum_out=max_b[:, h, q, c:c + 1]))
                        else:
                            last = ve.mark(rmax(max_b[:, h, q, c:c + 1], bank[:, 0:cn]))
                        work.freed[i] = (last,)
                        yield Step(pe=0.2, ve=0.5, ring=work)
            ready = negate_maximum(s, max_b, GROUP, len(chunks))
            yield Step(ve=1.5, late=0.3)
            last = rows_of_maximum(s, ready)
            sp.wait(last)
            for n in range(3):
                l_neg[s].dma(qbuf[STACK + n:STACK + n + 1, s, 0:GROUP, :],
                             neg_rows[GROUP * n:GROUP * n + GROUP, s, :])
            negfree[s] = (l_neg[s].all(),)
            yield Step(pe=0.25, sc=0.5, ring=work, late=3)

        def slim_main(g, s, spec):
            grouped, masked, tiles = spec["grouped"], spec["masked"], spec["tiles"]
            pe.wait(l_neg[s].all(), *spec["v_ready"])
            if ("ones_in", s) in spec:
                pe.wait(spec["ones_in", s])
            if "v_dram" in spec:
                pe.wait(l_v[s].all())
            pending = []

            def value_columns(k, kn, h):
                if "v_dram" in spec:
                    return v_group[s][0:kn, k, h, :]
                return v_self[0:kn, k, g if grouped else GROUP * g + h, :]

            def values_of(step):
                k, kn, made = step
                for h in range(GROUP):
                    i, view, ready = made[h]
                    pe.wait(ready, *free["pv_b"])
                    last = pe.mark(mm(pv_b[PAD * h:PAD * h + PAD, :], value_columns(k, kn, h),
                                      view[0:kn, :], start=k == 0, stop=k == len(tiles) - 1))
                for h in range(GROUP):
                    expo_b.freed[made[h][0]] = (last,)
                return last

            for k, (k0, kn) in enumerate(tiles):
                made = []
                for h in range(GROUP):
                    i, bank = score.next()
                    pe.wait(*score.freed[i])
                    op = mm(bank[0:kn, :], kbuf[0:STACK + 3, s, 0 if grouped else h, k0:k0 + kn],
                            qbuf[0:STACK + 3, s, h, :], stop=not masked)
                    if masked:
                        pe.do(op)
                        op = mm(bank[0:kn, :], ident_b[0:kn, 0:kn], maskT_sb[0:kn, k, :], start=False)
                    done = pe.mark(op)
                    e, view = expo_b.next()
                    sc.wait(done, *expo_b.freed[e])
                    ready = sc.mark(act(view[0:kn, :], bank[0:kn, :], ACT.Exp, spec["scale"]))
                    score.freed[i] = (ready,)
                    made.append((e, view, ready))
                    yield Step(pe=0.43 if masked else 0.22, sc=0.48, ring=score)
                pending.append((k, kn, made))
                if len(pending) > 1:
                    values_of(pending.pop(0))
                    yield Step(pe=0.94)
            kfree[s] = qfree[s] = (done,)
            last = values_of(pending.pop(0))
            vfree[1 if "v_dram" not in spec else s] = (last,)
            taken = sc.step(acopy(raw_b[:, :], pv_b), last, *free["raw_b"])
            free["pv_b"] = [taken]
            ve.step(turn(rest[:, :], raw_b[:, :]), taken)
            ve.step(lambda e: e.reciprocal(inverse[:, :], blocks(rest)[:, :, SLIM]))
            ve.step(tt(blocks(rest)[:, :, 0:SLIM], blocks(rest)[:, :, 0:SLIM],
                       inverse[:, :].unsqueeze(2).to_broadcast([P, S // 32, SLIM]), ALU.mult))
            last = ve.step(turn(outT_b[:, g, :], rest[:, :]), *free["outT_b"])
            free["raw_b"] = [last]
            spec["out"] = last
            yield Step(pe=0.94, ve=2.0, sc=0.5)

        def slim_attention(spec, sets):
            groups = HEADS // GROUP
            for g in range(len(sets)):
                slim_load(g, sets[g], spec)
            yield Step(late=spec["late"])
            yield from slim_prep(0, sets[0], spec)
            ratio = (64 / 60) if spec["keys"] == CTX else 1.0
            for g in range(groups):
                s = sets[g % len(sets)]
                if g + 1 < groups and len(sets) == 2:
                    nxt = slim_prep(g + 1, sets[(g + 1) % 2], spec)
                    yield from beside(slim_main(g, s, spec), nxt, ratio)
                    if g + 2 < groups:
                        slim_load(g + 2, s, spec)
                else:
                    yield from slim_main(g, s, spec)
                    if g + 1 < groups and len(sets) == 1:
                        slim_load(g + 1, s, spec)
                        yield Step(late=6)
                        yield from slim_prep(g + 1, s, spec)

        def scratch(name, rows_, n):
            return nc.dram_tensor(name, [3, rows_, n], BF16, kind="Internal").ap()

        def part_slots():
            flat = kbuf[:, 1, :, :].rearrange("p h n -> p (h n)")
            return [[flat[:, (3 * m + n) * S:(3 * m + n + 1) * S] for n in range(3)] for m in range(4)]

        def wide_view(ap):
            return ap.unsqueeze(2).to_broadcast([P, QT, EXPERTS])

        def top_two():
            tie_b = tie.unsqueeze(1).to_broadcast([P, QT, EXPERTS])
            src = prob
            for pick, best in ((pick1, best1), (pick2, best2)):
                ve.step(rmax(best[:, :], src[:, :, :]))
                ve.step(tt(hit[:, :, :], src[:, :, :], wide_view(best[:, :]), ALU.is_equal))
                ve.step(tt(hit[:, :, :], hit[:, :, :], tie_b, ALU.mult))
                ve.step(rmax(rstd[:, :], hit[:, :, :]))
                last = ve.step(tt(pick[:, :, :], hit[:, :, :], wide_view(rstd[:, :]), ALU.is_equal))
                if pick is pick1:
                    ve.step(stt(prob2[:, :, :], pick1[:, :, :], -4.0, prob[:, :, :], ALU.mult, ALU.add))
                    src = prob2
            return last

        def gate_logits(weights, ready):
            i, bank = work.next()
            pe.wait(ready, *work.freed[i])
            for q in range(QT):
                for f in range(FT):
                    done = pe.mark(mm(bank[:, q * EXPERTS:(q + 1) * EXPERTS], xnT_b[:, f, q * P:(q + 1) * P],
                                      weights[:, f, :], start=f == 0, stop=f == FT - 1))
            return i, bank[:, 0:QT * EXPERTS].rearrange("p (q e) -> p q e", q=QT), done

        def ones_in_values(heads):
            return po.step(memset(v_self[:, :, 0:heads, SLIM:PAD], 1.0), *vfree[1])

        def block_2(b, sets, now):
            x_sb = x_bufs[b % 2]
            kv = KV_HEADS * SLIM
            sp.wait(*free["out_w"])
            out_w_in = l_wp.dma(out_w[:, :, :], t["ow"])
            v_ones = ones_in_values(KV_HEADS)
            ready = layer_norm(x_sb, xn_b, now["x"])
            yield Step(ve=5, sc=1.0, late=2)
            _, xnT_ready = transpose_xn(xn_b, xnT_b, ready, *free["xnT_b"])
            yield Step(pe=1.0, sc=1.0, ring=work, late=0.2)
            q_dram, k_dram = scratch(f"q2_{b}", D, S), scratch(f"k2_{b}", kv, S)
            slots = part_slots()
            for m in range(3):
                n = P if m < 2 else 64
                i, bank = work.next()
                pe.wait(xnT_ready, small_in, *work.freed[i])
                for f in range(FT):
                    done = pe.mark(mm(bank[0:n, :], gqa_w[:, f, m * P:m * P + n], xnT_b[:, f, :],
                                      start=f == 0, stop=f == FT - 1))
                ve.wait(small_in)
                biased = ve.step(ts(raw_b[0:n, :], bank[0:n, :], qk_bias[0:n, m:m + 1], ALU.add), done, *free["raw_b"])
                work.freed[i] = (biased,)
                _, last = split(raw_b[0:n, :], [s_[0:n, :] for s_ in slots[m]], (n, S), biased, *kfree[1])
                free["raw_b"] = [last]
                sp.wait(last)
                for part in range(3):
                    dst = q_dram[part, m * P:m * P + n, :] if m < 2 else k_dram[part, :, :]
                    l_scratch.dma(dst, slots[m][part][0:n, :])
                yield Step(pe=1.7, ve=2.5, sc=0.5, ring=work)
            qk_in = l_scratch.all()
            kfree[1] = (qk_in,)
            i, bank = work.next()
            pe.wait(*work.freed[i])
            for k in range(QT):
                for f in range(FT):
                    done = pe.mark(mm(bank[:, k * kv:(k + 1) * kv], xnT_b[:, f, k * P:(k + 1) * P],
                                      gqa_w[:, f, D + kv:D + 2 * kv], start=f == 0, stop=f == FT - 1))
            last = ve.step(tt(v_self[:, :, 0:KV_HEADS, 0:SLIM],
                              bank[:, 0:QT * kv].rearrange("p (k h d) -> p k h d", k=QT, h=KV_HEADS),
                              row_vb.rearrange("p (h d) -> p h d", h=KV_HEADS).unsqueeze(1)
                              .to_broadcast([P, QT, KV_HEADS, SLIM]), ALU.add), done, *vfree[1])
            work.freed[i] = (last,)
            yield Step(pe=0.6, ve=0.5, ring=work, late=5)
            spec = {"grouped": True, "masked": False, "keys": S, "tiles": SELF_TILES, "scale": SLIM ** -0.5,
                    "k_dram": k_dram, "k_in": qk_in, "q_dram": q_dram, "q_in": qk_in,
                    "v_ready": (last, v_ones), "late": 9.0, "stale_ones": [True, True]}
            up_free, down_free = ([tuple(free["ws"]), tuple(free["ws"])] for _ in range(2))
            up_in, down_in = {}, {}

            def load_up(e):
                if e < EXPERTS:
                    sp.wait(*up_free[e % 2])
                    up_in[e] = l_up[e % 2].dma(w1_sb[:, e % 2, :, :], t["w1"][e])

            def load_down(e):
                if e < EXPERTS:
                    sp.wait(*down_free[e % 2])
                    down_in[e] = l_down[e % 2].dma(w2_sb[:, e % 2, :, :], t["w2"][e])

            for e in range(2):
                load_up(e)
                load_down(e)
            yield from slim_attention(spec, sets)
            for i, q, psum, done in project_out(lambda g: outT_b[:, g, :], lambda g: out_w[:, g, :], GROUP,
                                                (spec["out"], out_w_in)):
                ve.step(tt(xn_b[:, q, :], xn_b[:, q, :], row_ob, ALU.add), xnT_ready)
                last = ve.step(tt(xn_b[:, q, :], psum, xn_b[:, q, :], ALU.add), done)
                work.freed[i] = (last,)
                if q % 2:
                    yield Step(pe=3.5, ve=1.8, ring=work)
            free["outT_b"], free["out_w"] = [done], [done]
            rms(xn_b, RMS_EPS)
            for q in range(QT):
                last = ve.step(stt(xn_b[:, q, :], xn_b[:, q, :], rstd[:, q:q + 1], row_n1, ALU.mult, ALU.mult))
            yield Step(ve=4, sc=1.0, late=2)
            _, xnT_ready = transpose_xn(xn_b, xnT_b, last, done)
            yield Step(pe=1, sc=1, ring=work, late=0.2)
            i, logits, done = gate_logits(gate_w0, xnT_ready)
            sig = sc.step(act(prob[:, :, :], logits, ACT.Exp, -1.0), done, newest(ve))
            work.freed[i] = (sig,)
            ve.step(ts(prob[:, :, :], prob[:, :, :], 1.0, ALU.add), sig)
            ve.step(lambda e: e.reciprocal(prob[:, :, :], prob[:, :, :]))
            top_two()
            picked = pick2
            ve.step(tt(best1[:, :], best1[:, :], best2[:, :], ALU.add))
            ve.step(ts(best1[:, :], best1[:, :], 1e-6, ALU.add))
            ve.step(lambda e: e.reciprocal(best1[:, :], best1[:, :]))
            ve.step(tt(picked[:, :, :], pick1[:, :, :], pick2[:, :, :], ALU.add))
            ve.step(copy(before_b[:, :], before_f[:, :]), *free["chosen"])
            chosen = ve.step(copy(chosen_b[:, :, :], picked[:, :, :]))
            for q in range(QT):
                ve.step(tt(before_f[:, :], before_f[:, :], picked[:, q, :], ALU.add))
            ve.step(tt(combine[:, :, :], prob[:, :, :], picked[:, :, :], ALU.mult))
            ve.step(tt(combine[:, :, :], combine[:, :, :], wide_view(best1[:, :]), ALU.mult))
            yield Step(pe=2, ve=8, sc=1.5, late=0.5)
            i, bank = work.next()
            pe.wait(chosen, *work.freed[i])
            for q in range(QT):
                ranks_q = bank[:, q * EXPERTS:(q + 1) * EXPERTS]
                pe.do(mm(ranks_q, earlier_b[:, :], chosen_b[:, q, :], stop=False))
                for r in range(q):
                    pe.do(mm(ranks_q, ones_b[:, :], chosen_b[:, r, :], start=False, stop=False))
                done = pe.mark(mm(ranks_q, ones_b[:, :], before_b[:, :], start=False))
            free["chosen"] = [done]
            ranks = bank[:, 0:QT * EXPERTS].rearrange("p (q e) -> p q e", q=QT)
            last = ve.step(stt(combine[:, :, :], ranks, float(CAPACITY), combine[:, :, :], ALU.is_lt, ALU.mult), done)
            work.freed[i] = (last,)
            yield Step(ve=0.3, late=0.2)
            h_free = [tuple(m for i in range(4 * s, 4 * s + 4) for m in expo_b.freed[i]) for s in range(2)]
            hidden_ready = [None, None]

            def expert_up(e):
                s = e % 2
                for m in range(FFN // P):
                    i, bank = work.next()
                    pe.wait(up_in[e], xnT_ready, *work.freed[i])
                    for f in range(FT):
                        done = pe.mark(mm(bank, w1_sb[:, s, f, m * P:(m + 1) * P], xnT_b[:, f, :],
                                          start=f == 0, stop=f == FT - 1))
                    last = sc.step(act(hidden[:, s, m, :], bank, ACT.Gelu), done, *h_free[s])
                    work.freed[i] = (last,)
                    hidden_ready[s] = last
                    yield Step(pe=1.72, sc=0.5, ring=work)
                up_free[s] = (done,)
                load_up(e + 2)

            def expert_down(e):
                s = e % 2
                for q in range(0, QT, 2):
                    i, bank = work.next()
                    pe.wait(hidden_ready[s], down_in[e], *work.freed[i])
                    for j in range(2):
                        for m in range(FFN // P):
                            op = mm(bank[:, j * D:(j + 1) * D], hidden[:, s, m, (q + j) * P:(q + j + 1) * P],
                                    w2_sb[:, s, m, :], start=m == 0, stop=m == FFN // P - 1)
                            done = pe.mark(op) if m == FFN // P - 1 else pe.do(op)
                    for j in range(2):
                        last = ve.step(stt(xn_b[:, q + j, :], bank[:, j * D:(j + 1) * D],
                                           combine[:, q + j, e:e + 1], xn_b[:, q + j, :], ALU.mult, ALU.add), done)
                    work.freed[i] = (last,)
                    yield Step(pe=3.5, ve=0.8, ring=work)
                h_free[s] = down_free[s] = (done,)
                load_down(e + 2)

            yield from expert_up(0)
            for e in range(EXPERTS):
                if e + 1 < EXPERTS:
                    yield from expert_up(e + 1)
                yield from expert_down(e)
            done = h_free[(EXPERTS - 1) % 2][0]
            free["ws"], free["xnT_b"] = [done], [done]
            for i in range(8):
                expo_b.freed[i] = (done,)
            rms(xn_b, RMS_EPS)
            for q in range(QT):
                ve.step(stt(xn_b[:, q, :], xn_b[:, q, :], rstd[:, q:q + 1], row_n2, ALU.mult, ALU.mult))
                now["x"] = ve.step(stt(x_sb[:, q, :], xn_b[:, q, :], gates[:, 2:3], x_sb[:, q, :], ALU.mult, ALU.add))
            yield Step(ve=7, sc=2.5, late=1)

        def block_3(b, sets, now):
            x_sb = x_bufs[b % 2]
            sp.wait(masks_stored[0], *free["ws"])
            a, z = key_rows(maskT_dram)
            l_ws.dma(maskT_sb[0:CTX_TILE, 0:full, :], a)
            l_ws.dma(maskT_sb[0:tail, full, :], z)
            masks_in = l_ws.dma(maskQ_sb, maskQ_dram.rearrange("(q p) n -> p q n", p=P))
            sp.wait(*free["out_w"])
            out_w_in = l_wp.dma(out_w[:, :, :], t["w_out"])
            ready = layer_norm(x_sb, xn_b, now["x"])
            yield Step(ve=5, sc=1.0, late=2)
            _, xnT_ready = transpose_xn(xn_b, xnT_b, ready, *free["xnT_b"])
            yield Step(pe=1.0, sc=1.0, ring=work, late=0.2)
            q_dram = scratch(f"q3_{b}", D, S)
            slots = part_slots()
            for m in range(FT):
                _, last = split(xnT_b[:, m, :], slots[m], (P, S), xnT_ready, *kfree[1])
                sp.wait(last)
                for part in range(3):
                    l_scratch.dma(q_dram[part, m * P:(m + 1) * P, :], slots[m][part])
                yield Step(ve=2, sc=0.5, late=3)
            free["xnT_b"] = [last]
            kfree[1] = (l_scratch.all(),)
            spec = {"grouped": False, "masked": True, "keys": CTX, "tiles": CTX_TILES, "scale": D ** -0.5,
                    "k_dram": now["k_ctx"], "k_in": now["k_ctx_in"], "q_dram": q_dram, "q_in": l_scratch.all(),
                    "v_dram": t["ctx_v"][b], "v_ready": (), "late": 13.0, "stale_ones": [True, True]}
            ve.wait(masks_in)
            pe.wait(masks_in)
            yield from slim_attention(spec, sets)
            free["ws"] = [*kfree[0], *kfree[1], newest(ve)]
            for i, q, psum, done in project_out(lambda g: outT_b[:, g, :], lambda g: out_w[:, g, :], GROUP,
                                                (spec["out"], out_w_in)):
                ve.step(tt(xn_b[:, q, :], psum, row_bo, ALU.add), done)
                now["x"] = ve.step(stt(x_sb[:, q, :], xn_b[:, q, :], gates[:, 1:2], x_sb[:, q, :], ALU.mult, ALU.add))
                work.freed[i] = (now["x"],)
                if q % 2:
                    yield Step(pe=3.5, ve=1.8, ring=work)
            free["outT_b"], free["out_w"] = [done], [done]

        def block_4(b, sets, now):
            x_sb = x_bufs[b % 2]
            sp.wait(*free["ws"])
            l_ws.dma(wqkv_sb, t["wqkv"])
            ws_in = l_ws.dma(we_sb, t["we"])
            sp.wait(*free["out_w"])
            out_w_in = l_wp.dma(out_w[:, :, :], t["scatter"])
            v_ones = ones_in_values(HEADS)
            ready = layer_norm(x_sb, xn_b, now["x"])
            yield Step(ve=5, sc=1.0, late=2)
            _, xnT_ready = transpose_xn(xn_b, xnT_b, ready, *free["xnT_b"])
            yield Step(pe=1.0, sc=1.0, ring=work, late=0.2)
            q_dram, k_dram = scratch(f"q4_{b}", D, S), scratch(f"k4_{b}", D, S)
            slots = part_slots()
            for m in range(4):
                i, bank = work.next()
                pe.wait(xnT_ready, ws_in, *work.freed[i])
                for f in range(FT):
                    done = pe.mark(mm(bank, wqkv_sb[:, f, m * P:(m + 1) * P], xnT_b[:, f, :],
                                      start=f == 0, stop=f == FT - 1))
                biased = ve.step(ts(raw_b[:, :], bank, qk_bias[:, 3 + m:4 + m], ALU.add), done, *free["raw_b"])
                work.freed[i] = (biased,)
                _, last = split(raw_b[:, :], slots[m], (P, S), biased, *kfree[1])
                free["raw_b"] = [last]
                sp.wait(last)
                dst = q_dram if m < 2 else k_dram
                for part in range(3):
                    l_scratch.dma(dst[part, (m % 2) * P:(m % 2 + 1) * P, :], slots[m][part])
                yield Step(pe=1.7, ve=2.5, sc=0.5, ring=work)
            qk_in = l_scratch.all()
            kfree[1] = (qk_in,)
            for k in range(0, QT, 2):
                i, bank = work.next()
                pe.wait(*work.freed[i])
                for j in range(2):
                    for f in range(FT):
                        done = pe.mark(mm(bank[:, j * D:(j + 1) * D], xnT_b[:, f, (k + j) * P:(k + j + 1) * P],
                                          wqkv_sb[:, f, 2 * D:3 * D], start=f == 0, stop=f == FT - 1))
                last = ve.step(tt(v_self[:, k:k + 2, :, 0:SLIM],
                                  bank.rearrange("p (k h d) -> p k h d", k=2, h=HEADS),
                                  row_v1.rearrange("p (h d) -> p h d", h=HEADS).unsqueeze(1)
                                  .to_broadcast([P, 2, HEADS, SLIM]), ALU.add), done, *vfree[1])
                work.freed[i] = (last,)
                yield Step(pe=1.7, ve=0.6, ring=work)
            v_ready = (last, v_ones)
            i, logits, done = gate_logits(gate_w1, xnT_ready)
            work.freed[i] = (ve.step(tt(prob[:, :, :], logits,
                                        row_bg.unsqueeze(1).to_broadcast([P, QT, EXPERTS]), ALU.add), done),)
            ve.step(rmax(best1[:, :], prob[:, :, :]))
            last = ve.step(tt(prob[:, :, :], prob[:, :, :], wide_view(best1[:, :]), ALU.subtract))
            last = sc.step(act(prob[:, :, :], prob[:, :, :], ACT.Exp), last)
            ve.step(lambda e: e.reduce_sum(best1[:, :], prob[:, :, :], AX.X), last)
            ve.step(lambda e: e.reciprocal(best1[:, :], best1[:, :]))
            ve.step(tt(prob[:, :, :], prob[:, :, :], wide_view(best1[:, :]), ALU.mult))
            top_two()
            ve.step(tt(combine[:, :, :], pick1[:, :, :], pick2[:, :, :], ALU.add))
            comb = ve.step(tt(combine[:, :, :], combine[:, :, :], prob[:, :, :], ALU.mult))
            yield Step(ve=6, sc=1.5, late=1)
            i, bank = work.next()
            pe.wait(comb, *work.freed[i])
            for q in range(QT):
                done = pe.mark(transpose(bank[0:EXPERTS, q * P:(q + 1) * P], combine[:, q, :], ident))
            combT_ready = sc.step(acopy(combT, bank[0:EXPERTS, :]), done, *free["raw_b"])
            work.freed[i] = (combT_ready,)
            yield Step(pe=0.4, sc=0.5, late=0.3)
            for q in range(0, QT, 2):
                i, bank = work.next()
                pe.wait(combT_ready, *work.freed[i])
                for j in range(2):
                    done = pe.mark(mm(bank[:, j * D:(j + 1) * D], combT[:, (q + j) * P:(q + j + 1) * P], b_exp[:, :]))
                last = ve.step(copy(xn_b[:, q:q + 2, :], bank.rearrange("p (q n) -> p q n", q=2)), done, xnT_ready)
                work.freed[i] = (last,)
            free["raw_b"] = [done]
            yield Step(pe=1, ve=1, sc=0.5, late=3)
            spec = {"grouped": False, "masked": False, "keys": S, "tiles": SELF_TILES, "scale": SLIM ** -0.5,
                    "k_dram": k_dram, "k_in": qk_in, "q_dram": q_dram, "q_in": qk_in,
                    "v_ready": v_ready, "late": 1.0, "stale_ones": [True, True]}

            def experts():
                for e in range(EXPERTS):
                    for q in range(0, QT, 2):
                        i, bank = work.next()
                        pe.wait(*work.freed[i])
                        for j in range(2):
                            for f in range(FT):
                                done = pe.mark(mm(bank[:, j * D:(j + 1) * D], xnT_b[:, f, (q + j) * P:(q + j + 1) * P],
                                                  we_sb[:, e, f, :], start=f == 0, stop=f == FT - 1))
                        for j in range(2):
                            last = ve.step(stt(xn_b[:, q + j, :], bank[:, j * D:(j + 1) * D],
                                               combine[:, q + j, e:e + 1], xn_b[:, q + j, :], ALU.mult, ALU.add), done)
                        work.freed[i] = (last,)
                        yield Step(pe=1.72, ve=0.8, ring=work)
                free["ws"], free["xnT_b"] = [done], [done]

            yield from beside(slim_attention(spec, sets), experts(), 16 / 150)
            for i, q, psum, done in project_out(lambda g: outT_b[:, g, :], lambda g: out_w[:, g, :], GROUP,
                                                (spec["out"], out_w_in)):
                ve.step(tt(xn_b[:, q, :], psum, xn_b[:, q, :], ALU.add), done)
                last = ve.step(stt(x_sb[:, q, :], xn_b[:, q, :], gates[:, 3:4], x_sb[:, q, :], ALU.mult, ALU.add))
                work.freed[i] = (last,)
                if q % 2:
                    yield Step(pe=3.5, ve=1.8, ring=work)
            free["outT_b"], free["out_w"] = [done], [done]
            sp.wait(last)
            stored = l_out[b % 2].dma(out[b].rearrange("(q p) n -> p q n", p=P), x_sb[:, :, :])
            free[f"x{b % 2}"] = [stored]

        def blocks_2_to_4(b, sets, now):
            yield from block_2(b, sets, now)
            yield from block_3(b, sets, now)
            yield from block_4(b, sets, now)

        handed = {"ctxT_in": ctxT_in}
        pace = Pace()
        merge([block_1(0, [0, 1], x_in, first_pair_in, handed), make_masks()], [500.0, 5.0], pace)
        for b in range(BATCHES):
            now = dict(handed)
            if b + 1 < BATCHES:
                a = block_1(b + 1, [0], load_x(b + 1), load_pair(0), handed)
                costs = merge([a, blocks_2_to_4(b, [1], now)], [COST_A, COST_B], pace)
            else:
                costs = merge([blocks_2_to_4(b, [1, 0], now)], [COST_B], pace)
            if SHOW:
                print("costs", costs, pace.pe, pace.ve, pace.sc)

        sp.wait(l_out[0].all(), l_out[1].all(), l_scratch.all(), l_kctx.all(), l_stored.all())

        block = ctx.enter_context(nc.Block())

        @block.sync
        def _(eng):
            sp.run(eng)

        @block.tensor
        def _(eng):
            pe.run(eng)

        @block.scalar
        def _(eng):
            sc.run(eng)

        @block.vector
        def _(eng):
            ve.run(eng)

        @block.gpsimd
        def _(eng):
            po.run(eng)


BATCHES = B
COST_A, COST_B = 500.0, 550.0
SLACK = 0.3
WORK, SCORE = 3, 3
SHOW = False


def lay_out(inputs):
    def a(name):
        return np.asarray(inputs[name])

    def tiles(w):
        return np.ascontiguousarray(w.reshape(-1, P, w.shape[-1]).transpose(1, 0, 2))

    def padded(w):
        out = np.zeros((HEADS, PAD, w.shape[-1]), w.dtype)
        out[:, :SLIM] = w.reshape(HEADS, SLIM, -1)
        return tiles(out.reshape(HEADS * PAD, -1))

    consts = np.zeros((P, C_ALL), np.float32)
    consts[:, C_IDENT:C_IDENT + P] = np.eye(P)
    for h in range(2):
        consts[h:6:2, C_SELECT + h * P:C_SELECT + (h + 1) * P] = 1
    consts[:, C_TIE:C_EARLIER] = EXPERTS - np.arange(EXPERTS)
    consts[:, C_EARLIER:] = np.triu(np.ones((P, P)), 1)
    mask = a("mask_1x1xSxS2_ik0")[0, 0]
    pair = np.stack([a(n).reshape(FT, P, PAIRS, P) for n in ("L0_xattn_Wq", "L0_xattn_Wk", "L0_xattn_Wv")])
    pair = pair.transpose(3, 2, 0, 1, 4).reshape(PAIRS, P, 3, D)
    pair_out = a("L0_xattn_Wo").reshape(PAIRS, P, 1, D)
    ctx_v = np.ones((B, HEADS // GROUP, CTX, GROUP, PAD), np.float32)
    ctx_v[..., :SLIM] = a("ctx_1024").reshape(B, CTX, HEADS // GROUP, GROUP, SLIM).transpose(0, 2, 1, 3, 4)
    arrays = {
        "x": a("x"), "ctx_v": ctx_v.reshape(B, HEADS // GROUP, CTX, GROUP * PAD),
        "ctxT": np.ascontiguousarray(a("ctx_1024").transpose(0, 2, 1)),
        "maskQ": np.ascontiguousarray(mask), "maskT": np.ascontiguousarray(mask.T),
        "consts": consts,
        "w_pair": np.ascontiguousarray(np.concatenate([pair, pair_out], 2)),
        "gqa_w": tiles(np.concatenate([a("L0_ffn_qw"), a("L0_ffn_kw"), a("L0_ffn_vw")], 1)),
        "ow": padded(a("L0_ffn_ow")), "w_out": padded(a("L1_xattn_w_out").T),
        "scatter": padded(np.eye(D, dtype=np.float32)),
        "gate0": tiles(a("L0_ffn_gate_w")), "gate1": tiles(a("L1_ffn_W_gate")),
        "w1": np.stack([tiles(w) for w in a("L0_ffn_w1")]),
        "w2": np.stack([tiles(w) for w in a("L0_ffn_w2")]),
        "wqkv": tiles(a("L1_ffn_W_qkv")),
        "we": np.ascontiguousarray(a("L1_ffn_W_experts").reshape(EXPERTS, FT, P, D).transpose(2, 0, 1, 3)),
    }
    qk = np.zeros((7, P), np.float32)
    qk[0:2], qk[2, 0:64] = a("L0_ffn_qb").reshape(2, P), a("L0_ffn_kb")
    qk[3:7] = a("L1_ffn_b_qkv")[0:2 * D].reshape(4, P)
    arrays["qk_bias"] = np.ascontiguousarray(qk.T)
    for n in ("g_xattn", "g_ffn", "L0_ffn_vb", "L0_ffn_ob", "L0_ffn_norm1_w",
              "L0_ffn_norm2_w", "L1_xattn_b_out", "L1_ffn_b_qkv", "L1_ffn_b_gate", "L1_ffn_b_experts"):
        arrays[n] = a(n)
    return arrays


def kernel(**inputs):
    import concourse.bacc as bacc
    from concourse.bass_utils import run_bass_kernel_spmd

    nc = bacc.Bacc("TRN2", target_bir_lowering=False, num_devices=1)
    arrays = {"in_" + n: v for n, v in lay_out(inputs).items()}
    t = {n[3:]: nc.dram_tensor(n, v.shape, mybir.dt.from_np(v.dtype), kind="ExternalInput").ap()
         for n, v in arrays.items()}
    out = nc.dram_tensor("out_x", (B, S, D), F32, kind="ExternalOutput").ap()
    flamingo(nc, t, out)
    r = run_bass_kernel_spmd(nc, [arrays], core_ids=[0])
    return r.results[0]["out_x"]
```

```python
import numpy as np
import concourse.bass as bass
from concourse import mybir
from contextlib import ExitStack
from itertools import chain

B, S, D = 4, 512, 256
CTX = 1601
HEADS = 16
WIDE = 64
SLIM = 16
KV_HEADS = 4
EXPERTS, FFN = 8, 512
CAPACITY = int(1.25 * B * S * 2 / EXPERTS)
P = 128
BANK = 512
QT = S // P
FT = D // P
LN_EPS, RMS_EPS = 1e-5, 1e-6
MASKED = -1e20
GROUP = 4
PAD = P // GROUP
PAIRS = HEADS // 2

CTX_TILE = 124
CTX_TILES = [(k, min(CTX_TILE, CTX - k)) for k in range(0, CTX, CTX_TILE)]
CTX_CHUNKS = [(0, 401), (401, 400), (801, 400), (1201, 400)]
SELF_TILES = [(k, P) for k in range(0, S, P)]
NKT = len(CTX_TILES)

TERMS = [(0, 0), (0, 1), (0, 2), (1, 0), (1, 1), (2, 0)]
KEY_RUNS = (3, 2, 1)
QUERY_RUNS = [(0, 0, 3), (1, 3, 2), (2, 5, 1)]
STACK = len(TERMS) * SLIM

WORK, SCORE = 3, 3

HOP = 0.3
SLACK = 0.2
COST_A, COST_B = 500.0, 495.0
WIDE_PACE = (1.4, 3)
SHORT_PACE = (1.6, 8)
LONG_PACE = (1.5, 8)

F32, BF16, I32 = mybir.dt.float32, mybir.dt.bfloat16, mybir.dt.int32
ALU, ACT, AX = mybir.AluOpType, mybir.ActivationFunctionType, mybir.AxisListType

C_IDENT, C_SELECT, C_TIE, C_EARLIER = 0, P, 3 * P, 3 * P + EXPERTS
C_ALL = 4 * P + EXPERTS


class Lane:

    def __init__(self, sem):
        self.sem, self.queue, self.marks, self.seen = sem, [], 0, {}

    def do(self, emit):
        self.queue.append(emit)

    def mark(self, emit):
        self.marks += 1
        self.queue.append(lambda e: emit(e).then_inc(self.sem, 1))
        return (self.sem, self.marks)

    def wait(self, *marks):
        for sem, value in marks:
            if self.seen.get(sem.name, 0) < value:
                self.seen[sem.name] = value
                self.queue.append(lambda e, s=sem, v=value: e.wait_ge(s, v))

    def step(self, emit, *marks):
        if self.marks:
            self.wait((self.sem, self.marks))
        self.wait(*marks)
        return self.mark(emit)

    def run(self, engine):
        for emit in self.queue:
            emit(engine)


class Landing:

    def __init__(self, lane, sem):
        self.lane, self.sem, self.count = lane, sem, 0

    def dma(self, out, in_):
        self.count += 16
        self.lane.do(lambda e: e.dma_start(out, in_).then_inc(self.sem, 16))
        return (self.sem, self.count)

    def all(self):
        return (self.sem, self.count)


class Ring:

    def __init__(self, views):
        self.views, self.freed, self.turn = views, [()] * len(views), 0

    def next(self):
        i = self.turn % len(self.views)
        self.turn += 1
        return i, self.views[i]


def mm(out, lhsT, rhs, start=True, stop=True):
    return lambda e: e.matmul(out, lhsT, rhs, start=start, stop=stop)


def transpose(out, in_, ident):
    return lambda e: e.transpose(out, in_, ident)


def copy(out, in_):
    return lambda e: e.tensor_copy(out, in_)


def acopy(out, in_):
    return lambda e: e.activation(out, in_, ACT.Copy)


def act(out, in_, func, scale=1.0):
    return lambda e: e.activation(out, in_, func, scale=scale)


def tt(out, a, b, op):
    return lambda e: e.tensor_tensor(out, a, b, op)


def ts(out, a, s1, op0, s2=None, op1=None):
    if op1 is None:
        return lambda e: e.tensor_scalar(out, a, s1, None, op0)
    return lambda e: e.tensor_scalar(out, a, s1, s2, op0, op1)


def stt(out, a, s, b, op0, op1):
    return lambda e: e.scalar_tensor_tensor(out=out, in0=a, scalar=s, in1=b, op0=op0, op1=op1)


def rmax(out, in_):
    return lambda e: e.reduce_max(out, in_, AX.X)


def turn(out, in_):
    return lambda e: e.transpose(out, in_)


def blocks(tile):
    return tile[:, :].rearrange("p (b r) -> p b r", r=32)


def memset(ap, value):
    return lambda e: e.memset(ap, value)


def beside(main, prep, ratio, lead=0):
    debt = -lead * ratio
    for step in main:
        yield step
        debt += ratio
        while debt >= 1:
            debt -= 1
            more = next(prep, None)
            if more is not None:
                yield more
    yield from prep


class Step:

    def __init__(self, pe=0.0, ve=0.0, sc=0.0, ring=None, late=None):
        self.pe, self.ve, self.sc, self.ring, self.late = pe, ve, sc, ring, late


class Pace:

    def __init__(self):
        self.pe = self.ve = self.sc = 0.0
        self.rings = {}

    def start(self, step, ready):
        at = max(self.pe, ready)
        if step.ring:
            held = self.rings.setdefault(id(step.ring), [0.0] * len(step.ring.views))
            at = max(at, held[0])
        return at

    def add(self, step, ready):
        at = self.start(step, ready)
        end = at + step.pe
        if step.pe:
            self.pe = end
        if step.sc:
            self.sc = max(self.sc, end + HOP) + step.sc
        if step.ve:
            self.ve = max(self.ve, end + HOP, self.sc + HOP if step.sc else 0) + step.ve
        last = max(end, self.ve if step.ve else 0, self.sc if step.sc else 0)
        if step.ring:
            held = self.rings[id(step.ring)]
            held.pop(0)
            held.append(last + HOP)
        return end if step.late is None else last + step.late


def merge(chains, totals, pace):
    last, ready, done = {}, {}, {}
    for n in range(len(chains)):
        last[n], ready[n], done[n] = Step(), pace.pe, 0.0
    alive = list(range(len(chains)))
    while alive:
        at = {n: pace.start(last[n], ready[n]) for n in alive}
        first = min(at.values())
        n = min((n for n in alive if at[n] <= first + SLACK),
                key=lambda n: (not (last[n].ve > 0 and last[n].pe < 0.5), done[n] / totals[n]))
        step = next(chains[n], None)
        if step is None:
            alive.remove(n)
            continue
        ready[n] = pace.add(step, ready[n])
        done[n] += max(step.pe, 0.1)
        last[n] = step


def flamingo(nc, t, out):
    ctx = ExitStack()
    with ctx:
        def sb(name, shape, dt=F32):
            return ctx.enter_context(nc.sbuf_tensor(name, shape, dt))

        def sem(name):
            return ctx.enter_context(nc.semaphore(name))

        x_bufs = [sb(f"x{i}", [P, QT, D]) for i in range(2)]
        xnT_a = sb("xnT_a", [P, FT, S])
        xn_b = sb("xn_b", [P, QT, D])
        xnT_b = sb("xnT_b", [P, FT, S])
        ctxT = sb("ctxT", [P, FT, CTX])
        vbuf = sb("vbuf", [P, 2, QT * HEADS * PAD])
        kbuf = sb("kbuf", [P, 2, GROUP, CTX + 1], BF16)
        qbuf = sb("qbuf", [P, 2, 6, S], BF16)
        exps_a = sb("exps_a", [P, 6, S])
        exps_b = sb("exps_b", [P, 8, S])
        sums = sb("sums", [P, 2, S])
        ws = sb("ws", [P, NKT * 512])
        outT_a = sb("outT_a", [P, S])
        outT_b = sb("outT_b", [P, GROUP, S])
        kparts_t = sb("kparts", [P, 3 * CTX + 1], BF16)
        kparts = kparts_t[:, 0:3 * CTX].rearrange("p (a n) -> p a n", a=3)
        qparts = sb("qparts", [P, 3, S], BF16)
        rest = sb("rest", [P, S])
        raw_a = sb("raw_a", [P, S])
        raw_b = sb("raw_b", [P, S])
        inverse = sb("inverse", [P, S // 32])
        w_pair = sb("w_pair", [P, 2, 3, D])
        wo_pair = sb("wo_pair", [P, 2, D])
        ident_f = sb("ident_f", [P, C_ALL])
        ident_b = sb("ident_b", [P, P], BF16)
        select_b = sb("select_b", [P, 2, P], BF16)
        earlier_b = sb("earlier_b", [P, P], BF16)
        ones_b = sb("ones_b", [P, P], BF16)
        ones_f = sb("ones_f", [P, WIDE])
        max_a = sb("max_a", [P, 2, QT, 4])
        max_b = sb("max_b", [P, GROUP, QT, 4])
        neg_max = sb("neg_max", [P, GROUP, QT])
        neg_rest = sb("neg_rest", [P, GROUP, QT])
        max_junk = sb("max_junk", [P, 3, 402], BF16)
        neg_cols = sb("neg_cols", [P, 3, QT, P], BF16)
        neg_rows = sb("neg_rows", [P, 3, S], BF16)
        stats = sb("stats", [P, QT, 6])
        moments = sb("moments", [P, QT, 2])
        rstd = sb("rstd", [P, QT])
        gates = sb("gates", [P, 4])
        prob = sb("prob", [P, QT, EXPERTS])
        prob2 = sb("prob2", [P, QT, EXPERTS])
        hit = sb("hit", [P, QT, EXPERTS])
        pick1 = sb("pick1", [P, QT, EXPERTS])
        pick2 = sb("pick2", [P, QT, EXPERTS])
        best1 = sb("best1", [P, QT])
        best2 = sb("best2", [P, QT])
        combine = sb("combine", [P, QT, EXPERTS])
        chosen_b = sb("chosen_b", [P, QT, EXPERTS], BF16)
        before_b = sb("before_b", [P, EXPERTS], BF16)
        before_f = sb("before_f", [P, EXPERTS])
        combT = raw_b[0:EXPERTS, :]
        gqa_w = sb("gqa_w", [P, FT, D + 2 * KV_HEADS * SLIM])
        out_w = sb("out_w", [P, GROUP, D])
        gate_w0 = sb("gate_w0", [P, FT, EXPERTS])
        gate_w1 = sb("gate_w1", [P, FT, EXPERTS])
        qk_bias = sb("qk_bias", [P, 7])
        rows = sb("rows", [P, 4 * D + KV_HEADS * SLIM + D + EXPERTS])
        b_exp = sb("b_exp", [EXPERTS, D])

        row_ob, row_n1, row_n2, row_bo = (rows[:, i * D:(i + 1) * D] for i in range(4))
        row_vb = rows[:, 4 * D:4 * D + KV_HEADS * SLIM]
        row_v1 = rows[:, 4 * D + KV_HEADS * SLIM:5 * D + KV_HEADS * SLIM]
        row_bg = rows[:, 5 * D + KV_HEADS * SLIM:]

        ident = ident_f[:, C_IDENT:C_IDENT + P]
        tie = ident_f[:, C_TIE:C_TIE + EXPERTS]

        work_t = ctx.enter_context(nc.psum_tensor("work", [P, WORK, BANK], F32))
        score_t = ctx.enter_context(nc.psum_tensor("score", [P, SCORE, BANK], F32))
        pv_t = ctx.enter_context(nc.psum_tensor("pv", [P, 2, BANK], F32))
        work = Ring([work_t[:, i, :] for i in range(WORK)])
        score = Ring([score_t[:, i, :] for i in range(SCORE)])
        pv_a, pv_b = pv_t[:, 0, :], pv_t[:, 1, :]
        expo_a = Ring([exps_a[:, i, :] for i in range(6)])
        junks = Ring([max_junk[:, i, :] for i in range(3)])
        expo_b = Ring([exps_b[:, i, :] for i in range(8)])

        xn_a = kparts_t[:, :].bitcast(F32)[:, 0:QT * D].rearrange("p (q n) -> p q n", q=QT)
        w1_sb = ws[:, 0:2048].rearrange("p (s f n) -> p s f n", s=2, f=FT)
        w2_sb = ws[:, 2048:4096].rearrange("p (s f n) -> p s f n", s=2, f=FFN // P)
        hidden = exps_b[:, :, :].rearrange("p (s f) n -> p s f n", s=2)
        masks = ws[:, :].bitcast(BF16)
        maskT_sb = masks[:, 0:NKT * S].rearrange("p (k n) -> p k n", k=NKT)
        maskQ_sb = masks[:, NKT * S:NKT * S + QT * CTX].rearrange("p (q n) -> p q n", q=QT)
        we_sb = ws[:, 0:4096].rearrange("p (e f n) -> p e f n", e=EXPERTS, f=FT)
        wqkv_sb = ws[:, 4096:4096 + FT * 3 * D].rearrange("p (f n) -> p f n", f=FT)
        v_wide = [vbuf[:, s, 0:NKT * P].rearrange("p (k n) -> p k n", k=NKT) for s in range(2)]
        v_group = [vbuf[:, s, 0:NKT * P].rearrange("p (k h c) -> p k h c", k=NKT, h=GROUP) for s in range(2)]
        v_self = vbuf[:, 1, :].rearrange("p (k h c) -> p k h c", k=QT, h=HEADS)

        pe, sc, ve, po, sp = (Lane(sem("s_" + n)) for n in ("pe", "sc", "ve", "po", "sp"))

        def landing(name):
            return Landing(sp, sem("d_" + name))

        l_const, l_ctxT, l_ws, l_wp = (landing(n) for n in ("const", "ctxT", "ws", "wp"))
        l_x = [landing(f"x{i}") for i in range(2)]
        l_pair = [landing(f"pair{i}") for i in range(2)]
        l_wo = [landing(f"wo{i}") for i in range(2)]
        l_kst = [landing(f"kst{i}") for i in range(3)]
        l_neg = [landing(f"neg{i}") for i in range(3)]
        l_qst = [landing(f"qst{i}") for i in range(3)]
        l_v = [landing(f"v{i}") for i in range(2)]
        l_up = [landing(f"up{i}") for i in range(2)]
        l_down = [landing(f"down{i}") for i in range(2)]
        l_scratch, l_kctx, l_mask, l_stored, l_qmask = (
            landing(n) for n in ("scratch", "kctx", "mask", "stored", "qmask"))
        l_out = [landing(f"out{i}") for i in range(2)]

        free = {n: [] for n in ("ws", "outT_a", "outT_b", "kparts", "qparts", "out_w", "ctxT",
                                "raw_a", "raw_b", "pv_a", "pv_b", "sum0", "sum1",
                                "xnT_a", "xnT_b", "x0", "x1", "chosen")}
        kfree, qfree, vfree, negfree, colfree, pairfree, wofree = ([(), (), ()] for _ in range(7))

        def newest(lane):
            return (lane.sem, lane.marks)

        def load_x(b):
            sp.wait(*free[f"x{b % 2}"])
            return l_x[b % 2].dma(x_bufs[b % 2][:, :, :], t["x"][b].rearrange("(q p) n -> p q n", p=P))

        def load_ctxT(b):
            sp.wait(*free["ctxT"])
            return l_ctxT.dma(ctxT[:, :, :], t["ctxT"][b].rearrange("(f p) n -> p f n", p=P))

        def load_pair(p):
            sp.wait(*pairfree[p % 2])
            return l_pair[p % 2].dma(w_pair[:, p % 2, :, :], t["w_pair"][p])

        def load_wo(p):
            sp.wait(*wofree[p % 2])
            return l_wo[p % 2].dma(wo_pair[:, p % 2, :], t["L0_xattn_Wo"][p * P:(p + 1) * P, :])

        l_const.dma(ident_f[:, :], t["consts"])
        l_const.dma(gates[:, 0:2], t["g_xattn"].partition_broadcast(P))
        l_const.dma(gates[:, 2:4], t["g_ffn"].partition_broadcast(P))
        consts_in = l_const.all()
        x_in, ctxT_in, first_pair_in = load_x(0), load_ctxT(0), load_pair(0)

        po.mark(memset(ones_f[:, :], 1.0))
        po.mark(memset(ones_b[:, :], 1.0))
        po.mark(memset(before_f[:, :], 0.0))
        pool_ready = po.mark(memset(neg_cols[:, :, :, :], 0.0))
        gates_ready = sc.step(act(gates[:, :], gates[:, :], ACT.Tanh), consts_in)
        ve.wait(consts_in, pool_ready, gates_ready)
        ve.step(copy(ident_b[:, :], ident))
        ve.step(copy(select_b[:, :, :], ident_f[:, C_SELECT:C_TIE].rearrange("p (h n) -> p h n", h=2)))
        consts_ready = ve.step(copy(earlier_b[:, :], ident_f[:, C_EARLIER:C_ALL]))
        pe.wait(consts_ready)
        po.wait(consts_ready)

        l_small = landing("small")
        l_small.dma(gqa_w[:, :, :], t["gqa_w"])
        l_small.dma(gate_w0[:, :, :], t["gate0"])
        l_small.dma(gate_w1[:, :, :], t["gate1"])
        l_small.dma(qk_bias[:, :], t["qk_bias"])
        for row, src in ((row_ob, t["L0_ffn_ob"]), (row_n1, t["L0_ffn_norm1_w"]),
                         (row_n2, t["L0_ffn_norm2_w"]), (row_bo, t["L1_xattn_b_out"]),
                         (row_vb, t["L0_ffn_vb"]), (row_v1, t["L1_ffn_b_qkv"][2 * D:3 * D]),
                         (row_bg, t["L1_ffn_b_gate"])):
            l_small.dma(row, src.partition_broadcast(P))
        small_in = l_small.dma(b_exp[:, :], t["L1_ffn_b_experts"])

        maskT_dram = nc.dram_tensor("maskT_add", [NKT * CTX_TILE, S], BF16, kind="Internal").ap()
        maskQ_dram = nc.dram_tensor("maskQ_add", [S, CTX], BF16, kind="Internal").ap()
        full = NKT - 1
        tail = CTX_TILES[-1][1]

        def key_rows(ap):
            return (ap[0:full * CTX_TILE].rearrange("(k p) n -> p k n", p=CTX_TILE),
                    ap[full * CTX_TILE:CTX])

        def make_masks():
            ints = exps_b[:, :, :].bitcast(I32)
            landed = ()
            for k in range(0, full, 6):
                sp.wait(*landed)
                a, _ = key_rows(t["maskT"])
                here = l_mask.dma(ints[0:CTX_TILE, 0:6, :], a[:, k:k + 6, :])
                landed = (ve.step(ts(maskT_sb[0:CTX_TILE, k:k + 6, :], ints[0:CTX_TILE, 0:6, :], 0.0,
                                     ALU.is_equal, MASKED, ALU.mult), here),)
                yield Step(ve=4, late=4)
            sp.wait(*landed)
            here = l_mask.dma(ints[0:tail, 0, :], key_rows(t["maskT"])[1])
            landed = (ve.step(ts(maskT_sb[0:tail, full, :], ints[0:tail, 0, :], 0.0, ALU.is_equal,
                                 MASKED, ALU.mult), here),)
            sp.wait(*landed)
            a, z = key_rows(maskT_dram)
            l_stored.dma(a, maskT_sb[0:CTX_TILE, 0:full, :])
            l_stored.dma(z, maskT_sb[0:tail, full, :])
            yield Step()
            flat = ints.rearrange("p a n -> p (a n)")
            for q in range(0, QT, 2):
                sp.wait(*landed)
                view = flat[:, 0:2 * CTX].rearrange("p (q n) -> p q n", q=2)
                here = l_mask.dma(view, t["maskQ"][q * P:(q + 2) * P].rearrange("(q p) n -> p q n", p=P))
                landed = (ve.step(ts(maskQ_sb[:, q:q + 2, :], view, 0.0, ALU.is_equal, MASKED, ALU.mult), here),)
                yield Step(ve=4, late=4)
            sp.wait(*landed)
            masks_stored[0] = l_stored.dma(maskQ_dram.rearrange("(q p) n -> p q n", p=P), maskQ_sb)
            free["ws"] = [masks_stored[0]]
            for i in range(8):
                expo_b.freed[i] = landed

        masks_stored = [None]

        def inverse_root(src, scale, eps):
            ve.step(ts(rstd[:, :], src, scale, ALU.mult, eps, ALU.add))
            last = ve.step(lambda e: e.reciprocal(rstd[:, :], rstd[:, :]))
            return sc.step(act(rstd[:, :], rstd[:, :], ACT.Sqrt), last)

        def rms(src, eps):
            ve.wait(newest(ve))
            for q in range(QT):
                half = (q % 2) * D
                last = ve.mark(lambda e, q=q, half=half: e.tensor_tensor_reduce(
                    out=rest[:, half:half + D], in0=src[:, q, :], in1=src[:, q, :], scale=1.0, scalar=0.0,
                    op0=ALU.mult, op1=ALU.add, accum_out=rstd[:, q:q + 1]))
                if q % 2:
                    ve.wait(last)
            ve.wait(inverse_root(rstd[:, :], 1.0 / D, eps))

        def layer_norm(x_sb, xn, *after, stacked=False):
            ve.wait(newest(ve), *after)
            for q in range(QT):
                last = ve.mark(lambda e, q=q: e.bn_stats(stats[:, q, :], x_sb[:, q, :]))
            ve.wait(last)
            for q in range(QT):
                ve.mark(lambda e, q=q: e.bn_aggr(moments[:, q, :], stats[:, q, :]))
            ve.wait(inverse_root(moments[:, :, 1], 1.0, LN_EPS))
            return [ve.mark(ts(*(stacked_order(xn[:, q, :], x_sb[:, q, :]) if stacked else
                                 (xn[:, q, :], x_sb[:, q, :])),
                               moments[:, q, 0:1], ALU.subtract, rstd[:, q:q + 1], ALU.mult))
                    for q in range(QT)]

        def stacked_order(out_, in_):
            return (out_.rearrange("p (g d h) -> p g d h", g=HEADS // GROUP, h=GROUP),
                    in_.rearrange("p (g h d) -> p g d h", g=HEADS // GROUP, h=GROUP))

        def transpose_xn(xn, xnT, ready, *readers):
            for f in range(FT):
                i, bank = work.next()
                pe.wait(*work.freed[i])
                for q in range(QT):
                    pe.wait(ready[q])
                    done = pe.mark(transpose(bank[:, q * P:(q + 1) * P],
                                             xn[:, q, f * P:(f + 1) * P], ident))
                last = sc.step(acopy(xnT[:, f, :], bank), done, *readers)
                work.freed[i] = (last,)
            return done, last

        def split(src, parts, n, *after):
            high = sc.step(acopy(parts[0], src), *after)
            read = ve.step(tt(rest[0:n[0], 0:n[1]], src, parts[0], ALU.subtract), high, *after)
            ve.step(copy(parts[1], rest[0:n[0], 0:n[1]]))
            last = ve.step(tt(parts[2], rest[0:n[0], 0:n[1]], parts[1], ALU.subtract))
            return read, last

        def negate_maximum(s, chunked, heads, chunks):
            if chunks > 1:
                ve.step(rmax(neg_max[:, 0:heads, :], chunked[:, 0:heads, :, 0:chunks]), *colfree[s])
                src = neg_max[:, 0:heads, :]
            else:
                src = chunked[:, 0:heads, :, 0]
                ve.wait(*colfree[s])
            ve.step(ts(neg_max[:, 0:heads, :], src, -1.0, ALU.mult))
            src = neg_max[:, 0:heads, :]
            for i in range(3):
                part = neg_cols[:, s, :, i * heads:i * heads + heads].rearrange("p q h -> p h q")
                last = ve.step(copy(part, src))
                if i < 2:
                    ve.step(tt(neg_rest[:, 0:heads, :], src, part, ALU.subtract))
                    src = neg_rest[:, 0:heads, :]
            return last

        def rows_of_maximum(s, ready):
            i, bank = work.next()
            pe.wait(ready, *work.freed[i])
            for q in range(QT):
                done = pe.mark(mm(bank[:, q * P:(q + 1) * P], neg_cols[:, s, q, :], ident_b[:, :]))
            last = sc.step(acopy(neg_rows[:, s, :], bank), done, *negfree[s])
            work.freed[i] = (last,)
            colfree[s] = (done,)
            return last

        def project_out(lhs, weights, tiles, ready):
            for q in range(0, QT, 2):
                i, bank = work.next()
                pe.wait(*ready, *work.freed[i])
                for j in range(2):
                    for g in range(tiles):
                        op = mm(bank[:, j * D:(j + 1) * D],
                                lhs(g)[:, (q + j) * P:(q + j + 1) * P], weights(g),
                                start=g == 0, stop=g == tiles - 1)
                        done = pe.mark(op) if g == tiles - 1 else pe.do(op)
                for j in range(2):
                    yield i, q + j, bank[:, j * D:(j + 1) * D], done

        def wide_project(p, pair_in, now):
            w = w_pair[:, p % 2, :, :].rearrange("p a (f n) -> p a f n", f=FT)
            for c0, cn in CTX_CHUNKS:
                i, bank = work.next()
                pe.wait(pair_in, now["ctxT"], *work.freed[i])
                for f in range(FT):
                    done = pe.mark(mm(bank[:, 0:cn], w[:, 1, f, :], ctxT[:, f, c0:c0 + cn],
                                      start=f == 0, stop=f == FT - 1))
                read, last = split(bank[:, 0:cn], [kparts[:, n, c0:c0 + cn] for n in range(3)],
                                   (P, cn), done, *free["kparts"])
                work.freed[i] = (read,)
                yield Step(pe=1.34, ve=1.7, sc=0.45, ring=work)
            now["k"] = last
            i, bank = work.next()
            pe.wait(now["xnT"], *work.freed[i])
            for f in range(FT):
                done = pe.mark(mm(bank, w[:, 0, f, :], xnT_a[:, f, :], start=f == 0, stop=f == FT - 1))
            read, last = split(bank, [qparts[:, n, :] for n in range(3)], (P, S), done, *free["qparts"])
            work.freed[i] = (read,)
            now["q"] = last
            free["xnT_a"] = [done]
            yield Step(pe=1.72, ve=1.9, sc=0.5, ring=work)

        def wide_stack(p, s, now):
            sp.wait(now["k"], *kfree[s])
            for h in range(2):
                own, other = slice(64 * h, 64 * h + 64), slice(64 - 64 * h, 128 - 64 * h)
                for kind in range(2):
                    l_kst[s].dma(kbuf[own, s, 2 * h + kind, 0:CTX], kparts[own, 0, :])
                l_kst[s].dma(kbuf[other, s, 2 * h:2 * h + 2, 0:CTX], kparts[own, 1:3, :])
            k_in = l_kst[s].all()
            free["kparts"] = [k_in]
            sp.wait(now["q"], *qfree[s])
            for h in range(2):
                own, other = slice(64 * h, 64 * h + 64), slice(64 - 64 * h, 128 - 64 * h)
                l_qst[s].dma(qbuf[own, s, 3 * h:3 * h + 3, :], qparts[own, :, :])
                l_qst[s].dma(qbuf[other, s, 3 * h:3 * h + 2, :], qparts[own, 0:2, :])
                l_qst[s].dma(qbuf[other, s, 3 * h + 2, :], qparts[own, 0, :])
            q_in = l_qst[s].all()
            free["qparts"] = [q_in]
            w = w_pair[:, p % 2, :, :].rearrange("p a (f n) -> p a f n", f=FT)
            for k in range(0, NKT, 4):
                some = CTX_TILES[k:k + 4]
                i, bank = work.next()
                pe.wait(*work.freed[i])
                for j, (k0, kn) in enumerate(some):
                    for f in range(FT):
                        op = mm(bank[0:kn, j * P:(j + 1) * P], ctxT[:, f, k0:k0 + kn], w[:, 2, f, :],
                                start=f == 0, stop=f == FT - 1)
                        done = pe.mark(op) if f == FT - 1 else pe.do(op)
                kn, n = some[0][1], len(some)
                last = sc.step(acopy(v_wide[s][0:kn, k:k + n, :],
                                     bank[0:kn, 0:n * P].rearrange("p (j n) -> p j n", j=n)), done, *vfree[s])
                work.freed[i] = (last,)
                yield Step(pe=1.72, sc=0.5, ring=work)
            now["v", s] = last
            free["ctxT"] = pairfree[p % 2] = (done,)
            pe.wait(k_in, q_in)
            for h in range(2):
                for q in range(QT):
                    for c, (c0, cn) in enumerate(CTX_CHUNKS):
                        i, bank = work.next()
                        pe.wait(*work.freed[i])
                        done = pe.mark(mm(bank[:, 0:cn], qbuf[:, s, 3 * h, q * P:(q + 1) * P],
                                          kbuf[:, s, 2 * h, c0:c0 + cn]))
                        ve.wait(done)
                        work.freed[i] = (ve.mark(rmax(max_a[:, h, q, c:c + 1], bank[:, 0:cn])),)
                        yield Step(pe=0.18, ve=0.5, ring=work)
            ready = negate_maximum(s, max_a, 2, len(CTX_CHUNKS))
            yield Step(ve=1.3, late=0.3)
            yield Step()
            now["neg", s] = rows_of_maximum(s, ready)
            yield Step(pe=0.25, sc=0.5, ring=work, late=0.3)

        def wide_main(p, s, x_sb, now):
            pe.wait(now["neg", s], now["v", s])
            pending = []
            head_slot = [None, None]

            def values_of(step):
                k, kn, made = step
                for h in range(2):
                    i, view, ready = made[h]
                    pe.wait(ready, *free["pv_a"])
                    last = pe.mark(mm(pv_a[64 * h:64 * h + 64, :], v_wide[s][0:kn, k, 64 * h:64 * h + 64],
                                      view[0:kn, :], start=k == 0, stop=k == NKT - 1))
                for h in range(2):
                    i = made[h][0]
                    expo_a.freed[i] = expo_a.freed[i] + (last,)
                return last

            added = [None, None]
            for k, (k0, kn) in enumerate(CTX_TILES):
                made = []
                for h in range(2):
                    i, bank = score.next()
                    pe.wait(*score.freed[i])
                    for kind in range(3):
                        pe.do(mm(bank[0:kn, :], kbuf[:, s, 2 * h + kind // 2, k0:k0 + kn],
                                 qbuf[:, s, 3 * h + kind, :], start=kind == 0, stop=False))
                    done = pe.mark(mm(bank[0:kn, :], select_b[:, h, 0:kn], neg_rows[:, s, :], start=False))
                    e, view = expo_a.next()
                    sc.wait(done, *expo_a.freed[e])
                    ready = sc.mark(act(view[0:kn, :], bank[0:kn, :], ACT.Exp, WIDE ** -0.5))
                    score.freed[i] = (ready,)
                    made.append((e, view, ready))
                    expo_a.freed[e] = ()
                    if k == 0:
                        head_slot[h] = (e, view)
                    elif k == 1:
                        first, first_view = head_slot[h]
                        added[h] = po.step(tt(sums[0:kn, h, :], first_view[0:kn, :], view[0:kn, :], ALU.add),
                                           ready, *free[f"sum{h}"])
                        expo_a.freed[first] = expo_a.freed[first] + (added[h],)
                        expo_a.freed[e] = (added[h],)
                    else:
                        added[h] = po.step(tt(sums[0:kn, h, :], sums[0:kn, h, :], view[0:kn, :], ALU.add), ready)
                        expo_a.freed[e] = (added[h],)
                    yield Step(pe=0.87, sc=0.48, ring=score)
                pending.append((k, kn, made))
                if len(pending) > 1:
                    values_of(pending.pop(0))
                    yield Step(pe=0.91)
            kfree[s] = qfree[s] = negfree[s] = (done,)
            last = values_of(pending.pop(0))
            vfree[s] = (last,)
            taken = sc.step(acopy(raw_a[:, :], pv_a), last, *free["raw_a"])
            free["pv_a"] = [taken]
            yield Step(pe=0.91, sc=0.5, late=0.5)
            i, bank = work.next()
            pe.wait(*work.freed[i])
            for h in range(2):
                pe.wait(added[h])
                done = pe.mark(mm(bank[64 * h:64 * h + 64, :], ones_f[0:CTX_TILE, :], sums[0:CTX_TILE, h, :]))
                free[f"sum{h}"] = [done]
            ve.step(turn(rest[:, :], raw_a[:, :]), taken)
            work.freed[i] = (ve.step(turn(raw_a[:, :], bank), done),)
            ve.step(lambda e: e.reciprocal(inverse[:, :], blocks(raw_a)[:, :, 0]))
            ve.step(tt(blocks(rest), blocks(rest),
                       inverse[:, :].unsqueeze(2).to_broadcast([P, S // 32, 32]), ALU.mult))
            last = ve.step(turn(outT_a[:, :], rest[:, :]), *free["outT_a"])
            free["raw_a"] = [last]
            now["out"] = last
            yield Step(pe=0.9, ve=2.9, ring=work, late=0.3)

        def wide_output(p, x_sb, now):
            for i, q, psum, done in project_out(lambda g: outT_a, lambda g: wo_pair[:, p % 2, :], 1,
                                                (now["out"], now["wo", p])):
                ve.wait(now["rows"][q], done)
                now["x"] = now["rows"][q] = ve.mark(
                    stt(x_sb[:, q, :], psum, gates[:, 0:1], x_sb[:, q, :], ALU.mult, ALU.add))
                work.freed[i] = (now["x"],)
                if q % 2:
                    yield Step(pe=0.86, ve=0.9, ring=work)
            free["outT_a"] = [done]
            wofree[p % 2] = (done,)

        def context_parts(k_dram):
            readers = list(free["ctxT"])
            for f in range(FT):
                for c0, cn in CTX_CHUNKS:
                    _, last = split(ctxT[:, f, c0:c0 + cn], [kparts[:, n, c0:c0 + cn] for n in range(3)],
                                    (P, cn), *free["kparts"])
                    yield Step(ve=1.7, sc=0.45)
                sp.wait(last)
                store_keys(l_kctx, k_dram, f, kparts)
                free["kparts"] = [l_kctx.all()]
            free["ctxT"] = readers + [last]
            yield Step()

        def block_1(b, sets, x_in, pair_in, handed):
            x_sb = x_bufs[b % 2]
            now = {"ctxT": handed["ctxT_in"]}
            ve.wait(*free["kparts"])
            ready = layer_norm(x_sb, xn_a, x_in)
            yield Step(ve=3, sc=1.5, late=1.5)
            xn_read, now["xnT"] = transpose_xn(xn_a, xnT_a, ready, *free["xnT_a"])
            free["kparts"] = [xn_read]
            yield Step(pe=1.0, sc=1.0, ring=work, late=0.2)
            now["rows"] = ready
            yield from wide_project(0, pair_in, now)
            yield from wide_stack(0, sets[0], now)
            k_ctx = scratch(f"ctx_parts{b}", 3, GROUP, CTX)
            for p in range(PAIRS):
                s = sets[p % len(sets)]
                now["wo", p] = load_wo(p)
                nxt = []
                if p + 1 < PAIRS:
                    nxt.append(wide_project(p + 1, load_pair(p + 1), now))
                else:
                    nxt.append(context_parts(k_ctx))
                if len(sets) == 2:
                    if p:
                        nxt.insert(0, wide_output(p - 1, x_sb, now))
                    if p + 1 < PAIRS:
                        nxt.append(wide_stack(p + 1, sets[(p + 1) % 2], now))
                    yield from beside(wide_main(p, s, x_sb, now), chain(*nxt), *WIDE_PACE)
                else:
                    yield from beside(wide_main(p, s, x_sb, now), chain(*nxt), 0.2 if p + 1 < PAIRS else 0.25)
                    if p + 1 < PAIRS:
                        yield from beside(wide_stack(p + 1, s, now), wide_output(p, x_sb, now), 0.1)
            yield from wide_output(PAIRS - 1, x_sb, now)
            if b + 1 < B:
                handed["ctxT_in"] = load_ctxT(b + 1)
            handed["k_ctx"], handed["k_ctx_in"], handed["x"] = k_ctx, l_kctx.all(), now["x"]

        def k_place(s, keys):
            return kbuf[:, s, :, 0:keys] if s < 2 else kbuf[:, 1, :, keys:2 * keys]

        def q_place(s):
            return qbuf[:, s, 0:GROUP, :] if s < 2 else kbuf[:, 1, :, 2 * S:3 * S]

        def load_keys(g, s, spec):
            keys = spec["keys"]
            sp.wait(spec["k_in"], *kfree[s])
            row = 0
            for count in KEY_RUNS:
                rows_, row = slice(row, row + count * SLIM), row + count * SLIM
                src = spec["k_dram"][g, 0:count].rearrange("a d h n -> (a d) h n")
                if spec["grouped"]:
                    l_kst[s].dma(k_place(s, keys)[rows_, 0, :], src[:, 0, :])
                else:
                    l_kst[s].dma(k_place(s, keys)[rows_, :, :], src)
            if "v_dram" in spec:
                sp.wait(*vfree[s])
                a, z = key_rows(spec["v_dram"][g])
                l_v[s].dma(v_group[s][0:CTX_TILE, 0:full, :, :].rearrange("p k h c -> p k (h c)"), a)
                l_v[s].dma(v_group[s][0:tail, full, :, :].rearrange("p h c -> p (h c)"), z)
            if spec["stale_ones"][s]:
                spec["stale_ones"][s] = False
                spec["ones_in", s] = po.step(memset(k_place(s, keys)[STACK:STACK + 3, :, :], 1.0), *kfree[s])

        def load_queries(g, s, spec):
            sp.wait(spec["q_in"], *qfree[s])
            l_qst[s].dma(q_place(s)[0:STACK, :, :], spec["q_dram"][g].rearrange("a d h n -> (a d) h n"))

        def slim_load(g, s, spec):
            load_keys(g, s, spec)
            load_queries(g, s, spec)

        def slim_prep(g, s, spec):
            grouped, masked, keys = spec["grouped"], spec["masked"], spec["keys"]
            chunks = CTX_CHUNKS if keys == CTX else [(0, keys)]
            pe.wait(l_kst[s].all(), l_qst[s].all())
            for h in range(GROUP):
                for q in range(QT):
                    for c, (c0, cn) in enumerate(chunks):
                        i, bank = work.next()
                        pe.wait(*work.freed[i])
                        done = pe.mark(mm(bank[:, 0:cn], q_place(s)[0:STACK, h, q * P:(q + 1) * P],
                                          k_place(s, keys)[0:STACK, 0 if grouped else h, c0:c0 + cn]))
                        ve.wait(done)
                        if masked:
                            j, junk = junks.next()
                            ve.wait(*junks.freed[j])
                            last = ve.mark(lambda e, h=h, q=q, c=c, c0=c0, cn=cn, bank=bank, junk=junk: (
                                e.tensor_tensor_reduce)(
                                out=junk[:, 0:cn], in0=bank[:, 0:cn], in1=maskQ_sb[:, q, c0:c0 + cn],
                                scale=1.0, scalar=-3e38, op0=ALU.add, op1=ALU.max,
                                accum_out=max_b[:, h, q, c:c + 1]))
                            junks.freed[j] = (last,)
                        else:
                            last = ve.mark(rmax(max_b[:, h, q, c:c + 1], bank[:, 0:cn]))
                        work.freed[i] = (last,)
                        yield Step(pe=0.2, ve=0.5, ring=work)
            ready = negate_maximum(s, max_b, GROUP, len(chunks))
            yield Step(ve=1.5, late=0.3)
            for _ in range(4):
                yield Step()
            last = rows_of_maximum(s, ready)
            sp.wait(last)
            for n in range(3):
                l_neg[s].dma(q_place(s)[STACK + n:STACK + n + 1, :, :],
                             neg_rows[GROUP * n:GROUP * n + GROUP, s, :])
            negfree[s] = (l_neg[s].all(),)
            yield Step(pe=0.25, sc=0.5, ring=work, late=3)

        def slim_main(g, s, spec):
            grouped, masked, tiles = spec["grouped"], spec["masked"], spec["tiles"]
            pe.wait(l_neg[s].all(), *spec["v_ready"])
            if ("ones_in", s) in spec:
                pe.wait(spec["ones_in", s])
            if "v_dram" in spec:
                pe.wait(l_v[s].all())
            pending = []

            def value_columns(k, kn, h):
                if "v_dram" in spec:
                    return v_group[s][0:kn, k, h, :]
                return v_self[0:kn, k, g if grouped else GROUP * g + h, :]

            def values_of(step):
                k, kn, made = step
                for h in range(GROUP):
                    i, view, ready = made[h]
                    pe.wait(ready, *free["pv_b"])
                    last = pe.mark(mm(pv_b[PAD * h:PAD * h + PAD, :], value_columns(k, kn, h),
                                      view[0:kn, :], start=k == 0, stop=k == len(tiles) - 1))
                for h in range(GROUP):
                    expo_b.freed[made[h][0]] = (last,)
                return last

            for k, (k0, kn) in enumerate(tiles):
                made = []
                for h in range(GROUP):
                    i, bank = score.next()
                    pe.wait(*score.freed[i])
                    op = mm(bank[0:kn, :], k_place(s, spec["keys"])[0:STACK + 3, 0 if grouped else h, k0:k0 + kn],
                            q_place(s)[0:STACK + 3, h, :], stop=not masked)
                    if masked:
                        pe.do(op)
                        op = mm(bank[0:kn, :], ident_b[0:kn, 0:kn], maskT_sb[0:kn, k, :], start=False)
                    done = pe.mark(op)
                    e, view = expo_b.next()
                    sc.wait(done, *expo_b.freed[e])
                    ready = sc.mark(act(view[0:kn, :], bank[0:kn, :], ACT.Exp, spec["scale"]))
                    score.freed[i] = (ready,)
                    made.append((e, view, ready))
                    yield Step(pe=0.43 if masked else 0.22, sc=0.48, ring=score)
                pending.append((k, kn, made))
                if len(pending) > 1:
                    values_of(pending.pop(0))
                    yield Step(pe=0.94)
            kfree[s] = qfree[s] = (done,)
            last = values_of(pending.pop(0))
            vfree[1 if "v_dram" not in spec else s] = (last,)
            taken = sc.step(acopy(raw_b[:, :], pv_b), last, *free["raw_b"])
            free["pv_b"] = [taken]
            ve.step(turn(rest[:, :], raw_b[:, :]), taken)
            ve.step(lambda e: e.reciprocal(inverse[:, :], blocks(rest)[:, :, SLIM]))
            ve.step(tt(blocks(rest)[:, :, 0:SLIM], blocks(rest)[:, :, 0:SLIM],
                       inverse[:, :].unsqueeze(2).to_broadcast([P, S // 32, SLIM]), ALU.mult))
            last = ve.step(turn(outT_b[:, g, :], rest[:, :]), *free["outT_b"])
            free["raw_b"] = [last]
            spec["out"] = last
            yield Step(pe=0.94, ve=2.0, sc=0.5)

        def first_loads(spec, sets):
            if sets == [1] and spec["keys"] == S:
                sets = [1, 2]
                kfree[2] = qfree[2] = kfree[1]
            for g, s in enumerate(sets):
                if not spec.get("keys_loaded"):
                    load_keys(g, s, spec)
                load_queries(g, s, spec)
            return sets

        def slim_attention(spec, sets):
            groups = HEADS // GROUP
            if spec["masked"]:
                a, z = key_rows(maskT_dram)
                l_ws.dma(maskT_sb[0:CTX_TILE, 0:full, :], a)
                spec["v_ready"] = (l_ws.dma(maskT_sb[0:tail, full, :], z),)
                ve.wait(spec["q_mask_in"])
            yield Step(late=spec["late"])
            yield from slim_prep(0, sets[0], spec)
            steps_behind = LONG_PACE if spec["keys"] == CTX else SHORT_PACE
            for g in range(groups):
                s = sets[g % len(sets)]
                if g + 1 < groups and len(sets) == 2:
                    nxt = slim_prep(g + 1, sets[(g + 1) % 2], spec)
                    yield from beside(slim_main(g, s, spec), nxt, *steps_behind)
                    if g + 2 < groups:
                        slim_load(g + 2, s, spec)
                else:
                    yield from slim_main(g, s, spec)
                    if g + 1 < groups and len(sets) == 1:
                        slim_load(g + 1, s, spec)
                        yield Step(late=6)
                        yield from slim_prep(g + 1, s, spec)
            if 2 in sets:
                kfree[1] = kfree[1] + kfree[2] + qfree[2]

        def scratch(name, parts, heads, n):
            return nc.dram_tensor(name, [HEADS // GROUP, parts, SLIM, heads, n], BF16, kind="Internal").ap()

        def store_keys(land, k_dram, m, parts):
            for j in range(2):
                land.dma(k_dram[2 * m + j].rearrange("a d h n -> (d h) a n"), parts[64 * j:64 * j + 64, :, :])

        def store_queries(q_dram, m, parts):
            for j in range(2):
                dst = q_dram[2 * m + j].rearrange("a d h n -> (d h) a n")
                for part, first, count in QUERY_RUNS:
                    src = parts[64 * j:64 * j + 64, part, :].unsqueeze(1).to_broadcast([64, count, S])
                    l_scratch.dma(dst[:, first:first + count, :], src)

        def part_slots():
            flat = exps_b[:, :, :].rearrange("p i n -> p (i n)").bitcast(BF16)
            slots = [flat[:, 3 * m * S:3 * (m + 1) * S].rearrange("p (a n) -> p a n", a=3) for m in range(4)]
            return slots, [mark for freed in expo_b.freed for mark in freed]

        def parts_stored(mark):
            for i in range(8):
                expo_b.freed[i] = (mark,)

        def wide_view(ap):
            return ap.unsqueeze(2).to_broadcast([P, QT, EXPERTS])

        def top_two():
            tie_b = tie.unsqueeze(1).to_broadcast([P, QT, EXPERTS])
            src = prob
            for pick, best in ((pick1, best1), (pick2, best2)):
                ve.step(rmax(best[:, :], src[:, :, :]))
                ve.step(tt(hit[:, :, :], src[:, :, :], wide_view(best[:, :]), ALU.is_equal))
                ve.step(tt(hit[:, :, :], hit[:, :, :], tie_b, ALU.mult))
                ve.step(rmax(rstd[:, :], hit[:, :, :]))
                last = ve.step(tt(pick[:, :, :], hit[:, :, :], wide_view(rstd[:, :]), ALU.is_equal))
                if pick is pick1:
                    ve.step(stt(prob2[:, :, :], pick1[:, :, :], -4.0, prob[:, :, :], ALU.mult, ALU.add))
                    src = prob2
            return last

        def gate_logits(weights, ready):
            i, bank = work.next()
            pe.wait(ready, *work.freed[i])
            for q in range(QT):
                for f in range(FT):
                    done = pe.mark(mm(bank[:, q * EXPERTS:(q + 1) * EXPERTS], xnT_b[:, f, q * P:(q + 1) * P],
                                      weights[:, f, :], start=f == 0, stop=f == FT - 1))
            return i, bank[:, 0:QT * EXPERTS].rearrange("p (q e) -> p q e", q=QT), done

        def ones_in_values(heads):
            return po.step(memset(v_self[:, :, 0:heads, SLIM:PAD], 1.0), *vfree[1])

        def block_2(b, sets, now):
            x_sb = x_bufs[b % 2]
            kv = KV_HEADS * SLIM
            sp.wait(*free["out_w"])
            out_w_in = l_wp.dma(out_w[:, :, :], t["ow"])
            v_ones = ones_in_values(KV_HEADS)
            ready = layer_norm(x_sb, xn_b, now["x"])
            yield Step(ve=3, sc=1.5, late=1.5)
            _, xnT_ready = transpose_xn(xn_b, xnT_b, ready, *free["xnT_b"])
            yield Step(pe=1.0, sc=1.0, ring=work, late=0.2)
            q_dram = scratch(f"q2_{b}", len(TERMS), GROUP, S)
            k_dram = scratch(f"k2_{b}", 3, 1, S)
            slots, slots_free = part_slots()
            spec = {"grouped": True, "masked": False, "keys": S, "tiles": SELF_TILES, "scale": SLIM ** -0.5,
                    "k_dram": k_dram, "q_dram": q_dram, "late": 9.0, "stale_ones": [True] * 3}
            for m in (0, 2, 1):
                n = P if m < 2 else 64
                i, bank = work.next()
                pe.wait(xnT_ready, small_in, *work.freed[i])
                for f in range(FT):
                    done = pe.mark(mm(bank[0:n, :], gqa_w[:, f, m * P:m * P + n], xnT_b[:, f, :],
                                      start=f == 0, stop=f == FT - 1))
                ve.wait(small_in)
                biased = ve.step(ts(raw_b[0:n, :], bank[0:n, :], qk_bias[0:n, m:m + 1], ALU.add), done, *free["raw_b"])
                work.freed[i] = (biased,)
                _, last = split(raw_b[0:n, :], [slots[m][0:n, part, :] for part in range(3)], (n, S),
                                biased, *slots_free)
                free["raw_b"] = [last]
                sp.wait(last)
                if m < 2:
                    store_queries(q_dram, m, slots[m])
                else:
                    for g in range(KV_HEADS):
                        l_scratch.dma(k_dram[g].rearrange("a d h n -> (d h) a n"),
                                      slots[m][g * SLIM:(g + 1) * SLIM, :, :])
                if m == 2:
                    spec["k_in"] = spec["q_in"] = l_scratch.all()
                    places = first_loads(spec, sets)
                yield Step(pe=1.7, ve=2.5, sc=0.5, ring=work)
            spec["q_in"] = l_scratch.all()
            parts_stored(spec["q_in"])
            i, bank = work.next()
            pe.wait(*work.freed[i])
            for k in range(QT):
                for f in range(FT):
                    done = pe.mark(mm(bank[:, k * kv:(k + 1) * kv], xnT_b[:, f, k * P:(k + 1) * P],
                                      gqa_w[:, f, D + kv:D + 2 * kv], start=f == 0, stop=f == FT - 1))
            last = ve.step(tt(v_self[:, :, 0:KV_HEADS, 0:SLIM],
                              bank[:, 0:QT * kv].rearrange("p (k h d) -> p k h d", k=QT, h=KV_HEADS),
                              row_vb.rearrange("p (h d) -> p h d", h=KV_HEADS).unsqueeze(1)
                              .to_broadcast([P, QT, KV_HEADS, SLIM]), ALU.add), done, *vfree[1])
            work.freed[i] = (last,)
            yield Step(pe=0.6, ve=0.5, ring=work, late=5)
            spec["v_ready"] = (last, v_ones)
            up_free, down_free = ([tuple(free["ws"]), tuple(free["ws"])] for _ in range(2))
            up_in, down_in = {}, {}

            def load_up(e):
                if e < EXPERTS:
                    sp.wait(*up_free[e % 2])
                    up_in[e] = l_up[e % 2].dma(w1_sb[:, e % 2, :, :], t["w1"][e])

            def load_down(e):
                if e < EXPERTS:
                    sp.wait(*down_free[e % 2])
                    down_in[e] = l_down[e % 2].dma(w2_sb[:, e % 2, :, :], t["w2"][e])

            for e in range(2):
                load_up(e)
                load_down(e)
            yield from slim_attention(spec, places)
            now["spec3"] = {
                "grouped": False, "masked": True, "keys": CTX, "tiles": CTX_TILES, "scale": D ** -0.5,
                "k_dram": now["k_ctx"], "k_in": now["k_ctx_in"], "v_dram": t["ctx_v"][b],
                "stale_ones": [True] * 3, "keys_loaded": True}
            for g, s in enumerate(sets):
                load_keys(g, s, now["spec3"])
            for i, q, psum, done in project_out(lambda g: outT_b[:, g, :], lambda g: out_w[:, g, :], GROUP,
                                                (spec["out"], out_w_in)):
                ve.step(tt(xn_b[:, q, :], xn_b[:, q, :], row_ob, ALU.add), xnT_ready)
                last = ve.step(tt(xn_b[:, q, :], psum, xn_b[:, q, :], ALU.add), done)
                work.freed[i] = (last,)
                if q % 2:
                    yield Step(pe=3.5, ve=1.8, ring=work)
            free["outT_b"], free["out_w"] = [done], [done]
            rms(xn_b, RMS_EPS)
            ready = [ve.mark(stt(xn_b[:, q, :], xn_b[:, q, :], rstd[:, q:q + 1], row_n1, ALU.mult, ALU.mult))
                     for q in range(QT)]
            yield Step(ve=4, sc=1.0, late=2)
            _, xnT_ready = transpose_xn(xn_b, xnT_b, ready, done)
            yield Step(pe=1, sc=1, ring=work, late=0.2)
            i, logits, done = gate_logits(gate_w0, xnT_ready)
            sig = sc.step(act(prob[:, :, :], logits, ACT.Exp, -1.0), done, newest(ve))
            work.freed[i] = (sig,)
            ve.step(ts(prob[:, :, :], prob[:, :, :], 1.0, ALU.add), sig)
            ve.step(lambda e: e.reciprocal(prob[:, :, :], prob[:, :, :]))
            top_two()
            picked = pick2
            ve.step(tt(best1[:, :], best1[:, :], best2[:, :], ALU.add))
            ve.step(ts(best1[:, :], best1[:, :], 1e-6, ALU.add))
            ve.step(lambda e: e.reciprocal(best1[:, :], best1[:, :]))
            ve.step(tt(picked[:, :, :], pick1[:, :, :], pick2[:, :, :], ALU.add))
            ve.step(copy(before_b[:, :], before_f[:, :]), *free["chosen"])
            chosen = ve.step(copy(chosen_b[:, :, :], picked[:, :, :]))
            for q in range(QT):
                ve.step(tt(before_f[:, :], before_f[:, :], picked[:, q, :], ALU.add))
            ve.step(tt(combine[:, :, :], prob[:, :, :], picked[:, :, :], ALU.mult))
            ve.step(tt(combine[:, :, :], combine[:, :, :], wide_view(best1[:, :]), ALU.mult))
            yield Step(pe=2, ve=8, sc=1.5, late=0.5)
            h_free = [tuple(m for i in range(4 * s, 4 * s + 4) for m in expo_b.freed[i]) for s in range(2)]
            hidden_ready = [None, None]
            written = [newest(ve)] * QT

            def expert_up(e):
                s = e % 2
                for m in range(FFN // P):
                    i, bank = work.next()
                    pe.wait(up_in[e], xnT_ready, *work.freed[i])
                    for f in range(FT):
                        done = pe.mark(mm(bank, w1_sb[:, s, f, m * P:(m + 1) * P], xnT_b[:, f, :],
                                          start=f == 0, stop=f == FT - 1))
                    last = sc.step(act(hidden[:, s, m, :], bank, ACT.Gelu), done, *h_free[s])
                    work.freed[i] = (last,)
                    hidden_ready[s] = last
                    yield Step(pe=1.72, sc=0.5, ring=work)
                up_free[s] = (done,)
                load_up(e + 2)

            def expert_down(e):
                s = e % 2
                for q in range(0, QT, 2):
                    i, bank = work.next()
                    pe.wait(hidden_ready[s], down_in[e], *work.freed[i])
                    for j in range(2):
                        for m in range(FFN // P):
                            op = mm(bank[:, j * D:(j + 1) * D], hidden[:, s, m, (q + j) * P:(q + j + 1) * P],
                                    w2_sb[:, s, m, :], start=m == 0, stop=m == FFN // P - 1)
                            done = pe.mark(op) if m == FFN // P - 1 else pe.do(op)
                    for j in range(2):
                        ve.wait(written[q + j], combined, done)
                        last = written[q + j] = ve.mark(
                            stt(xn_b[:, q + j, :], bank[:, j * D:(j + 1) * D],
                                combine[:, q + j, e:e + 1], xn_b[:, q + j, :], ALU.mult, ALU.add))
                    work.freed[i] = (last,)
                    yield Step(pe=3.5, ve=0.8, ring=work)
                h_free[s] = down_free[s] = (done,)
                load_down(e + 2)

            yield from expert_up(0)
            i, bank = work.next()
            pe.wait(chosen, *work.freed[i])
            for q in range(QT):
                ranks_q = bank[:, q * EXPERTS:(q + 1) * EXPERTS]
                pe.do(mm(ranks_q, earlier_b[:, :], chosen_b[:, q, :], stop=False))
                for r in range(q):
                    pe.do(mm(ranks_q, ones_b[:, :], chosen_b[:, r, :], start=False, stop=False))
                done = pe.mark(mm(ranks_q, ones_b[:, :], before_b[:, :], start=False))
            free["chosen"] = [done]
            ranks = bank[:, 0:QT * EXPERTS].rearrange("p (q e) -> p q e", q=QT)
            last = combined = ve.step(stt(combine[:, :, :], ranks, float(CAPACITY), combine[:, :, :],
                                          ALU.is_lt, ALU.mult), done)
            work.freed[i] = (last,)
            yield Step(ve=0.3, late=0.2)
            for e in range(EXPERTS):
                if e + 1 < EXPERTS:
                    yield from expert_up(e + 1)
                yield from expert_down(e)
            done = h_free[(EXPERTS - 1) % 2][0]
            free["ws"], free["xnT_b"] = [done], [done]
            for i in range(8):
                expo_b.freed[i] = (done,)
            rms(xn_b, RMS_EPS)
            for q in range(QT):
                ve.step(stt(xn_b[:, q, :], xn_b[:, q, :], rstd[:, q:q + 1], row_n2, ALU.mult, ALU.mult))
                now["x"] = ve.step(stt(x_sb[:, q, :], xn_b[:, q, :], gates[:, 2:3], x_sb[:, q, :], ALU.mult, ALU.add))
            yield Step(ve=7, sc=2.5, late=1)

        def block_3(b, sets, now):
            x_sb = x_bufs[b % 2]
            sp.wait(masks_stored[0], *free["ws"])
            q_mask_in = l_qmask.dma(maskQ_sb, maskQ_dram.rearrange("(q p) n -> p q n", p=P))
            sp.wait(*free["out_w"])
            out_w_in = l_wp.dma(out_w[:, :, :], t["w_out"])
            ready = layer_norm(x_sb, xn_b, now["x"], stacked=True)
            yield Step(ve=3, sc=1.5, late=1.5)
            _, xnT_ready = transpose_xn(xn_b, xnT_b, ready, *free["xnT_b"])
            yield Step(pe=1.0, sc=1.0, ring=work, late=0.2)
            q_dram = scratch(f"q3_{b}", len(TERMS), GROUP, S)
            slots, slots_free = part_slots()
            spec = now["spec3"]
            spec["q_dram"] = q_dram
            for m in range(FT):
                _, last = split(xnT_b[:, m, :], [slots[m][:, part, :] for part in range(3)], (P, S),
                                xnT_ready, *slots_free)
                sp.wait(last)
                store_queries(q_dram, m, slots[m])
                spec["q_in"] = l_scratch.all()
                if m == 0:
                    first_loads(spec, sets)
                yield Step(ve=2, sc=0.5)
            free["xnT_b"] = [last]
            parts_stored(l_scratch.all())
            spec["q_mask_in"], spec["late"] = q_mask_in, 9.0
            yield from slim_attention(spec, sets)
            free["ws"] = [*kfree[0], *kfree[1], newest(ve)]
            for i, q, psum, done in project_out(lambda g: outT_b[:, g, :], lambda g: out_w[:, g, :], GROUP,
                                                (spec["out"], out_w_in)):
                ve.step(tt(xn_b[:, q, :], psum, row_bo, ALU.add), done)
                now["x"] = ve.step(stt(x_sb[:, q, :], xn_b[:, q, :], gates[:, 1:2], x_sb[:, q, :], ALU.mult, ALU.add))
                work.freed[i] = (now["x"],)
                if q % 2:
                    yield Step(pe=3.5, ve=1.8, ring=work)
            free["outT_b"], free["out_w"] = [done], [done]

        def block_4(b, sets, now):
            x_sb = x_bufs[b % 2]
            sp.wait(*free["ws"])
            l_ws.dma(wqkv_sb, t["wqkv"])
            ws_in = l_ws.dma(we_sb, t["we"])
            sp.wait(*free["out_w"])
            out_w_in = l_wp.dma(out_w[:, :, :], t["scatter"])
            v_ones = ones_in_values(HEADS)
            ready = layer_norm(x_sb, xn_b, now["x"])
            yield Step(ve=3, sc=1.5, late=1.5)
            _, xnT_ready = transpose_xn(xn_b, xnT_b, ready, *free["xnT_b"])
            yield Step(pe=1.0, sc=1.0, ring=work, late=0.2)
            q_dram = scratch(f"q4_{b}", len(TERMS), GROUP, S)
            k_dram = scratch(f"k4_{b}", 3, GROUP, S)
            slots, slots_free = part_slots()
            spec = {"grouped": False, "masked": False, "keys": S, "tiles": SELF_TILES, "scale": SLIM ** -0.5,
                    "k_dram": k_dram, "q_dram": q_dram, "late": 1.0, "stale_ones": [True] * 3}
            for m in (0, 2, 1, 3):
                i, bank = work.next()
                pe.wait(xnT_ready, ws_in, *work.freed[i])
                for f in range(FT):
                    done = pe.mark(mm(bank, wqkv_sb[:, f, m * P:(m + 1) * P], xnT_b[:, f, :],
                                      start=f == 0, stop=f == FT - 1))
                biased = ve.step(ts(raw_b[:, :], bank, qk_bias[:, 3 + m:4 + m], ALU.add), done, *free["raw_b"])
                work.freed[i] = (biased,)
                _, last = split(raw_b[:, :], [slots[m][:, part, :] for part in range(3)], (P, S),
                                biased, *slots_free)
                free["raw_b"] = [last]
                sp.wait(last)
                if m < 2:
                    store_queries(q_dram, m, slots[m])
                else:
                    store_keys(l_scratch, k_dram, m - 2, slots[m])
                if m == 2:
                    spec["k_in"] = spec["q_in"] = l_scratch.all()
                    places = first_loads(spec, sets)
                yield Step(pe=1.7, ve=2.5, sc=0.5, ring=work)
            spec["k_in"] = spec["q_in"] = l_scratch.all()
            parts_stored(spec["q_in"])
            for k in range(0, QT, 2):
                i, bank = work.next()
                pe.wait(*work.freed[i])
                for j in range(2):
                    for f in range(FT):
                        done = pe.mark(mm(bank[:, j * D:(j + 1) * D], xnT_b[:, f, (k + j) * P:(k + j + 1) * P],
                                          wqkv_sb[:, f, 2 * D:3 * D], start=f == 0, stop=f == FT - 1))
                last = ve.step(tt(v_self[:, k:k + 2, :, 0:SLIM],
                                  bank.rearrange("p (k h d) -> p k h d", k=2, h=HEADS),
                                  row_v1.rearrange("p (h d) -> p h d", h=HEADS).unsqueeze(1)
                                  .to_broadcast([P, 2, HEADS, SLIM]), ALU.add), done, *vfree[1])
                work.freed[i] = (last,)
                yield Step(pe=1.7, ve=0.6, ring=work)
            v_ready = (last, v_ones)
            i, logits, done = gate_logits(gate_w1, xnT_ready)
            work.freed[i] = (ve.step(tt(prob[:, :, :], logits,
                                        row_bg.unsqueeze(1).to_broadcast([P, QT, EXPERTS]), ALU.add), done),)
            ve.step(rmax(best1[:, :], prob[:, :, :]))
            last = ve.step(tt(prob[:, :, :], prob[:, :, :], wide_view(best1[:, :]), ALU.subtract))
            last = sc.step(act(prob[:, :, :], prob[:, :, :], ACT.Exp), last)
            ve.step(lambda e: e.reduce_sum(best1[:, :], prob[:, :, :], AX.X), last)
            ve.step(lambda e: e.reciprocal(best1[:, :], best1[:, :]))
            ve.step(tt(prob[:, :, :], prob[:, :, :], wide_view(best1[:, :]), ALU.mult))
            top_two()
            ve.step(tt(combine[:, :, :], pick1[:, :, :], pick2[:, :, :], ALU.add))
            comb = ve.step(tt(combine[:, :, :], combine[:, :, :], prob[:, :, :], ALU.mult))
            yield Step(ve=6, sc=1.5, late=1)
            spec["v_ready"] = v_ready

            def experts():
                i, bank = work.next()
                pe.wait(comb, *work.freed[i])
                for q in range(QT):
                    done = pe.mark(transpose(bank[0:EXPERTS, q * P:(q + 1) * P], combine[:, q, :], ident))
                combT_ready = sc.step(acopy(combT, bank[0:EXPERTS, :]), done, *free["raw_b"])
                work.freed[i] = (combT_ready,)
                for q in range(0, QT, 2):
                    i, bank = work.next()
                    pe.wait(combT_ready, *work.freed[i])
                    for j in range(2):
                        done = pe.mark(mm(bank[:, j * D:(j + 1) * D], combT[:, (q + j) * P:(q + j + 1) * P], b_exp[:, :]))
                    last = ve.step(copy(xn_b[:, q:q + 2, :], bank.rearrange("p (q n) -> p q n", q=2)), done, xnT_ready)
                    work.freed[i] = (last,)
                written = [last] * QT
                free["raw_b"] = [done]
                yield Step(pe=1, ve=1, sc=0.5, late=3)
                for e in range(EXPERTS):
                    for q in range(0, QT, 2):
                        i, bank = work.next()
                        pe.wait(*work.freed[i])
                        for j in range(2):
                            for f in range(FT):
                                done = pe.mark(mm(bank[:, j * D:(j + 1) * D], xnT_b[:, f, (q + j) * P:(q + j + 1) * P],
                                                  we_sb[:, e, f, :], start=f == 0, stop=f == FT - 1))
                        for j in range(2):
                            ve.wait(written[q + j], done)
                            last = written[q + j] = ve.mark(
                                stt(xn_b[:, q + j, :], bank[:, j * D:(j + 1) * D],
                                    combine[:, q + j, e:e + 1], xn_b[:, q + j, :], ALU.mult, ALU.add))
                        work.freed[i] = (last,)
                        yield Step(pe=1.72, ve=0.8, ring=work)
                free["ws"], free["xnT_b"] = [done], [done]

            yield from beside(slim_attention(spec, places), experts(), 0.08)
            for i, q, psum, done in project_out(lambda g: outT_b[:, g, :], lambda g: out_w[:, g, :], GROUP,
                                                (spec["out"], out_w_in)):
                ve.step(tt(xn_b[:, q, :], psum, xn_b[:, q, :], ALU.add), done)
                last = ve.step(stt(x_sb[:, q, :], xn_b[:, q, :], gates[:, 3:4], x_sb[:, q, :], ALU.mult, ALU.add))
                work.freed[i] = (last,)
                if q % 2:
                    yield Step(pe=3.5, ve=1.8, ring=work)
            free["outT_b"], free["out_w"] = [done], [done]
            sp.wait(last)
            stored = l_out[b % 2].dma(out[b].rearrange("(q p) n -> p q n", p=P), x_sb[:, :, :])
            free[f"x{b % 2}"] = [stored]

        def blocks_2_to_4(b, sets, now):
            yield from block_2(b, sets, now)
            yield from block_3(b, sets, now)
            yield from block_4(b, sets, now)

        handed = {"ctxT_in": ctxT_in}
        pace = Pace()
        merge([block_1(0, [0, 1], x_in, first_pair_in, handed), make_masks()], [500.0, 5.0], pace)
        for b in range(B):
            now = dict(handed)
            if b + 1 < B:
                a = block_1(b + 1, [0], load_x(b + 1), load_pair(0), handed)
                merge([a, blocks_2_to_4(b, [1], now)], [COST_A, COST_B], pace)
            else:
                merge([blocks_2_to_4(b, [1, 0], now)], [COST_B], pace)

        sp.wait(l_out[0].all(), l_out[1].all(), l_scratch.all(), l_kctx.all(), l_stored.all())

        block = ctx.enter_context(nc.Block())

        @block.sync
        def _(eng):
            sp.run(eng)

        @block.tensor
        def _(eng):
            pe.run(eng)

        @block.scalar
        def _(eng):
            sc.run(eng)

        @block.vector
        def _(eng):
            ve.run(eng)

        @block.gpsimd
        def _(eng):
            po.run(eng)



STACKED = np.arange(D).reshape(HEADS // GROUP, GROUP, SLIM).transpose(0, 2, 1).reshape(D)


def lay_out(inputs):
    def a(name):
        return np.asarray(inputs[name])

    def tiles(w):
        return np.ascontiguousarray(w.reshape(-1, P, w.shape[-1]).transpose(1, 0, 2))

    def padded(w):
        out = np.zeros((HEADS, PAD, w.shape[-1]), w.dtype)
        out[:, :SLIM] = w.reshape(HEADS, SLIM, -1)
        return tiles(out.reshape(HEADS * PAD, -1))

    consts = np.zeros((P, C_ALL), np.float32)
    consts[:, C_IDENT:C_IDENT + P] = np.eye(P)
    for h in range(2):
        consts[h:6:2, C_SELECT + h * P:C_SELECT + (h + 1) * P] = 1
    consts[:, C_TIE:C_EARLIER] = EXPERTS - np.arange(EXPERTS)
    consts[:, C_EARLIER:] = np.triu(np.ones((P, P)), 1)
    mask = a("mask_1x1xSxS2_ik0")[0, 0]
    pair = np.stack([a("L0_xattn_Wq"), a("L0_xattn_Wk")[STACKED], a("L0_xattn_Wv")[STACKED]])
    pair = pair.reshape(3, FT, P, PAIRS, P)
    pair = pair.transpose(3, 2, 0, 1, 4).reshape(PAIRS, P, 3, D)
    ctx_v = np.ones((B, HEADS // GROUP, CTX, GROUP, PAD), np.float32)
    ctx_v[..., :SLIM] = a("ctx_1024").reshape(B, CTX, HEADS // GROUP, GROUP, SLIM).transpose(0, 2, 1, 3, 4)
    arrays = {
        "x": a("x"), "ctx_v": ctx_v.reshape(B, HEADS // GROUP, CTX, GROUP * PAD),
        "ctxT": np.ascontiguousarray(a("ctx_1024").transpose(0, 2, 1)[:, STACKED]),
        "maskQ": np.ascontiguousarray(mask), "maskT": np.ascontiguousarray(mask.T),
        "consts": consts,
        "w_pair": np.ascontiguousarray(pair), "L0_xattn_Wo": a("L0_xattn_Wo"),
        "gqa_w": tiles(np.concatenate([a("L0_ffn_qw")[:, STACKED], a("L0_ffn_kw"), a("L0_ffn_vw")], 1)),
        "ow": padded(a("L0_ffn_ow")), "w_out": padded(a("L1_xattn_w_out").T),
        "scatter": padded(np.eye(D, dtype=np.float32)),
        "gate0": tiles(a("L0_ffn_gate_w")), "gate1": tiles(a("L1_ffn_W_gate")),
        "w1": np.stack([tiles(w) for w in a("L0_ffn_w1")]),
        "w2": np.stack([tiles(w) for w in a("L0_ffn_w2")]),
        "wqkv": tiles(np.concatenate([a("L1_ffn_W_qkv")[:, c] for c in (STACKED, D + STACKED, slice(2 * D, None))], 1)),
        "we": np.ascontiguousarray(a("L1_ffn_W_experts").reshape(EXPERTS, FT, P, D).transpose(2, 0, 1, 3)),
    }
    qk = np.zeros((7, P), np.float32)
    qk[0:2], qk[2, 0:64] = a("L0_ffn_qb")[STACKED].reshape(2, P), a("L0_ffn_kb")
    qk[3:7] = a("L1_ffn_b_qkv")[np.concatenate([STACKED, D + STACKED])].reshape(4, P)
    arrays["qk_bias"] = np.ascontiguousarray(qk.T)
    for n in ("g_xattn", "g_ffn", "L0_ffn_vb", "L0_ffn_ob", "L0_ffn_norm1_w",
              "L0_ffn_norm2_w", "L1_xattn_b_out", "L1_ffn_b_qkv", "L1_ffn_b_gate", "L1_ffn_b_experts"):
        arrays[n] = a(n)
    return arrays


def kernel(**inputs):
    import concourse.bacc as bacc
    from concourse.bass_utils import run_bass_kernel_spmd

    nc = bacc.Bacc("TRN2", target_bir_lowering=False, num_devices=1)
    arrays = {"in_" + n: v for n, v in lay_out(inputs).items()}
    t = {n[3:]: nc.dram_tensor(n, v.shape, mybir.dt.from_np(v.dtype), kind="ExternalInput").ap()
         for n, v in arrays.items()}
    out = nc.dram_tensor("out_x", (B, S, D), F32, kind="ExternalOutput").ap()
    flamingo(nc, t, out)
    r = run_bass_kernel_spmd(nc, [arrays], core_ids=[0])
    return r.results[0]["out_x"]
```
